# Optimizing a Trainium2 kernel written in Bass

```python
import numpy as np
import jax
import jax.numpy as jnp

def _softmax(x, axis=-1):
    return jax.nn.softmax(x, axis=axis)

def _gelu(x):
    return jax.nn.gelu(x, approximate=True)

def _silu(x):
    return jax.nn.silu(x)

def _sigmoid(x):
    return jax.nn.sigmoid(x)

def _layernorm(x, axis=-1, eps=1e-05):
    m = jnp.mean(x, axis=axis, keepdims=True)
    v = jnp.var(x, axis=axis, keepdims=True)
    return (x - m) / jnp.sqrt(v + eps)

def _scatter_add(tgt, idx, src, axis=0):
    return tgt.at[idx].add(src)

def _segment_sum(src, seg, n):
    return jax.ops.segment_sum(src, seg, n)
kernel_name = 'mk_gnn_ffn_d4_gnn_r32_3b1894'

def setup_inputs(seed: int=0):
    np.random.seed(seed)
    _w = jnp.asarray

    def _rec_inputs():
        import jax
        import jax.numpy as jnp
        _gk = jax.random.key(seed)
        x = -0.0001538 + 1 * jax.random.normal(jax.random.fold_in(_gk, 1), (256, 768), jnp.float32)
        src = jax.random.randint(jax.random.fold_in(_gk, 2), (8192,), 0, 256, jnp.int32)
        dst = jnp.minimum((256 * jax.random.uniform(jax.random.fold_in(_gk, 3), (8192,)) ** 2.0).astype(jnp.int32), 8191)
        _o = jnp.argsort(dst, stable=True)
        src = src[_o]
        dst = dst[_o]
        edge_type_34 = jax.random.randint(jax.random.fold_in(_gk, 12), (8192,), 0, 34, jnp.int32)
        return (x, src, dst, edge_type_34)
    x, src, dst, edge_type_34 = _rec_inputs()

    def _L0_gnn_setup():
        import jax, jax.numpy as jnp
        import numpy as np
        N_NODES = 256
        N_EDGES = 1024
        D = 768
        H1 = 8
        NEG_SLOPE = 0.2

        def gat_conv(x, src, dst, W, a_src, a_dst, b, heads, out_ch):
            n = x.shape[0]
            h = (x @ W).reshape(n, heads, out_ch)
            alpha_src = jnp.einsum('nhc,hc->nh', h, a_src)
            alpha_dst = jnp.einsum('nhc,hc->nh', h, a_dst)
            e = jax.nn.leaky_relu(alpha_src[src] + alpha_dst[dst], NEG_SLOPE)
            m = jax.ops.segment_max(e, dst, num_segments=n)
            m = jnp.where(jnp.isfinite(m), m, 0.0)
            p = jnp.exp(e - m[dst])
            denom = jax.ops.segment_sum(p, dst, num_segments=n)
            alpha = p / denom[dst]
            msg = h[src] * alpha[:, :, None]
            out = jax.ops.segment_sum(msg, dst, num_segments=n)
            return out.reshape(n, heads * out_ch) + b
        key = jax.random.key(seed)
        ks = jax.random.split(key, 10)
        s = 0.02
        x = jax.random.normal(ks[0], (N_NODES, D), dtype=jnp.float32)
        edge_index = jax.random.randint(ks[1], (2, N_EDGES), 0, N_NODES, dtype=jnp.int64)
        W1 = jax.random.normal(ks[2], (D, H1 * D), dtype=jnp.float32) * s
        a_src1 = jax.random.normal(ks[3], (H1, D), dtype=jnp.float32) * s
        a_dst1 = jax.random.normal(ks[4], (H1, D), dtype=jnp.float32) * s
        b1 = jnp.zeros((H1 * D,), dtype=jnp.float32)
        W2 = jax.random.normal(ks[5], (H1 * D, D), dtype=jnp.float32) * s
        a_src2 = jax.random.normal(ks[6], (1, D), dtype=jnp.float32) * s
        a_dst2 = jax.random.normal(ks[7], (1, D), dtype=jnp.float32) * s
        b2 = jnp.zeros((D,), dtype=jnp.float32)
        return {'x': x, 'edge_index': edge_index, 'W1': W1, 'a_src1': a_src1, 'a_dst1': a_dst1, 'b1': b1, 'W2': W2, 'a_src2': a_src2, 'a_dst2': a_dst2, 'b2': b2}
    _L0_gnn_all = _L0_gnn_setup()
    _L0_gnn_in = {k: v for k, v in _L0_gnn_all.items() if k in ('W1', 'a_src1', 'a_dst1', 'b1', 'W2', 'a_src2', 'a_dst2', 'b2')}
    del _L0_gnn_all

    def _L0_ffn_setup():
        import jax, jax.numpy as jnp
        import numpy as np
        ATOM = {'vm': 0, 'im': 1, 'cm': 2, 'sc': 3, 'cc': 4}
        TASK_PAIRS = [('vm', 'sc'), ('vm', 'cc'), ('im', 'sc'), ('im', 'cc'), ('cm', 'sc'), ('cm', 'cc')]
        SRC_IDX = np.array([[ATOM[l], ATOM[r]] for l, r in TASK_PAIRS], dtype=np.int32)
        DST_IDX = np.array([[ATOM[r], ATOM[l]] for l, r in TASK_PAIRS], dtype=np.int32)
        NCLS = 6
        NATOMS = 5

        def _l2norm(x, eps=1e-12):
            return x / jnp.clip(jnp.linalg.norm(x, axis=-1, keepdims=True), eps)
        key = jax.random.key(seed)
        ks = jax.random.split(key, 12)
        B, NPATCH, D, H = (64, 197, 768, 96)
        std = 0.02
        x = jax.random.normal(ks[0], (B, NCLS + NPATCH, D), dtype=jnp.float32)
        fc1_w = jax.random.normal(ks[1], (H, D), dtype=jnp.float32) * std
        fc1_b = jnp.zeros((H,), jnp.float32)
        fc2_w = jax.random.normal(ks[2], (D, H), dtype=jnp.float32) * std
        fc2_b = jnp.zeros((D,), jnp.float32)
        gate_pair = jax.random.normal(ks[3], (NCLS, 2, D), dtype=jnp.float32) * std
        atom_in_w = jax.random.normal(ks[4], (NATOMS, H, D), dtype=jnp.float32) * std
        atom_in_b = jax.random.normal(ks[5], (NATOMS, H), dtype=jnp.float32) * std
        atom_out_w = jax.random.normal(ks[6], (NATOMS, D, H), dtype=jnp.float32) * std
        atom_out_b = jax.random.normal(ks[7], (NATOMS, D), dtype=jnp.float32) * std
        balance_bias = jnp.zeros((NCLS, 2), jnp.float32)
        return {'x': x, 'fc1_w': fc1_w, 'fc1_b': fc1_b, 'fc2_w': fc2_w, 'fc2_b': fc2_b, 'gate_pair': gate_pair, 'atom_in_w': atom_in_w, 'atom_in_b': atom_in_b, 'atom_out_w': atom_out_w, 'atom_out_b': atom_out_b, 'balance_bias': balance_bias}
    _L0_ffn_all = _L0_ffn_setup()
    _L0_ffn_in = {k: v for k, v in _L0_ffn_all.items() if k in ('fc1_w', 'fc1_b', 'fc2_w', 'fc2_b', 'gate_pair', 'atom_in_w', 'atom_in_b', 'atom_out_w', 'atom_out_b', 'balance_bias')}
    del _L0_ffn_all

    def _L1_gnn_setup():
        import jax, jax.numpy as jnp
        import numpy as np
        NEG_SLOPE = 0.2
        EPS = 1e-16
        N_NODES = 256
        N_EDGES = 2048
        D_IN = 768
        D_HID = 768
        H1 = 8
        H2 = 1

        def gat_layer(x, W, a_s, a_d, b, edge_index, concat):
            n = x.shape[0]
            H, C = a_s.shape
            h = (x @ W).reshape(n, H, C)
            src, dst = (edge_index[0], edge_index[1])
            alpha_s = jnp.einsum('nhc,hc->nh', h, a_s)
            alpha_d = jnp.einsum('nhc,hc->nh', h, a_d)
            e = jax.nn.leaky_relu(alpha_s[src] + alpha_d[dst], NEG_SLOPE)
            m = jax.ops.segment_max(e, dst, num_segments=n)
            e = jnp.exp(e - m[dst])
            denom = jax.ops.segment_sum(e, dst, num_segments=n)
            alpha = e / (denom[dst] + EPS)
            msg = h[src] * alpha[:, :, None]
            out = jax.ops.segment_sum(msg, dst, num_segments=n)
            out = out.reshape(n, H * C) if concat else out.mean(axis=1)
            return out + b
        key = jax.random.key(seed)
        ks = jax.random.split(key, 10)
        x = jax.random.normal(ks[0], (N_NODES, D_IN), dtype=jnp.float32)
        edge_list = jax.random.randint(ks[1], (2, N_EDGES), 0, N_NODES, dtype=jnp.int32)
        s = 0.05
        W1 = jax.random.normal(ks[2], (D_IN, H1 * D_HID), dtype=jnp.float32) * s
        a_src1 = jax.random.normal(ks[3], (H1, D_HID), dtype=jnp.float32) * s
        a_dst1 = jax.random.normal(ks[4], (H1, D_HID), dtype=jnp.float32) * s
        b1 = jnp.zeros((H1 * D_HID,), dtype=jnp.float32)
        W2 = jax.random.normal(ks[5], (H1 * D_HID, H2 * D_HID), dtype=jnp.float32) * s
        a_src2 = jax.random.normal(ks[6], (H2, D_HID), dtype=jnp.float32) * s
        a_dst2 = jax.random.normal(ks[7], (H2, D_HID), dtype=jnp.float32) * s
        b2 = jnp.zeros((H2 * D_HID,), dtype=jnp.float32)
        return {'x': x, 'W1': W1, 'a_src1': a_src1, 'a_dst1': a_dst1, 'b1': b1, 'W2': W2, 'a_src2': a_src2, 'a_dst2': a_dst2, 'b2': b2, 'edge_list': edge_list}
    _L1_gnn_all = _L1_gnn_setup()
    _L1_gnn_in = {k: v for k, v in _L1_gnn_all.items() if k in ('W1', 'a_src1', 'a_dst1', 'b1', 'W2', 'a_src2', 'a_dst2', 'b2')}
    del _L1_gnn_all

    def _L1_ffn_setup():
        import jax, jax.numpy as jnp
        import numpy as np
        HIDDEN = 768
        INNER = 512
        EPS = 1e-05
        key = jax.random.key(seed)
        ks = jax.random.split(key, 6)
        B, S = (8, 128)
        x = jax.random.normal(ks[0], (B, S, HIDDEN), dtype=jnp.float32)
        W1 = jax.random.normal(ks[1], (INNER, HIDDEN), dtype=jnp.float32) * 0.02
        b1 = jnp.zeros((INNER,), dtype=jnp.float32)
        W2 = jax.random.normal(ks[2], (HIDDEN, INNER), dtype=jnp.float32) * 0.02
        b2 = jnp.zeros((HIDDEN,), dtype=jnp.float32)
        bound = 1.0 / np.sqrt(HIDDEN)
        Wo = jax.random.uniform(ks[3], (HIDDEN, HIDDEN), minval=-bound, maxval=bound, dtype=jnp.float32)
        bo = jax.random.uniform(ks[4], (HIDDEN,), minval=-bound, maxval=bound, dtype=jnp.float32)
        gamma = jnp.ones((HIDDEN,), dtype=jnp.float32)
        beta = jnp.zeros((HIDDEN,), dtype=jnp.float32)
        return {'x': x, 'W1': W1, 'b1': b1, 'W2': W2, 'b2': b2, 'Wo': Wo, 'bo': bo, 'gamma': gamma, 'beta': beta}
    _L1_ffn_all = _L1_ffn_setup()
    _L1_ffn_in = {k: v for k, v in _L1_ffn_all.items() if k in ('W1', 'b1', 'W2', 'b2', 'Wo', 'bo', 'gamma', 'beta')}
    del _L1_ffn_all

    def _L2_gnn_setup():
        import jax, jax.numpy as jnp
        import numpy as np
        N_NODES = 10000
        key = jax.random.key(seed)
        k1, k2, k3 = jax.random.split(key, 3)
        x = jax.random.normal(k1, (N_NODES, 768), dtype=jnp.float32)
        edge_index = jax.random.randint(k2, (2, 3125), 0, N_NODES, dtype=jnp.int32)
        W = jax.random.normal(k3, (768, 768), dtype=jnp.float32) * (1.0 / np.sqrt(768))
        b = jnp.zeros((768,), dtype=jnp.float32)
        return {'x': x, 'edge_index': edge_index, 'W': W, 'b': b}
    _L2_gnn_all = _L2_gnn_setup()
    _L2_gnn_in = {k: v for k, v in _L2_gnn_all.items() if k in ('W', 'b')}
    del _L2_gnn_all

    def _L2_ffn_setup():
        import jax, jax.numpy as jnp
        import numpy as np
        S, B, DIM = (1024, 4, 768)
        N_EXPERTS = 8
        HID = 64
        key = jax.random.key(seed)
        ks = jax.random.split(key, 6)
        scale = 0.02
        return {'hidden_states': jax.random.normal(ks[0], (S, B, DIM), dtype=jnp.float32), 'router_w': jax.random.normal(ks[1], (DIM, N_EXPERTS), dtype=jnp.float32) * scale, 'router_b': jnp.zeros((N_EXPERTS,), dtype=jnp.float32), 'w1': jax.random.normal(ks[2], (N_EXPERTS, DIM, HID), dtype=jnp.float32) * scale, 'w2': jax.random.normal(ks[3], (N_EXPERTS, DIM, HID), dtype=jnp.float32) * scale, 'w3': jax.random.normal(ks[4], (N_EXPERTS, HID, DIM), dtype=jnp.float32) * scale}
    _L2_ffn_all = _L2_ffn_setup()
    _L2_ffn_in = {k: v for k, v in _L2_ffn_all.items() if k in ('router_w', 'router_b', 'w1', 'w2', 'w3')}
    del _L2_ffn_all

    def _L3_gnn_setup():
        import jax, jax.numpy as jnp
        import numpy as np
        N_NODES = 10000
        N_EDGES = 3125
        N_REL = 34
        DIM = 768

        def _graph_encoder(x, edge_index, edge_type, W_rel, W_root, b_rgcn, W_gcn, b_gcn):
            n = x.shape[0]
            src, dst = (edge_index[0], edge_index[1])
            ones = jnp.ones((src.shape[0],), dtype=x.dtype)
            seg = edge_type * n + dst
            agg = jax.ops.segment_sum(x[src], seg, num_segments=N_REL * n)
            cnt = jax.ops.segment_sum(ones, seg, num_segments=N_REL * n)
            mean = agg.reshape(N_REL, n, -1) / jnp.maximum(cnt, 1.0).reshape(N_REL, n, 1)
            h1 = jnp.einsum('rni,rio->no', mean, W_rel) + x @ W_root + b_rgcn
            xw = h1 @ W_gcn
            deg = jax.ops.segment_sum(ones, dst, num_segments=n) + 1.0
            dinv = jax.lax.rsqrt(deg)
            norm = dinv[src] * dinv[dst]
            out = jax.ops.segment_sum(xw[src] * norm[:, None], dst, num_segments=n)
            out = out + xw * (dinv * dinv)[:, None]
            return out + b_gcn
        key = jax.random.key(seed)
        ks = jax.random.split(key, 6)
        scale = 1.0 / np.sqrt(DIM)
        x = jax.random.normal(ks[0], (N_NODES, DIM), dtype=jnp.float32)
        edge_index = jax.random.randint(ks[1], (2, N_EDGES), 0, N_NODES, dtype=jnp.int32)
        edge_type = jax.random.randint(ks[2], (N_EDGES,), 0, N_REL, dtype=jnp.int32)
        W_rel = jax.random.normal(ks[3], (N_REL, DIM, DIM), dtype=jnp.float32) * scale
        W_root = jax.random.normal(ks[4], (DIM, DIM), dtype=jnp.float32) * scale
        b_rgcn = jnp.zeros((DIM,), dtype=jnp.float32)
        W_gcn = jax.random.normal(ks[5], (DIM, DIM), dtype=jnp.float32) * scale
        b_gcn = jnp.zeros((DIM,), dtype=jnp.float32)
        return {'x': x, 'edge_index': edge_index, 'edge_type': edge_type, 'W_rel': W_rel, 'W_root': W_root, 'b_rgcn': b_rgcn, 'W_gcn': W_gcn, 'b_gcn': b_gcn}
    _L3_gnn_all = _L3_gnn_setup()
    _L3_gnn_in = {k: v for k, v in _L3_gnn_all.items() if k in ('W_rel', 'W_root', 'b_rgcn', 'W_gcn', 'b_gcn')}
    del _L3_gnn_all

    def _L3_ffn_setup():
        import jax, jax.numpy as jnp
        import numpy as np
        D_MODEL = 768
        D_HID = 96
        D_OUT = 768
        N_EXP = 8
        TOP_K = 2
        B, S = (2, 64)
        LN_EPS = 1e-05
        key = jax.random.key(seed)
        ks = jax.random.split(key, 10)
        sc_in = 1.0 / np.sqrt(D_MODEL)
        sc_hid = 1.0 / np.sqrt(D_HID)
        return {'x': jax.random.normal(ks[0], (B, S, D_MODEL), dtype=jnp.float32), 'Wr': jax.random.normal(ks[1], (D_MODEL, N_EXP), dtype=jnp.float32) * sc_in, 'br': jnp.zeros((N_EXP,), dtype=jnp.float32), 'W1': jax.random.normal(ks[2], (N_EXP, D_MODEL, D_HID), dtype=jnp.float32) * sc_in, 'b1': jnp.zeros((N_EXP, D_HID), dtype=jnp.float32), 'W2': jax.random.normal(ks[3], (N_EXP, D_HID, D_OUT), dtype=jnp.float32) * sc_hid, 'b2': jnp.zeros((N_EXP, D_OUT), dtype=jnp.float32), 'ln_g': jnp.ones((D_OUT,), dtype=jnp.float32), 'ln_b': jnp.zeros((D_OUT,), dtype=jnp.float32)}
    _L3_ffn_all = _L3_ffn_setup()
    _L3_ffn_in = {k: v for k, v in _L3_ffn_all.items() if k in ('Wr', 'br', 'W1', 'b1', 'W2', 'b2', 'ln_g', 'ln_b')}
    del _L3_ffn_all
    return {'x': x, 'src': src, 'dst': dst, 'edge_type_34': edge_type_34, 'L0_gnn_W1': _L0_gnn_in['W1'], 'L0_gnn_a_src1': _L0_gnn_in['a_src1'], 'L0_gnn_a_dst1': _L0_gnn_in['a_dst1'], 'L0_gnn_b1': _L0_gnn_in['b1'], 'L0_gnn_W2': _L0_gnn_in['W2'], 'L0_gnn_a_src2': _L0_gnn_in['a_src2'], 'L0_gnn_a_dst2': _L0_gnn_in['a_dst2'], 'L0_gnn_b2': _L0_gnn_in['b2'], 'L0_ffn_fc1_w': _L0_ffn_in['fc1_w'], 'L0_ffn_fc1_b': _L0_ffn_in['fc1_b'], 'L0_ffn_fc2_w': _L0_ffn_in['fc2_w'], 'L0_ffn_fc2_b': _L0_ffn_in['fc2_b'], 'L0_ffn_gate_pair': _L0_ffn_in['gate_pair'], 'L0_ffn_atom_in_w': _L0_ffn_in['atom_in_w'], 'L0_ffn_atom_in_b': _L0_ffn_in['atom_in_b'], 'L0_ffn_atom_out_w': _L0_ffn_in['atom_out_w'], 'L0_ffn_atom_out_b': _L0_ffn_in['atom_out_b'], 'L0_ffn_balance_bias': _L0_ffn_in['balance_bias'], 'L1_gnn_W1': _L1_gnn_in['W1'], 'L1_gnn_a_src1': _L1_gnn_in['a_src1'], 'L1_gnn_a_dst1': _L1_gnn_in['a_dst1'], 'L1_gnn_b1': _L1_gnn_in['b1'], 'L1_gnn_W2': _L1_gnn_in['W2'], 'L1_gnn_a_src2': _L1_gnn_in['a_src2'], 'L1_gnn_a_dst2': _L1_gnn_in['a_dst2'], 'L1_gnn_b2': _L1_gnn_in['b2'], 'L1_ffn_W1': _L1_ffn_in['W1'], 'L1_ffn_b1': _L1_ffn_in['b1'], 'L1_ffn_W2': _L1_ffn_in['W2'], 'L1_ffn_b2': _L1_ffn_in['b2'], 'L1_ffn_Wo': _L1_ffn_in['Wo'], 'L1_ffn_bo': _L1_ffn_in['bo'], 'L1_ffn_gamma': _L1_ffn_in['gamma'], 'L1_ffn_beta': _L1_ffn_in['beta'], 'L2_gnn_W': _L2_gnn_in['W'], 'L2_gnn_b': _L2_gnn_in['b'], 'L2_ffn_router_w': _L2_ffn_in['router_w'], 'L2_ffn_router_b': _L2_ffn_in['router_b'], 'L2_ffn_w1': _L2_ffn_in['w1'], 'L2_ffn_w2': _L2_ffn_in['w2'], 'L2_ffn_w3': _L2_ffn_in['w3'], 'L3_gnn_W_rel': _L3_gnn_in['W_rel'], 'L3_gnn_W_root': _L3_gnn_in['W_root'], 'L3_gnn_b_rgcn': _L3_gnn_in['b_rgcn'], 'L3_gnn_W_gcn': _L3_gnn_in['W_gcn'], 'L3_gnn_b_gcn': _L3_gnn_in['b_gcn'], 'L3_ffn_Wr': _L3_ffn_in['Wr'], 'L3_ffn_br': _L3_ffn_in['br'], 'L3_ffn_W1': _L3_ffn_in['W1'], 'L3_ffn_b1': _L3_ffn_in['b1'], 'L3_ffn_W2': _L3_ffn_in['W2'], 'L3_ffn_b2': _L3_ffn_in['b2'], 'L3_ffn_ln_g': _L3_ffn_in['ln_g'], 'L3_ffn_ln_b': _L3_ffn_in['ln_b']}

def reference(x, src, dst, edge_type_34, L0_gnn_W1, L0_gnn_a_src1, L0_gnn_a_dst1, L0_gnn_b1, L0_gnn_W2, L0_gnn_a_src2, L0_gnn_a_dst2, L0_gnn_b2, L0_ffn_fc1_w, L0_ffn_fc1_b, L0_ffn_fc2_w, L0_ffn_fc2_b, L0_ffn_gate_pair, L0_ffn_atom_in_w, L0_ffn_atom_in_b, L0_ffn_atom_out_w, L0_ffn_atom_out_b, L0_ffn_balance_bias, L1_gnn_W1, L1_gnn_a_src1, L1_gnn_a_dst1, L1_gnn_b1, L1_gnn_W2, L1_gnn_a_src2, L1_gnn_a_dst2, L1_gnn_b2, L1_ffn_W1, L1_ffn_b1, L1_ffn_W2, L1_ffn_b2, L1_ffn_Wo, L1_ffn_bo, L1_ffn_gamma, L1_ffn_beta, L2_gnn_W, L2_gnn_b, L2_ffn_router_w, L2_ffn_router_b, L2_ffn_w1, L2_ffn_w2, L2_ffn_w3, L3_gnn_W_rel, L3_gnn_W_root, L3_gnn_b_rgcn, L3_gnn_W_gcn, L3_gnn_b_gcn, L3_ffn_Wr, L3_ffn_br, L3_ffn_W1, L3_ffn_b1, L3_ffn_W2, L3_ffn_b2, L3_ffn_ln_g, L3_ffn_ln_b):
    import jax
    import jax.numpy as jnp

    def _L0_gnn_ref(x, edge_index, W1, a_src1, a_dst1, b1, W2, a_src2, a_dst2, b2):
        import jax, jax.numpy as jnp
        import numpy as np
        N_NODES = 256
        N_EDGES = 1024
        D = 768
        H1 = 8
        NEG_SLOPE = 0.2

        def gat_conv(x, src, dst, W, a_src, a_dst, b, heads, out_ch):
            n = x.shape[0]
            h = (x @ W).reshape(n, heads, out_ch)
            alpha_src = jnp.einsum('nhc,hc->nh', h, a_src)
            alpha_dst = jnp.einsum('nhc,hc->nh', h, a_dst)
            e = jax.nn.leaky_relu(alpha_src[src] + alpha_dst[dst], NEG_SLOPE)
            m = jax.ops.segment_max(e, dst, num_segments=n)
            m = jnp.where(jnp.isfinite(m), m, 0.0)
            p = jnp.exp(e - m[dst])
            denom = jax.ops.segment_sum(p, dst, num_segments=n)
            alpha = p / denom[dst]
            msg = h[src] * alpha[:, :, None]
            out = jax.ops.segment_sum(msg, dst, num_segments=n)
            return out.reshape(n, heads * out_ch) + b
        n = x.shape[0]
        loops = jnp.arange(n, dtype=edge_index.dtype)
        src = jnp.concatenate([edge_index[0], loops])
        dst = jnp.concatenate([edge_index[1], loops])
        h = gat_conv(x, src, dst, W1, a_src1, a_dst1, b1, H1, D)
        h = jax.nn.elu(h)
        out = gat_conv(h, src, dst, W2, a_src2, a_dst2, b2, 1, D)
        return out

    def _L0_ffn_ref(x, fc1_w, fc1_b, fc2_w, fc2_b, gate_pair, atom_in_w, atom_in_b, atom_out_w, atom_out_b, balance_bias):
        import jax, jax.numpy as jnp
        import numpy as np
        ATOM = {'vm': 0, 'im': 1, 'cm': 2, 'sc': 3, 'cc': 4}
        TASK_PAIRS = [('vm', 'sc'), ('vm', 'cc'), ('im', 'sc'), ('im', 'cc'), ('cm', 'sc'), ('cm', 'cc')]
        SRC_IDX = np.array([[ATOM[l], ATOM[r]] for l, r in TASK_PAIRS], dtype=np.int32)
        DST_IDX = np.array([[ATOM[r], ATOM[l]] for l, r in TASK_PAIRS], dtype=np.int32)
        NCLS = 6
        NATOMS = 5

        def _l2norm(x, eps=1e-12):
            return x / jnp.clip(jnp.linalg.norm(x, axis=-1, keepdims=True), eps)
        src = jnp.asarray(SRC_IDX)
        dst = jnp.asarray(DST_IDX)
        D = x.shape[-1]
        H = atom_in_w.shape[1]
        cls_tokens = x[:, :NCLS]
        patch_tokens = x[:, NCLS:]
        patch_out = jax.nn.gelu(patch_tokens @ fc1_w.T + fc1_b, approximate=False) @ fc2_w.T + fc2_b
        gate_in = _l2norm(cls_tokens.astype(jnp.float32))
        gate_w = _l2norm(gate_pair.astype(jnp.float32))
        gate_logits = jnp.einsum('bnd,nrd->bnr', gate_in, gate_w) + balance_bias[None]
        route_probs = jax.nn.softmax(gate_logits, axis=-1)
        chosen_route = jnp.argmax(route_probs, axis=-1)
        hid_all = jax.nn.gelu(jnp.einsum('bnd,ahd->bnah', cls_tokens, atom_in_w) + atom_in_b[None, None], approximate=False)
        sh_pair = hid_all[:, jnp.arange(NCLS)[:, None], src, :]
        route_out_w = atom_out_w[dst.reshape(-1)].reshape(NCLS, 2, D, H)
        route_candidates = jnp.einsum('bnrh,nrdh->bnrd', sh_pair, route_out_w) + atom_out_b[dst][None]
        chosen_w = jnp.take_along_axis(route_probs, chosen_route[..., None], axis=-1)
        chosen_cand = jnp.take_along_axis(route_candidates, chosen_route[:, :, None, None], axis=2)[:, :, 0]
        cls_out = chosen_cand * chosen_w.astype(chosen_cand.dtype)
        return jnp.concatenate([cls_out, patch_out], axis=1)

    def _L1_gnn_ref(x, W1, a_src1, a_dst1, b1, W2, a_src2, a_dst2, b2, edge_list):
        import jax, jax.numpy as jnp
        import numpy as np
        NEG_SLOPE = 0.2
        EPS = 1e-16
        N_NODES = 256
        N_EDGES = 2048
        D_IN = 768
        D_HID = 768
        H1 = 8
        H2 = 1

        def gat_layer(x, W, a_s, a_d, b, edge_index, concat):
            n = x.shape[0]
            H, C = a_s.shape
            h = (x @ W).reshape(n, H, C)
            src, dst = (edge_index[0], edge_index[1])
            alpha_s = jnp.einsum('nhc,hc->nh', h, a_s)
            alpha_d = jnp.einsum('nhc,hc->nh', h, a_d)
            e = jax.nn.leaky_relu(alpha_s[src] + alpha_d[dst], NEG_SLOPE)
            m = jax.ops.segment_max(e, dst, num_segments=n)
            e = jnp.exp(e - m[dst])
            denom = jax.ops.segment_sum(e, dst, num_segments=n)
            alpha = e / (denom[dst] + EPS)
            msg = h[src] * alpha[:, :, None]
            out = jax.ops.segment_sum(msg, dst, num_segments=n)
            out = out.reshape(n, H * C) if concat else out.mean(axis=1)
            return out + b
        h = gat_layer(x, W1, a_src1, a_dst1, b1, edge_list, concat=True)
        h = jax.nn.elu(h)
        out = gat_layer(h, W2, a_src2, a_dst2, b2, edge_list, concat=True)
        return out

    def _L1_ffn_ref(x, W1, b1, W2, b2, Wo, bo, gamma, beta):
        import jax, jax.numpy as jnp
        import numpy as np
        HIDDEN = 768
        INNER = 512
        EPS = 1e-05
        h = jax.nn.relu(jnp.einsum('bsd,id->bsi', x, W1) + b1)
        pred = jnp.einsum('bsi,di->bsd', h, W2) + b2
        out = jnp.einsum('bsd,ed->bse', pred, Wo) + bo
        mu = jnp.mean(out, axis=-1, keepdims=True)
        var = jnp.mean(jnp.square(out - mu), axis=-1, keepdims=True)
        out = (out - mu) * jax.lax.rsqrt(var + EPS) * gamma + beta
        return out

    def _L2_gnn_ref(x, edge_index, W, b):
        import jax, jax.numpy as jnp
        import numpy as np
        N_NODES = 10000
        n = x.shape[0]
        loops = jnp.arange(n, dtype=edge_index.dtype)
        row = jnp.concatenate([edge_index[0], loops])
        col = jnp.concatenate([edge_index[1], loops])
        ones = jnp.ones(row.shape[0], dtype=x.dtype)
        deg = jax.ops.segment_sum(ones, col, num_segments=n)
        dinv = jnp.where(deg > 0, jax.lax.rsqrt(deg), 0.0)
        norm = dinv[row] * dinv[col]
        h = x @ W
        msg = h[row] * norm[:, None]
        out = jax.ops.segment_sum(msg, col, num_segments=n) + b
        return out

    def _L2_ffn_ref(hidden_states, router_w, router_b, w1, w2, w3):
        import jax, jax.numpy as jnp
        import numpy as np
        S, B, DIM = (1024, 4, 768)
        N_EXPERTS = 8
        HID = 64
        s, b, h = hidden_states.shape
        route = jax.nn.softmax(hidden_states @ router_w + router_b, axis=2)
        max_prob = jnp.max(route, axis=2).reshape(-1, 1)
        max_ind = jnp.argmax(route, axis=2).reshape(-1)
        x = hidden_states.reshape(-1, h)
        out = jnp.zeros_like(x)
        for e in range(N_EXPERTS):
            mask = (max_ind == e)[:, None]
            xe = jnp.where(mask, x, 0.0)
            oe = jax.nn.silu(xe @ w1[e]) * (xe @ w2[e]) @ w3[e]
            out = out + jnp.where(mask, oe, 0.0)
        out = out.astype(jnp.bfloat16) * max_prob
        return out.reshape(s, b, h)

    def _L3_gnn_ref(x, edge_index, edge_type, W_rel, W_root, b_rgcn, W_gcn, b_gcn):
        import jax, jax.numpy as jnp
        import numpy as np
        N_NODES = 10000
        N_EDGES = 3125
        N_REL = 34
        DIM = 768

        def _graph_encoder(x, edge_index, edge_type, W_rel, W_root, b_rgcn, W_gcn, b_gcn):
            n = x.shape[0]
            src, dst = (edge_index[0], edge_index[1])
            ones = jnp.ones((src.shape[0],), dtype=x.dtype)
            seg = edge_type * n + dst
            agg = jax.ops.segment_sum(x[src], seg, num_segments=N_REL * n)
            cnt = jax.ops.segment_sum(ones, seg, num_segments=N_REL * n)
            mean = agg.reshape(N_REL, n, -1) / jnp.maximum(cnt, 1.0).reshape(N_REL, n, 1)
            h1 = jnp.einsum('rni,rio->no', mean, W_rel) + x @ W_root + b_rgcn
            xw = h1 @ W_gcn
            deg = jax.ops.segment_sum(ones, dst, num_segments=n) + 1.0
            dinv = jax.lax.rsqrt(deg)
            norm = dinv[src] * dinv[dst]
            out = jax.ops.segment_sum(xw[src] * norm[:, None], dst, num_segments=n)
            out = out + xw * (dinv * dinv)[:, None]
            return out + b_gcn
        return _graph_encoder(x, edge_index, edge_type, W_rel, W_root, b_rgcn, W_gcn, b_gcn)

    def _L3_ffn_ref(x, Wr, br, W1, b1, W2, b2, ln_g, ln_b):
        import jax, jax.numpy as jnp
        import numpy as np
        D_MODEL = 768
        D_HID = 96
        D_OUT = 768
        N_EXP = 8
        TOP_K = 2
        B, S = (2, 64)
        LN_EPS = 1e-05
        logits = jnp.einsum('bsd,de->bse', x, Wr) + br
        probs = jax.nn.softmax(logits, axis=-1)
        top_vals, top_idx = jax.lax.top_k(probs, TOP_K)
        routing_weights = top_vals / jnp.sum(top_vals, axis=-1, keepdims=True)
        onehot = jax.nn.one_hot(top_idx, N_EXP, dtype=x.dtype)
        expert_weights = jnp.einsum('bsk,bske->bse', routing_weights, onehot)
        h = jax.nn.gelu(jnp.einsum('bsd,edh->besh', x, W1) + b1[None, :, None, :])
        y = jnp.einsum('besh,eho->beso', h, W2) + b2[None, :, None, :]
        out = jnp.einsum('beso,bse->bso', y, expert_weights)
        mu = jnp.mean(out, axis=-1, keepdims=True)
        var = jnp.mean(jnp.square(out - mu), axis=-1, keepdims=True)
        out = (out - mu) * jax.lax.rsqrt(var + LN_EPS) * ln_g + ln_b
        return out
    edge_index = jnp.stack([src, dst])
    x = x + _L0_gnn_ref(_layernorm(x, axis=-1), edge_index, L0_gnn_W1, L0_gnn_a_src1, L0_gnn_a_dst1, L0_gnn_b1, L0_gnn_W2, L0_gnn_a_src2, L0_gnn_a_dst2, L0_gnn_b2)
    x = x + _L0_ffn_ref(_layernorm(x, axis=-1)[None], L0_ffn_fc1_w, L0_ffn_fc1_b, L0_ffn_fc2_w, L0_ffn_fc2_b, L0_ffn_gate_pair, L0_ffn_atom_in_w, L0_ffn_atom_in_b, L0_ffn_atom_out_w, L0_ffn_atom_out_b, L0_ffn_balance_bias)[0]
    x = x + _L1_gnn_ref(_layernorm(x, axis=-1), L1_gnn_W1, L1_gnn_a_src1, L1_gnn_a_dst1, L1_gnn_b1, L1_gnn_W2, L1_gnn_a_src2, L1_gnn_a_dst2, L1_gnn_b2, edge_index)
    x = x + _L1_ffn_ref(_layernorm(x, axis=-1)[None], L1_ffn_W1, L1_ffn_b1, L1_ffn_W2, L1_ffn_b2, L1_ffn_Wo, L1_ffn_bo, L1_ffn_gamma, L1_ffn_beta)[0]
    x = x + _L2_gnn_ref(_layernorm(x, axis=-1), edge_index, L2_gnn_W, L2_gnn_b)
    x = x + _L2_ffn_ref(_layernorm(x, axis=-1)[None], L2_ffn_router_w, L2_ffn_router_b, L2_ffn_w1, L2_ffn_w2, L2_ffn_w3)[0]
    x = x + _L3_gnn_ref(_layernorm(x, axis=-1), edge_index, edge_type_34, L3_gnn_W_rel, L3_gnn_W_root, L3_gnn_b_rgcn, L3_gnn_W_gcn, L3_gnn_b_gcn)
    x = x + _L3_ffn_ref(_layernorm(x, axis=-1)[None], L3_ffn_Wr, L3_ffn_br, L3_ffn_W1, L3_ffn_b1, L3_ffn_W2, L3_ffn_b2, L3_ffn_ln_g, L3_ffn_ln_b)[0]
    return x

_drawn_inputs = setup_inputs


def setup_inputs(seed=0):
    import zlib

    import numpy as np

    out = dict(_drawn_inputs(seed))
    spreads = {'L0_gnn_b1': (0.0, 0.1),
     'L0_gnn_b2': (0.0, 0.1),
     'L0_ffn_fc1_b': (0.0, 0.1),
     'L0_ffn_fc2_b': (0.0, 0.1),
     'L0_ffn_balance_bias': (0.0, 0.8),
     'L1_gnn_b1': (0.0, 0.1),
     'L1_gnn_b2': (0.0, 0.1),
     'L1_ffn_b1': (0.0, 0.1),
     'L1_ffn_b2': (0.0, 0.1),
     'L1_ffn_gamma': (1.0, 0.2),
     'L1_ffn_beta': (0.0, 0.1),
     'L2_gnn_b': (0.0, 0.1),
     'L2_ffn_router_b': (0.0, 0.634),
     'L3_gnn_b_rgcn': (0.0, 0.359),
     'L3_gnn_b_gcn': (0.0, 0.423),
     'L3_ffn_br': (0.0, 0.1),
     'L3_ffn_b1': (0.0, 0.272),
     'L3_ffn_b2': (0.0, 0.325),
     'L3_ffn_ln_g': (1.0, 0.2),
     'L3_ffn_ln_b': (0.0, 0.29)}
    factors = {'L0_gnn_a_dst1': 4.551,
     'L0_gnn_a_src2': 2.977,
     'L0_gnn_a_dst2': 8.0,
     'L0_ffn_gate_pair': 50.904,
     'L0_ffn_atom_in_w': 3.752,
     'L0_ffn_atom_in_b': 6.362,
     'L0_ffn_atom_out_w': 3.184,
     'L0_ffn_atom_out_b': 8.0,
     'L2_ffn_router_w': 5.563,
     'L2_ffn_w1': 8.0,
     'L2_ffn_w2': 3.807,
     'L2_ffn_w3': 8.0}
    for name, (base, spread) in spreads.items():
        noise = np.random.default_rng([zlib.crc32(name.encode()), seed]).standard_normal(out[name].shape)
        drawn = base * np.exp(spread * noise) if base else spread * noise
        out[name] = jnp.asarray(drawn.astype(out[name].dtype))
    for name, factor in factors.items():
        out[name] = (out[name] * factor).astype(out[name].dtype)
    return out
```

```python
from contextlib import ExitStack, contextmanager

import numpy as np

import concourse.bass as bass
from concourse import mybir

FP32 = mybir.dt.float32
BF16 = mybir.dt.bfloat16
INT32 = mybir.dt.int32
UINT32 = mybir.dt.uint32
ALU = mybir.AluOpType
ACT = mybir.ActivationFunctionType
AX = mybir.AxisListType

P = 128
N = 256
M = N // P
D = 768
K = D // P
E = 8192
ET = E // P
G = 8
HEADS = 8
REL = 34
HALF = D // 2
NONE = -1.0e30
LN_EPS = 1e-5
DUMP = REL * N
ROWS = DUMP + 2 * N
NCLS, ATOMS, FH = 6, 5, 96
INNER = 512
EXP2, HID2 = 8, 64
EXP3, HID3 = 8, 96


class Steps:

    def __init__(self, eng, sem):
        self.eng, self.sem, self.base, self.n = eng, sem, 0, 0

    def __call__(self, ins):
        ins.then_inc(self.sem, 1)
        self.n += 1
        self.eng.wait_ge(self.sem, self.base + self.n)

    @contextmanager
    def loop(self, first, last, each):
        before = self.n
        with self.eng.Fori(first, last) as i:
            self.base, self.n = (i - first) * each + before, 0
            yield i
            assert self.n == each, self.n
        self.base, self.n = 0, before + (last - first) * each


def gnn_ffn_kernel(nc, t):
    ctx = ExitStack()
    with ctx:
        def sb(name, shape, dt=FP32):
            return ctx.enter_context(nc.sbuf_tensor(name, shape, dt))

        def sem(name):
            return ctx.enter_context(nc.semaphore(name))

        w = sb("w", [P, 2, K, D])
        x_sb = sb("x_sb", [P, M, D])
        xn = sb("xn", [P, M, D])
        xT = sb("xT", [P, K, N])
        h_sb = sb("h_sb", [P, M, D])
        hidT = sb("hidT", [P, K, N])
        z_b = sb("z_b", [P, K, N])
        b1_head = sb("b1_head", [P, K])
        neg_b = sb("neg_b", [P, K, N])
        junk = sb("junk", [P, D])
        a_bc = sb("a_bc", [P, 2, D])
        bias_bc = sb("bias_bc", [P, D])
        gamma_bc = sb("gamma_bc", [P, D])
        beta_bc = sb("beta_bc", [P, D])
        hbias_bc = sb("hbias_bc", [P, D])
        b1c = sb("b1c", [P, 2, HEADS * K])
        sbias = sb("sbias", [P, 16])
        ident = sb("ident", [P, P])
        ones = sb("ones", [P, P])
        tril = sb("tril", [P, P])
        zero = sb("zero", [P, 512], BF16)
        zrow = sb("zrow", [P, N])
        iota = sb("iota", [P, N], BF16)
        selfloop = sb("selfloop", [P, M, N])
        pcol = sb("pcol", [P, 1])
        iota8 = sb("iota8", [P, 8])
        edge_i = sb("edge_i", [P, 3, ET], INT32)
        edge_f = sb("edge_f", [P, 3, ET])
        key = sb("key", [P, ET])
        dup = sb("dup", [P, ET])
        dup_b = sb("dup_b", [P, G])
        row_f = sb("row_f", [P, ET])
        row_i = sb("row_i", [P, ET], UINT32)
        osrc = sb("osrc", [P, G, N], BF16)
        odst = sb("odst", [P, G, N], BF16)
        kdiag = sb("kdiag", [P, G, P])
        same = sb("same", [P, G, P], BF16)
        rows = sb("rows", [P, ET, N], BF16)
        add_rows = sb("add_rows", [P, N])
        add_idx = sb("add_idx", [P, 1], UINT32)
        cnt = sb("cnt", [P, 2, M, N])
        mask = sb("mask", [P, 2, M, N])
        cntT = sb("cntT", [P, M, N])
        dinv = sb("dinv", [P, M])
        scal = sb("scal", [P, 4])
        score = sb("score", [P, M, N])
        leaky = sb("leaky", [P, M, N])
        prob = sb("prob", [P, M, N])
        alpha = sb("alpha", [P, M, N])
        alphaT = sb("alphaT", [P, M, N])
        small = sb("small", [P, 64])
        stats = sb("stats", [P, M, 2, 6])
        mv = sb("mv", [P, M, 2])
        std = sb("std", [P, M])
        rstd = sb("rstd", [P, M])
        gp = sb("gp", [NCLS, 2, D])
        bb = sb("bb", [NCLS, 2])
        gate = sb("gate", [NCLS, 40])
        wdiag = sb("wdiag", [NCLS, 2, NCLS])
        hat = sb("hat", [FH + 1, ATOMS * NCLS])
        zt = sb("zt", [FH + 1, ATOMS, P])
        rw = sb("rw", [P, K, 8])
        rb = sb("rb", [P, 8])
        lg = sb("lg", [P, 16, M, 8])
        ge = sb("ge", [P, M, EXP3, HID3 + 1])
        deg = sb("deg", [P, M])
        sd = sb("sd", [P, M])
        outb = sb("outb", [P, M, D], BF16)
        ct = sb("ct", [P, 2, M, N])

        bank = [ctx.enter_context(nc.psum_tensor(f"bank{i}", [P, 512], FP32)) for i in range(8)]
        table = nc.dram_tensor("table", (ROWS, N), FP32, kind="Internal").ap()

        w_full = [sem("w_full_a"), sem("w_full_b")]
        w_used = sem("w_used")
        ld_x, ld_edge, ld_const = sem("ld_x"), sem("ld_edge"), sem("ld_const")
        ld_a, ld_bias = sem("ld_a"), sem("ld_bias")
        ld_mid = sem("ld_mid")
        ld_ct = [sem("ld_ct0"), sem("ld_ct1")]
        zeroed, cleared = sem("zeroed"), sem("cleared")
        dve_step, pool_step, act_step = sem("dve_step"), sem("pool_step"), sem("act_step")
        consts = sem("consts")
        e_hot, e_key, e_same, e_rows, e_kept = sem("e_hot"), sem("e_key"), sem("e_same"), sem("e_rows"), sem("e_kept")
        e_taken, e_dup, e_turn = sem("e_taken"), sem("e_dup"), sem("e_turn")
        e_cnt, e_mask, e_idx, e_added = sem("e_cnt"), sem("e_mask"), sem("e_idx"), sem("e_added")
        e_cntT, e_deg, e_std, e_dinv, e_cntT_kept = sem("e_cntT"), sem("e_deg"), sem("e_std"), sem("e_dinv"), sem("e_cntT_kept")
        seeded = sem("seeded")
        ln_var, ln_std, ln_xn, ln_t, ln_kept_v, ln_kept_a = [sem("ln_" + s) for s in ("var", "std", "xn", "t", "kept_v", "kept_a")]
        h_mm, h_kept = sem("h_mm"), sem("h_kept")
        scored, src_row, masked, exped, normed = [sem(s) for s in ("scored", "src_row", "masked", "exped", "normed")]
        aT_mm, aT_kept = sem("aT_mm"), sem("aT_kept")
        att_mm, z_kept, z_neg, z_exp, elu = sem("att_mm"), sem("z_kept"), sem("z_neg"), sem("z_exp"), sem("elu")
        h2_mm, att2_mm, x_new = sem("h2_mm"), sem("att2_mm"), sem("x_new")
        f_mm = [sem(f"ffn{s}_mm") for s in range(4)]
        f_act = [sem(f"ffn{s}_act") for s in range(4)]
        f_dve = [sem(f"ffn{s}_dve") for s in range(4)]
        g_mm, g_kept, g_out = sem("gcn_mm"), sem("gcn_kept"), sem("gcn_out")
        r_norm, r_t, r_tkept, r_mm, r_kept, r_out = [sem("rel_" + s) for s in ("norm", "t", "tkept", "mm", "kept", "out")]
        stored = sem("stored")


        C_GAT, C_FFN0, C_FFN1, C_GCN2, C_FFN2, C_ROOT, C_REL, C_GCN3, C_FFN3 = (0, 20), 18, 38, 41, 42, 45, 46, 80, 81

        def full(c):
            return 16 * (9 if c < C_GAT[1] else 18 + (c - C_FFN1) // 2)

        def full_head(layer, h):
            return (h + (9 * layer + 1)) * 16

        def used(c):
            return c + 3

        NCONST = 8
        LD_MID = {1: 16 * 3, 2: 16 * 6, 3: 16 * 11}

        def row_tiles(dram, n):
            return dram.rearrange("(k p) n -> p k n", p=n)

        def flat(ap):
            return ap.rearrange("p a b -> p (a b)")

        NODE_BANKS = [[(3, 0, 512, 0), (5, 0, 256, 512)], [(4, 0, 512, 0), (7, 0, 256, 512)]]
        SUM_BANKS = [[(0, 0, 512, 0), (2, 0, 256, 512)], [(1, 0, 512, 0), (2, 256, 512, 512)]]
        HT3 = [flat(hidT[0:HID3 + 1, 2 * j:2 * j + 2, :]) for j in range(3)] + [flat(z_b[0:HID3 + 1, 0:2, :])]
        REL_A = [alpha, prob]
        REL_T = [hidT, z_b]

        block = ctx.enter_context(nc.Block())

        @block.sync
        def _(sp):
            sp.dma_start(x_sb[:, :, :], row_tiles(t["x"], P)).then_inc(ld_x, 16)
            for j, name in enumerate(("src", "dst", "edge_type_34")):
                sp.dma_start(edge_i[:, j, :], t[name]).then_inc(ld_edge, 16)
            sp.wait_ge(zeroed, 1)
            sp.dma_start(table.rearrange("(p t) n -> p t n", p=P),
                         zrow[:, :].unsqueeze(1).to_broadcast([P, ROWS // P, N])).then_inc(cleared, 16)

            def load(c, half, out, dram):
                sp.wait_ge(w_used, c + 1)
                sp.dma_start(out, dram).then_inc(w_full[half], 16)

            def gat(layer, c0):
                w1, w2 = t[f"L{layer}_gnn_W1"], t[f"L{layer}_gnn_W2"]

                def up(h):
                    load(h * 2 + c0, 0, w[:, 0, :, :], row_tiles(w1[:, bass.ds(h * D, D)], P))

                def down(h):
                    load(h * 2 + (c0 + 3), 1, w[:, 1, :, :], row_tiles(w2[bass.ds(h * D, D), :], P))

                up(0)
                with sp.Fori(1, HEADS) as h:
                    up(h)
                    down(h - 1)
                down(HEADS - 1)

            gat(0, C_GAT[0])
            load(C_FFN0, 0, w[:, 0, :, 0:(ATOMS + 1) * FH], row_tiles(t["ffn0_in"], P))
            load(C_FFN0 + 1, 1, w[0:FH + 1, 1, :, :], row_tiles(t["ffn0_out"], FH + 1))
            gat(1, C_GAT[1])
            load(C_FFN1, 0, w[:, 0, :, 0:INNER], row_tiles(t["L1_ffn_W1"], P))
            load(C_FFN1 + 1, 1, w[:, 1, 0:INNER // P, :], row_tiles(t["L1_ffn_W2"], P))
            load(C_FFN1 + 2, 0, w[:, 0, :, :], row_tiles(t["L1_ffn_Wo"], P))
            load(C_GCN2, 1, w[:, 1, :, :], row_tiles(t["L2_gnn_W"], P))
            load(C_FFN2, 0, w[:, 0, :, 0:INNER], row_tiles(t["L2_ffn_w1"], P))
            load(C_FFN2 + 1, 1, w[:, 1, :, 0:INNER], row_tiles(t["L2_ffn_w2"], P))
            load(C_FFN2 + 2, 0, w[:, 0, 0:INNER // P, :], row_tiles(t["L2_ffn_w3"], P))
            load(C_ROOT, 1, w[:, 1, :, :], row_tiles(t["L3_gnn_W_root"], P))
            w_rel = t["L3_gnn_W_rel"]
            with sp.Fori(0, REL // 2) as i:
                for half in range(2):
                    load(i * 2 + (C_REL + half), half, w[:, half, :, :],
                         row_tiles(w_rel[bass.ds((i * 2 + half) * D, D), :], P))
            load(C_GCN3, 0, w[:, 0, :, :], row_tiles(t["L3_gnn_W_gcn"], P))
            load(C_FFN3, 1, w[:, 1, :, :], row_tiles(t["L3_ffn_W1"], P))
            load(C_FFN3 + 1, 0, w[0:HID3 + 1, 0, :, :], row_tiles(t["ffn3_out"][0:K * (HID3 + 1), :], HID3 + 1))
            load(C_FFN3 + 2, 1, w[0:HID3 + 1, 1, 0:EXP3 - K, :], row_tiles(t["ffn3_out"][K * (HID3 + 1):, :], HID3 + 1))
            sp.wait_ge(x_new, 8)
            sp.dma_start(row_tiles(t["out"], P), x_sb[:, :, :]).then_inc(stored, 16)
            sp.wait_ge(stored, 16)

        @block.gpsimd
        def _(pool):
            step = Steps(pool, pool_step)
            pool.memset(zrow[:, :], 0.0).then_inc(zeroed, 1)
            pool.memset(ones[:, :], 1.0).then_inc(consts, 1)
            pool.memset(zero[:, :], 0.0).then_inc(consts, 1)
            pool.memset(hat[:, :], 1.0).then_inc(w_used, 2)
            pool.memset(zt[:, :, :], 0.0).then_inc(e_kept, 4)
            step(pool.memset(ident[:, :], 0.0))
            step(pool.memset(selfloop[:, :, :], 0.0))
            step(pool.memset(tril[:, :], 1.0))
            pool.affine_select(out=ident[:, :], in_=ident[:, :], compare_op=ALU.not_equal, fill=1.0, base=0,
                               pattern=[[-1, P]], channel_multiplier=1).then_inc(consts, 1)
            pool.affine_select(out=selfloop[:, :, :], in_=selfloop[:, :, :], compare_op=ALU.not_equal, fill=1.0,
                               base=0, pattern=[[P, M], [-1, N]], channel_multiplier=1).then_inc(consts, 1)
            pool.affine_select(out=tril[:, :], in_=tril[:, :], compare_op=ALU.is_gt, fill=0.0, base=0,
                               pattern=[[-1, P]], channel_multiplier=1).then_inc(consts, 1)
            pool.iota(iota[:, :], pattern=[[1, N]], base=0, channel_multiplier=0,
                      allow_small_or_imprecise_dtypes=True).then_inc(consts, 1)
            pool.iota(pcol[:, :], pattern=[[0, 1]], base=DUMP, channel_multiplier=1,
                      allow_small_or_imprecise_dtypes=True).then_inc(consts, 1)
            pool.iota(iota8[:, :], pattern=[[1, 8]], base=-8, channel_multiplier=0,
                      allow_small_or_imprecise_dtypes=True).then_inc(consts, 1)

            pool.wait_ge(e_idx, 1)
            pool.wait_ge(e_kept, 4 + ET // 2)
            pool.wait_ge(cleared, 16)
            with pool.Fori(0, ET) as i:
                pool.tensor_copy(add_rows[:, :], rows[:, bass.ds(i, 1), :].rearrange("p a n -> p (a n)")).then_inc(e_taken, 1)
                pool.tensor_copy(add_idx[:, :], row_i[:, bass.ds(i, 1)]).then_inc(e_taken, 1)
                pool.wait_ge(e_taken, i * 2 + 2)
                pool.sem_inc(e_turn, 1)
                pool.indirect_dma_start(
                    out=table, out_offset=bass.IndirectOffsetOnAxis(ap=add_idx[:, :], axis=0),
                    in_=add_rows[:, :], in_offset=None, compute_op=ALU.add).then_inc(e_added, 16)
                pool.wait_ge(e_added, i * 16 + 16)

        @block.tensor
        def _(pe):
            def mm(out, lhsT, rhs, start=True, stop=True, **kw):
                return pe.matmul(out, lhsT, rhs, start=start, stop=stop, **kw)

            def seed(banks):
                for b in banks:
                    last = mm(bank[b][:, :], zero[:, 0:P], zero[:, :], True, False, skip_group_check=True)
                return last

            def transposed(i):
                pe.wait_ge(ln_xn, 2 * i + 2)
                for j in range(3):
                    for k in (2 * j, 2 * j + 1):
                        for m in range(M):
                            last = pe.transpose(bank[3 + j][:, (k % 2) * N + m * P:(k % 2) * N + (m + 1) * P],
                                                xn[:, m, k * P:(k + 1) * P], ident[:, :])
                    last.then_inc(ln_t, 1)
                pe.wait_ge(ln_kept_v, 2 * i + 2)
                pe.wait_ge(ln_kept_a, i + 1)

            def nodes(m, banks, lhs, rhs):
                for (b, c0, c1, o) in banks[m]:
                    n = len(lhs)
                    for k in range(n):
                        last = mm(bank[b][:, c0:c1], lhs[k], rhs(k, o, o + c1 - c0), k == 0, k == n - 1)
                return last

            def add(m, lhs, rhs, end=False):
                n = len(lhs)
                for k in range(n):
                    for (b, c0, c1, o) in SUM_BANKS[m]:
                        last = mm(bank[b][:, c0:c1], lhs[k], rhs(k, o, o + c1 - c0), False, end and k == n - 1,
                                  skip_group_check=True)
                return last

            def node_tile(buf, m, ks):
                return [buf[:, k, m * P:(m + 1) * P] for k in range(ks)]

            def of_w(half, rows_=P):
                return lambda k, c0, c1: w[0:rows_, half, k, c0:c1]

            pe.wait_ge(consts, NCONST)
            seed((0,)).then_inc(e_rows, 1)
            with pe.Fori(0, ET // G) as b:
                pe.wait_ge(e_hot, b + 1)
                for g in range(G):
                    for m in range(M):
                        mm(bank[0][:, m * N:(m + 1) * N], odst[:, g, m * P:(m + 1) * P], osrc[:, g, :], False, False,
                           skip_group_check=True)
                    last = mm(bank[1 + g // 4][:, (g % 4) * P:(g % 4 + 1) * P], ones[:, :], kdiag[:, g, :])
                last.then_inc(e_key, 1)
                pe.wait_ge(e_same, b + 1)
                pe.wait_ge(e_kept, b * 4 + 4)
                for g in range(G):
                    last = mm(bank[3 + g // 2][:, (g % 2) * N:(g % 2 + 1) * N], same[:, g, :], osrc[:, g, :])
                last.then_inc(e_rows, 1)
            mm(bank[0][:, :], zero[:, 0:P], zero[:, :], False, True, skip_group_check=True).then_inc(e_cnt, 1)
            pe.wait_ge(e_mask, 1)
            for sm in range(M):
                for m in range(M):
                    last = pe.transpose(bank[1][:, sm * N + m * P:sm * N + (m + 1) * P], cnt[:, 0, m, sm * P:(sm + 1) * P], ident[:, :])
            last.then_inc(e_cntT, 1)
            pe.wait_ge(e_cntT_kept, 1)

            def spread(u):
                pe.wait_ge(scored, u + 1)
                for m in range(M):
                    last = mm(bank[7][:, m * P:(m + 1) * P], scal[:, m:m + 1].to_broadcast([P, P]), ident[:, :])
                last.then_inc(src_row, 1)

            def turn(u):
                pe.wait_ge(normed, u + 1)
                for sm in range(M):
                    for m in range(M):
                        last = pe.transpose(bank[7][:, sm * N + m * P:sm * N + (m + 1) * P], alpha[:, m, sm * P:(sm + 1) * P], ident[:, :])
                last.then_inc(aT_mm, 1)
                pe.wait_ge(aT_kept, u + 1)

            def gat(layer):
                c0 = C_GAT[layer]
                seed((0, 1, 2))

                def up(h, first=False):
                    pe.wait_ge(w_full[0], full_head(layer, h))
                    for m, banks in ((0, (5, 6)), (1, (3, 4))):
                        if not first:
                            pe.wait_ge(z_kept, (h + HEADS * layer) * 3 + (-2 if m == 0 else 0))
                        for k in range(K):
                            for j in range(2):
                                last = mm(bank[banks[j]][:, 0:HALF], xT[:, k, m * P:(m + 1) * P],
                                          w[:, 0, k, j * HALF:(j + 1) * HALF], k == 0, k == K - 1)
                        last.then_inc(*((h_mm, 1) if m == 0 else (w_used, 2 if first else 1)))

                def down(h, m, last_head=False):
                    if m == 0:
                        pe.wait_ge(elu, (h + HEADS * layer) * 3 + 3)
                        pe.wait_ge(w_full[1], full_head(layer, h))
                    last = add(m, node_tile(hidT, m, K), of_w(1), last_head)
                    if m == 1:
                        last.then_inc(w_used, 2 if last_head else 1)

                def attend(h):
                    for j, b in enumerate((5, 3, 4)):
                        for k in (2 * j, 2 * j + 1):
                            for sm in range(M):
                                last = mm(bank[b][:, (k % 2) * N:(k % 2 + 1) * N], h_sb[:, sm, k * P:(k + 1) * P],
                                          alphaT[:, sm, :], sm == 0, sm == M - 1)
                        last.then_inc(att_mm, 1)

                up(0, True)
                spread(9 * layer)
                turn(9 * layer)
                attend(0)
                with pe.Fori(1, HEADS) as h:
                    up(h)
                    down(h - 1, 0)
                    spread(h + 9 * layer)
                    down(h - 1, 1)
                    turn(h + 9 * layer)
                    attend(h)
                down(HEADS - 1, 0, True)
                down(HEADS - 1, 1, True)
                spread(HEADS + 9 * layer)
                turn(HEADS + 9 * layer)
                for m in range(M):
                    nodes(m, NODE_BANKS, [alphaT[:, sm, m * P:(m + 1) * P] for sm in range(M)],
                          lambda sm, a, b: h_sb[:, sm, a:b]).then_inc(att2_mm, 1)

            transposed(0)
            gat(0)

            transposed(1)
            pe.wait_ge(w_full[0], full(C_FFN0))
            for k in range(K):
                last = mm(bank[3][0:FH, 0:N], w[:, 0, k, 0:FH], xT[:, k, :], k == 0, k == K - 1)
            last.then_inc(f_mm[0], 1)
            for a in range(ATOMS):
                for k in range(K):
                    last = mm(bank[4][0:FH, a * NCLS:(a + 1) * NCLS], w[:, 0, k, (a + 1) * FH:(a + 2) * FH],
                              xT[:, k, 0:NCLS], k == 0, k == K - 1)
            last.then_inc(w_used, 1)
            pe.wait_ge(f_dve[0], 3)
            mm(bank[5][0:FH + 1, 0:2 * NCLS], ones[0:NCLS, 0:FH + 1], flat(wdiag[:, :, :])).then_inc(f_mm[0], 1)
            pe.wait_ge(f_dve[0], 5)
            pe.wait_ge(w_full[1], full(C_FFN0 + 1))
            nodes(0, NODE_BANKS, [hidT[0:FH + 1, 0, 0:P]] + [zt[:, d, :] for d in range(ATOMS)], of_w(1, FH + 1)).then_inc(f_mm[0], 1)
            nodes(1, NODE_BANKS, [hidT[0:FH + 1, 0, P:N]], of_w(1, FH + 1)).then_inc(w_used, 1)

            transposed(2)
            gat(1)

            transposed(3)

            def columns(count, half, rhs, ks, first_bank, marks):
                for c in range(count):
                    for k in range(ks):
                        last = mm(bank[first_bank + c // 2][:, (c % 2) * N:(c % 2 + 1) * N], w[:, half, k, c * P:(c + 1) * P],
                                  rhs[:, k, :], k == 0, k == ks - 1)
                    if c % 2:
                        last.then_inc(marks[c // 2], 1)

            pe.wait_ge(w_full[0], full(C_FFN1))
            columns(INNER // P, 0, xT, K, 3, (f_mm[1], w_used))
            pe.wait_ge(f_act[1], 4)
            pe.wait_ge(w_full[1], full(C_FFN1 + 1))
            columns(K, 1, z_b, INNER // P, 5, (f_mm[1], f_mm[1], w_used))
            pe.wait_ge(f_act[1], 10)
            pe.wait_ge(w_full[0], full(C_FFN1 + 2))
            nodes(0, NODE_BANKS, node_tile(hidT, 0, K), of_w(0)).then_inc(f_mm[1], 1)
            nodes(1, NODE_BANKS, node_tile(hidT, 1, K), of_w(0)).then_inc(w_used, 1)

            def gcn(s, half, c):
                pe.wait_ge(w_full[half], full(c))
                nodes(0, NODE_BANKS, node_tile(xT, 0, K), of_w(half)).then_inc(g_mm, 1)
                nodes(1, NODE_BANKS, node_tile(xT, 1, K), of_w(half)).then_inc(w_used, 1)
                pe.wait_ge(g_kept, 4 * s + 4)
                for m in range(M):
                    nodes(m, NODE_BANKS, [cntT[:, sm, m * P:(m + 1) * P] for sm in range(M)],
                          lambda sm, a, b: h_sb[:, sm, a:b]).then_inc(g_out, 1)

            def router(s):
                pe.wait_ge(ld_mid, LD_MID[s])
                for m in range(M):
                    for k in range(K):
                        last = mm(bank[6][:, m * 8:(m + 1) * 8], xT[:, k, m * P:(m + 1) * P], rw[:, k, :], k == 0, k == K - 1)
                last.then_inc(f_mm[s], 1)

            transposed(4)
            gcn(0, 1, C_GCN2)

            transposed(5)
            router(2)
            pe.wait_ge(w_full[0], full(C_FFN2))
            for m in range(M):
                for k in range(K):
                    last = mm(bank[3 + m][:, :], xT[:, k, m * P:(m + 1) * P], w[:, 0, k, 0:INNER], k == 0, k == K - 1)
            last.then_inc(w_used, 1)
            pe.wait_ge(w_full[1], full(C_FFN2 + 1))
            for m, b in enumerate((5, 7)):
                for k in range(K):
                    last = mm(bank[b][:, :], xT[:, k, m * P:(m + 1) * P], w[:, 1, k, 0:INNER], k == 0, k == K - 1)
            last.then_inc(w_used, 1)
            pe.wait_ge(f_dve[2], 2)
            for j in range(2):
                for k in (2 * j, 2 * j + 1):
                    for m in range(M):
                        last = pe.transpose(bank[3 + j][:, (k % 2) * N + m * P:(k % 2) * N + (m + 1) * P],
                                            flat(neg_b[:, 2 * m:2 * m + 2, :])[:, k * P:(k + 1) * P], ident[:, :])
                last.then_inc(f_mm[2], 1)
            pe.wait_ge(f_act[2], 5)
            pe.wait_ge(w_full[0], full(C_FFN2 + 2))
            nodes(0, NODE_BANKS, node_tile(hidT, 0, INNER // P), of_w(0)).then_inc(f_mm[2], 1)
            nodes(1, NODE_BANKS, node_tile(hidT, 1, INNER // P), of_w(0)).then_inc(w_used, 1)

            transposed(6)
            seed((0, 1, 2))
            pe.wait_ge(w_full[1], full(C_ROOT))
            add(0, node_tile(xT, 0, K), of_w(1))
            add(1, node_tile(xT, 1, K), of_w(1)).then_inc(w_used, 1)

            def turn_rel(r, half):
                pe.wait_ge(r_norm, r + 1)
                for sm in range(M):
                    for m in range(M):
                        last = pe.transpose(bank[7][:, sm * N + m * P:sm * N + (m + 1) * P], REL_A[half][:, m, sm * P:(sm + 1) * P], ident[:, :])
                last.then_inc(r_t, 1)

            def mean(r):
                pe.wait_ge(r_tkept, r + 1)
                for j in range(3):
                    for k in (2 * j, 2 * j + 1):
                        for sm in range(M):
                            last = mm(bank[3 + j][:, (k % 2) * N:(k % 2 + 1) * N], xn[:, sm, k * P:(k + 1) * P],
                                      alphaT[:, sm, :], sm == 0, sm == M - 1)
                    last.then_inc(r_mm, 1)

            def relation(r, half, ahead=True, end=False):
                if ahead:
                    turn_rel(r + 1, 1 - half)
                pe.wait_ge(r_kept, r * 3 + 3)
                pe.wait_ge(w_full[half], full(C_REL) + (r - half) * 8)
                add(0, node_tile(REL_T[half], 0, K), of_w(half), end)
                if ahead:
                    mean(r + 1)
                add(1, node_tile(REL_T[half], 1, K), of_w(half), end).then_inc(w_used, 1)

            turn_rel(0, 0)
            mean(0)
            with pe.Fori(0, REL // 2 - 1) as i:
                relation(i * 2, 0)
                relation(i * 2 + 1, 1)
            relation(REL - 2, 0)
            relation(REL - 1, 1, False, True)
            transposed(7)
            gcn(1, 0, C_GCN3)

            transposed(8)
            router(3)
            pe.wait_ge(w_full[1], full(C_FFN3))
            nodes(0, NODE_BANKS, node_tile(xT, 0, K), of_w(1)).then_inc(f_mm[3], 1)
            nodes(1, NODE_BANKS, node_tile(xT, 1, K), of_w(1)).then_inc(w_used, 1)
            pe.wait_ge(f_dve[3], 3)
            for j in range(4):
                for e in (2 * j, 2 * j + 1):
                    for m in range(M):
                        last = pe.transpose(bank[3 + j][0:HID3 + 1, (e % 2) * N + m * P:(e % 2) * N + (m + 1) * P],
                                            ge[:, m, e, :], ident[:, :])
                last.then_inc(f_mm[3], 1)
            pe.wait_ge(f_act[3], 6)
            pe.wait_ge(w_full[0], full(C_FFN3 + 1))
            pe.wait_ge(w_full[1], full(C_FFN3 + 2))
            for m in range(M):
                last = nodes(m, NODE_BANKS, [HT3[e // 2][:, (e % 2) * N + m * P:(e % 2) * N + (m + 1) * P] for e in range(EXP3)],
                             lambda e, a, b: w[0:HID3 + 1, e // K, e % K, a:b])
                last.then_inc(w_used, 1)

        @block.scalar
        def _(act):
            act.dma_start(b1c[:, 0, :], t["L0_gnn_b1"]).then_inc(ld_const, 16)
            act.dma_start(b1c[:, 1, :], t["L1_gnn_b1"]).then_inc(ld_const, 16)
            act.dma_start(gp[:, :, :], t["L0_ffn_gate_pair"]).then_inc(ld_const, 16)
            act.dma_start(bb[:, :], t["L0_ffn_balance_bias"]).then_inc(ld_const, 16)
            act.dma_start(sbias[0:FH, 0:ATOMS + 1], t["ffn0_bias"]).then_inc(ld_const, 16)
            act.dma_start(sbias[:, 6:10], t["L1_ffn_b1"]).then_inc(ld_const, 16)
            act.dma_start(sbias[:, 10:16], t["L1_ffn_b2"]).then_inc(ld_const, 16)

            def row_bc(out, dram, mark):
                act.dma_start(out, dram.partition_broadcast(P)).then_inc(mark, 16)

            def load_heads(layer, h):
                for j, a in enumerate(("a_src1", "a_dst1")):
                    row_bc(a_bc[:, j, :], t[f"L{layer}_gnn_{a}"][bass.ds(h, 1), :].rearrange("a n -> (a n)"), ld_a)

            def load_last(layer):
                for j, a in enumerate(("a_src2", "a_dst2")):
                    row_bc(a_bc[:, j, :], t[f"L{layer}_gnn_{a}"][0, :], ld_a)

            def keep(out, ps, mark, func=ACT.Copy, **kw):
                act.activation(out, ps, func, **kw).then_inc(mark, 1)

            row_bc(bias_bc[:, :], t["L0_gnn_b2"], ld_bias)
            load_heads(0, 0)
            act.wait_ge(ld_const, 16 * 7)

            with act.Fori(0, ET // G) as b:
                act.wait_ge(e_rows, b + 2)
                for j in range(G // 2):
                    keep(flat(rows[:, bass.ds(b * G + 2 * j, 2), :]), bank[3 + j][:, :], e_kept)
            act.wait_ge(e_deg, 1)
            keep(sd[:, :], deg[:, :], e_std, ACT.Sqrt)
            act.wait_ge(e_cntT, 1)
            keep(flat(cntT[:, :, :]), bank[1][:, :], e_cntT_kept)

            def deviation(s):
                act.wait_ge(ln_var, s + 1)
                keep(std[:, :], mv[:, :, 1], ln_std, ACT.Sqrt, bias=LN_EPS)

            def transposed(i):
                act.wait_ge(ln_t, 3 * i + 2)
                keep(flat(xT[:, 2:4, :]), bank[4][:, :], ln_kept_a)

            def attend(u, ahead):
                act.wait_ge(masked, u + 1)
                for m in range(M):
                    keep(prob[:, m, :], score[:, m, :], exped, ACT.Exp, bias=small[:, m:m + 1])
                ahead()
                act.wait_ge(aT_mm, u + 1)
                keep(flat(alphaT[:, :, :]), bank[7][:, :], aT_kept)

            def gat(layer, after):
                def head(h, ahead):
                    u = h + 9 * layer
                    for m, banks in ((0, (5, 6)), (1, (3, 4))):
                        if m == 0:
                            act.wait_ge(h_mm, h + (HEADS * layer + 1))
                        else:
                            act.wait_ge(w_used, h * 2 + used(C_GAT[layer]))
                        for j in range(2):
                            keep(h_sb[:, m, j * HALF:(j + 1) * HALF], bank[banks[j]][:, 0:HALF], h_kept)
                    attend(u, ahead)
                    a = (h + HEADS * layer) * 3
                    for j, b in enumerate((5, 3, 4)):
                        act.wait_ge(att_mm, a + (j + 1))
                        for k in (2 * j, 2 * j + 1):
                            last = act.activation(z_b[:, k, :], bank[b][:, (k % 2) * N:(k % 2 + 1) * N], ACT.Identity,
                                                  bias=b1_head[:, k:k + 1])
                        last.then_inc(z_kept, 1)
                    for j in range(3):
                        act.wait_ge(z_neg, a + (j + 1))
                        keep(neg_b[:, 2 * j:2 * j + 2, :], neg_b[:, 2 * j:2 * j + 2, :], z_exp, ACT.Exp)

                with act.Fori(0, HEADS - 1) as h:
                    head(h, lambda: load_heads(layer, h + 1))
                head(HEADS - 1, lambda: load_last(layer))
                act.wait_ge(w_used, used(C_GAT[layer] + 17))
                for m in range(M):
                    for (b, c0, c1, o) in SUM_BANKS[m]:
                        keep(h_sb[:, m, o:o + c1 - c0], bank[b][:, c0:c1], h_kept)
                attend(HEADS + 9 * layer, after)

            deviation(0)
            transposed(0)
            gat(0, lambda: load_heads(1, 0))

            deviation(1)
            transposed(1)
            row_bc(bias_bc[:, :], t["L1_gnn_b2"], ld_bias)
            act.wait_ge(f_dve[0], 1)
            keep(gate[:, 8:11], gate[:, 0:3], f_act[0], ACT.Sqrt)
            act.wait_ge(f_dve[0], 2)
            keep(gate[:, 24:26], gate[:, 22:24], f_act[0], ACT.Exp)
            act.wait_ge(f_mm[0], 1)
            keep(hidT[0:FH, 0, :], bank[3][0:FH, 0:N], f_act[0], ACT.Gelu, bias=sbias[0:FH, 0:1])
            act.wait_ge(w_used, used(C_FFN0))
            for a in range(ATOMS):
                keep(hat[0:FH, a * NCLS:(a + 1) * NCLS], bank[4][0:FH, a * NCLS:(a + 1) * NCLS], f_act[0], ACT.Gelu,
                     bias=sbias[0:FH, a + 1:a + 2])

            deviation(2)
            transposed(2)
            gat(1, lambda: None)

            deviation(3)
            transposed(3)
            row_bc(hbias_bc[:, :], t["L1_ffn_bo"], ld_mid)
            row_bc(gamma_bc[:, :], t["L1_ffn_gamma"], ld_mid)
            row_bc(beta_bc[:, :], t["L1_ffn_beta"], ld_mid)
            row_bc(bias_bc[:, :], t["L2_gnn_b"], ld_bias)
            for c in range(INNER // P):
                act.wait_ge(*((f_mm[1], 1) if c < 2 else (w_used, used(C_FFN1))))
                keep(z_b[:, c, :], bank[3 + c // 2][:, (c % 2) * N:(c % 2 + 1) * N], f_act[1], ACT.Relu,
                     bias=sbias[:, 6 + c:7 + c])
            for c in range(K):
                act.wait_ge(*((f_mm[1], 2 + c // 2) if c < 4 else (w_used, used(C_FFN1 + 1))))
                keep(hidT[:, c, :], bank[5 + c // 2][:, (c % 2) * N:(c % 2 + 1) * N], f_act[1], ACT.Identity,
                     bias=sbias[:, 10 + c:11 + c])
            deviation(4)

            def gcn(s, c):
                act.wait_ge(e_dinv, 1)
                for m in range(M):
                    act.wait_ge(*((g_mm, s + 1) if m == 0 else (w_used, used(c))))
                    for (b, c0, c1, o) in NODE_BANKS[m]:
                        keep(h_sb[:, m, o:o + c1 - c0], bank[b][:, c0:c1], g_kept, scale=dinv[:, m:m + 1])

            deviation(5)
            transposed(4)
            act.dma_start(rw[:, :, :], row_tiles(t["L2_ffn_router_w"], P)).then_inc(ld_mid, 16)
            row_bc(rb[:, :], t["L2_ffn_router_b"], ld_mid)
            row_bc(hbias_bc[:, :], t["L3_gnn_b_rgcn"], ld_mid)
            gcn(0, C_GCN2)

            deviation(6)
            transposed(5)
            row_bc(bias_bc[:, :], t["L3_gnn_b_gcn"], ld_bias)
            act.wait_ge(f_dve[2], 1)
            keep(lg[:, 2, :, :], lg[:, 1, :, :], f_act[2], ACT.Exp)
            act.wait_ge(w_used, used(C_FFN2))
            for m in range(M):
                keep(flat(z_b[:, 2 * m:2 * m + 2, :]), bank[3 + m][:, :], f_act[2], ACT.Silu)
            for j in range(2):
                act.wait_ge(f_mm[2], 2 + j)
                keep(flat(hidT[:, 2 * j:2 * j + 2, :]), bank[3 + j][:, :], f_act[2])
            for m in range(M):
                act.wait_ge(*((f_mm[2], 4) if m == 0 else (w_used, used(C_FFN2 + 2))))
                for (b, c0, c1, o) in NODE_BANKS[m]:
                    keep(outb[:, m, o:o + c1 - c0], bank[b][:, c0:c1], f_act[2])

            deviation(7)
            transposed(6)
            act.wait_ge(e_added, 16 * ET)

            def load_counts(r, half):
                act.dma_start(ct[:, half, :, :], table[bass.ds(r * N, N), :].rearrange("(m p) n -> p m n", p=P))\
                   .then_inc(ld_ct[half], 16)

            load_counts(0, 0)
            load_counts(1, 1)
            with act.Fori(0, REL // 2) as i:
                for half in range(2):
                    act.wait_ge(r_t, i * 2 + (half + 1))
                    keep(flat(alphaT[:, :, :]), bank[7][:, :], r_tkept)
                    load_counts(i * 2 + (half + 2), half)
                    for j in range(3):
                        act.wait_ge(r_mm, i * 6 + (3 * half + j + 1))
                        keep(flat(REL_T[half][:, 2 * j:2 * j + 2, :]), bank[3 + j][:, :], r_kept)
            transposed(7)
            gcn(1, C_GCN3)

            deviation(8)
            transposed(8)
            act.dma_start(rw[:, :, :], row_tiles(t["L3_ffn_Wr"], P)).then_inc(ld_mid, 16)
            row_bc(rb[:, :], t["L3_ffn_br"], ld_mid)
            row_bc(hbias_bc[:, :], t["L3_ffn_b1"], ld_mid)
            row_bc(gamma_bc[:, :], t["L3_ffn_ln_g"], ld_mid)
            row_bc(beta_bc[:, :], t["L3_ffn_ln_b"], ld_mid)
            act.wait_ge(f_dve[3], 1)
            keep(lg[:, 2, :, :], lg[:, 1, :, :], f_act[3], ACT.Exp)
            act.wait_ge(f_dve[3], 2)
            keep(h_sb[:, :, :], h_sb[:, :, :], f_act[3], ACT.Gelu_apprx_tanh)
            for j in range(4):
                act.wait_ge(f_mm[3], 3 + j)
                keep(HT3[j], bank[3 + j][0:HID3 + 1, :], f_act[3])
            deviation(9)

        @block.vector
        def _(dve):
            step = Steps(dve, dve_step)
            add_, mul, mx = ALU.add, ALU.mult, ALU.max

            def tt(out, a, b, op):
                return dve.tensor_tensor(out, a, b, op)

            def ts(out, a, s1, op0, s2=None, op1=None):
                return dve.tensor_scalar(out, a, s1, s2, op0, op1) if op1 is not None else dve.tensor_scalar(out, a, s1, None, op0)

            def dot(out, a, b, acc, op0=mul, op1=add_):
                return dve.tensor_tensor_reduce(out=out, in0=a, in1=b, scale=1.0, scalar=0.0, op0=op0, op1=op1, accum_out=acc)

            def stats_of(buf):
                for m in range(M):
                    for j in range(2):
                        last = dve.bn_stats(stats[:, m, j, :], buf[:, m, j * HALF:(j + 1) * HALF])
                step(last)
                for m in range(M):
                    last = dve.bn_aggr(mv[:, m, :], flat(stats[:, m, :, :]))
                last.then_inc(ln_var, 1)

            def normalised(s, buf):
                stats_of(buf)
                dve.wait_ge(ln_std, s + 1)
                step(dve.reciprocal(rstd[:, :], std[:, :]))
                return [ts(xn[:, m, :], buf[:, m, :], mv[:, m, 0:1], ALU.subtract, rstd[:, m:m + 1], mul) for m in range(M)]

            def transposed(i):
                for j, b in ((0, 3), (2, 5)):
                    dve.wait_ge(ln_t, 3 * i + j + 1)
                    dve.tensor_copy(flat(xT[:, 2 * j:2 * j + 2, :]), bank[b][:, :]).then_inc(ln_kept_v, 1)

            def norm(s, i, bias=None):
                for ins in normalised(s, x_sb):
                    ins.then_inc(ln_xn, 1)
                dve.wait_ge(ln_xn, 2 * i + 2)
                transposed(i)
                if bias is not None:
                    dve.wait_ge(ld_bias, 16 * (bias + 1))
                    for m in range(M):
                        last = tt(x_sb[:, m, :], x_sb[:, m, :], bias_bc[:, :], add_)
                    step(last)

            dve.wait_ge(ld_edge, 48)
            dve.wait_ge(consts, NCONST)
            step(dve.tensor_copy(edge_f[:, :, :], edge_i[:, :, :]))
            step(dve.scalar_tensor_tensor(key[:, :], edge_f[:, 2, :], float(N), edge_f[:, 1, :], mul, add_))
            with dve.Fori(0, ET // G) as b:
                dve.wait_ge(e_rows, b + 1)
                for g in range(G):
                    dve.tensor_scalar(osrc[:, g, :], iota[:, :], edge_f[:, 0, bass.ds(b * G + g, 1)], None, ALU.is_equal)
                    dve.tensor_scalar(odst[:, g, :], iota[:, :], edge_f[:, 1, bass.ds(b * G + g, 1)], None, ALU.is_equal)
                    last = dve.tensor_scalar(kdiag[:, g, :], ident[:, :], key[:, bass.ds(b * G + g, 1)], None, mul)
                last.then_inc(e_hot, 1)
                dve.wait_ge(e_key, b + 1)
                for g in range(G):
                    last = dve.tensor_scalar(same[:, g, :], bank[1 + g // 4][:, (g % 4) * P:(g % 4 + 1) * P],
                                             key[:, bass.ds(b * G + g, 1)], None, ALU.is_equal)
                last.then_inc(e_same, 1)
                dve.wait_ge(e_same, b + 1)
                for g in range(G):
                    last = dot(kdiag[:, g, :], same[:, g, :], tril[:, :], dup_b[:, g:g + 1])
                last.then_inc(e_dup, 1)
                dve.wait_ge(e_dup, b + 1)
                dve.tensor_copy(dup[:, bass.ds(b * G, G)], dup_b[:, :])
            step(ts(junk[:, 0:1], pcol[:, 0:1], 1.0, mul))
            step(ts(dup[:, :], dup[:, :], 1.0, ALU.min))
            step(ts(row_f[:, :], key[:, :], -1.0, mul, pcol[:, 0:1], add_))
            step(tt(row_f[:, :], row_f[:, :], dup[:, :], mul))
            step(tt(row_f[:, :], row_f[:, :], key[:, :], add_))
            dve.tensor_copy(row_i[:, :], row_f[:, :]).then_inc(e_idx, 1)
            dve.wait_ge(e_cnt, 1)
            dve.tensor_copy(flat(cnt[:, 1, :, :]), bank[0][:, :])
            tt(flat(cnt[:, 0, :, :]), bank[0][:, :], flat(selfloop[:, :, :]), add_).then_inc(e_mask, 1)
            dve.wait_ge(e_mask, 1)
            for j in range(2):
                last = ts(flat(mask[:, j, :, :]), flat(cnt[:, j, :, :]), 0.0, ALU.is_equal, NONE, mul)
            step(last)
            dve.tensor_reduce(deg[:, :], cnt[:, 0, :, :], AX.X, add_).then_inc(e_deg, 1)
            dve.wait_ge(e_std, 1)
            dve.reciprocal(dinv[:, :], sd[:, :]).then_inc(e_dinv, 1)
            dve.wait_ge(e_dinv, 1)

            def scores(u, layer):
                dve.wait_ge(ld_a, u * 32 + 32)
                for m in range(M):
                    dve.wait_ge(h_kept, u * 4 + (2 * m + 2))
                    for j in range(2):
                        last = dot(junk[:, :], h_sb[:, m, :], a_bc[:, j, :], scal[:, 2 * j + m:2 * j + m + 1])
                        if m == 0 or j == 0:
                            step(last)
                last.then_inc(scored, 1)
                dve.wait_ge(src_row, u + 1)
                for m in range(M):
                    last = ts(score[:, m, :], bank[7][:, 0:N], scal[:, 2 + m:3 + m], add_)
                step(last)
                step(dve.scalar_tensor_tensor(flat(leaky[:, :, :]), flat(score[:, :, :]), 0.2, flat(score[:, :, :]), mul, mx))
                step(tt(flat(score[:, :, :]), flat(leaky[:, :, :]), flat(mask[:, layer, :, :]), add_))
                dve.tensor_reduce(small[:, 0:M], score[:, :, :], AX.X, mx, negate=True).then_inc(masked, 1)
                dve.wait_ge(exped, u * 2 + 2)
                for m in range(M):
                    last = dot(leaky[:, m, :], prob[:, m, :], cnt[:, layer, m, :], small[:, 2 + m:3 + m])
                step(last)
                if layer == 1:
                    step(ts(small[:, 2:4], small[:, 2:4], 1e-16, add_))
                step(dve.reciprocal(small[:, 4:6], small[:, 2:4]))
                for m in range(M):
                    last = ts(alpha[:, m, :], leaky[:, m, :], small[:, 4 + m:5 + m], mul)
                last.then_inc(normed, 1)

            def gat(layer):
                steps = 9 + layer
                with step.loop(0, HEADS, steps) as h:
                    step(dve.tensor_copy(b1_head[:, :], b1c[:, layer, bass.ds(h * K, K)]))
                    scores(h + 9 * layer, layer)
                    a = (h + HEADS * layer) * 3
                    for j in range(3):
                        dve.wait_ge(z_kept, a + (j + 1))
                        ts(flat(neg_b[:, 2 * j:2 * j + 2, :]), flat(z_b[:, 2 * j:2 * j + 2, :]), 0.0, ALU.min).then_inc(z_neg, 1)
                    for j in range(3):
                        dve.wait_ge(z_exp, a + (j + 1))
                        dve.scalar_tensor_tensor(flat(hidT[:, 2 * j:2 * j + 2, :]), flat(neg_b[:, 2 * j:2 * j + 2, :]), -1.0,
                                                 flat(z_b[:, 2 * j:2 * j + 2, :]), add_, mx).then_inc(elu, 1)
                scores(HEADS + 9 * layer, layer)
                for m in range(M):
                    dve.wait_ge(att2_mm, 2 * layer + m + 1)
                    last = to_stream(m)
                done(last)

            def to_stream(m):
                for (b, c0, c1, o) in NODE_BANKS[m]:
                    last = tt(x_sb[:, m, o:o + c1 - c0], x_sb[:, m, o:o + c1 - c0], bank[b][:, c0:c1], add_)
                return last

            blocks = [0]

            def done(last):
                blocks[0] += 1
                last.then_inc(x_new, 1)
                dve.wait_ge(x_new, blocks[0])

            dve.wait_ge(ld_x, 16)
            norm(0, 0, bias=0)
            gat(0)

            norm(1, 1)
            cls = xn[0:NCLS, 0, :]
            dve.wait_ge(ld_const, 16 * 7)
            step(dot(junk[0:NCLS, :], cls, cls, gate[:, 0:1]))
            for r in range(2):
                step(dot(junk[0:NCLS, :], gp[:, r, :], gp[:, r, :], gate[:, 1 + r:2 + r]))
                last = dot(junk[0:NCLS, :], cls, gp[:, r, :], gate[:, 3 + r:4 + r])
                if r == 0:
                    step(last)
            last.then_inc(f_dve[0], 1)
            dve.wait_ge(f_act[0], 1)
            step(ts(gate[:, 12:15], gate[:, 8:11], 1e-12, mx))
            step(dve.reciprocal(gate[:, 16:19], gate[:, 12:15]))
            step(ts(gate[:, 20:22], gate[:, 3:5], gate[:, 16:17], mul))
            step(tt(gate[:, 20:22], gate[:, 20:22], gate[:, 17:19], mul))
            step(tt(gate[:, 20:22], gate[:, 20:22], bb[:, :], add_))
            step(dve.tensor_reduce(gate[:, 19:20], gate[:, 20:22], AX.X, mx, negate=True))
            ts(gate[:, 22:24], gate[:, 20:22], gate[:, 19:20], add_).then_inc(f_dve[0], 1)
            dve.wait_ge(f_act[0], 2)
            step(dve.tensor_reduce(gate[:, 26:27], gate[:, 24:26], AX.X, add_))
            step(dve.reciprocal(gate[:, 27:28], gate[:, 26:27]))
            step(ts(gate[:, 28:30], gate[:, 24:26], gate[:, 27:28], mul))
            step(tt(gate[:, 30:31], gate[:, 28:29], gate[:, 29:30], ALU.is_ge))
            step(ts(gate[:, 31:32], gate[:, 30:31], -1.0, mul, 1.0, add_))
            step(tt(gate[:, 32:34], gate[:, 28:30], gate[:, 30:32], mul))
            for r in range(2):
                last = ts(wdiag[:, r, :], ident[0:NCLS, 0:NCLS], gate[:, 32 + r:33 + r], mul)
            last.then_inc(f_dve[0], 1)
            dve.wait_ge(f_act[0], 3)
            step(dve.memset(hidT[FH:FH + 1, 0, :], 1.0))
            dve.memset(hidT[0:FH + 1, 0, 0:NCLS], 0.0).then_inc(f_dve[0], 1)
            dve.wait_ge(f_act[0], 3 + ATOMS)
            dve.wait_ge(f_mm[0], 2)
            for d, n0, dn, s0, ds_, cnt_, r in [(3, 0, 2, 0, 1, 3, 0), (4, 1, 2, 0, 1, 3, 0)] + \
                    [(l, 2 * l, 1, 3, 1, 2, 1) for l in range(3)]:
                a0, da = s0 * NCLS + n0, ds_ * NCLS + dn
                last = tt(zt[:, d, n0:n0 + dn * (cnt_ - 1) + 1:dn], hat[:, a0:a0 + da * (cnt_ - 1) + 1:da],
                          bank[5][0:FH + 1, r * NCLS + n0:r * NCLS + n0 + dn * (cnt_ - 1) + 1:dn], mul)
            last.then_inc(f_dve[0], 1)
            dve.wait_ge(f_mm[0], 3)
            to_stream(0)
            dve.wait_ge(w_used, used(C_FFN0 + 1))
            done(to_stream(1))

            norm(2, 2, bias=1)
            gat(1)

            def affine_out(s, banks_ready, bias):
                for m in range(M):
                    banks_ready(m)
                    for (b, c0, c1, o) in NODE_BANKS[m]:
                        if bias:
                            last = tt(h_sb[:, m, o:o + c1 - c0], bank[b][:, c0:c1], hbias_bc[:, o:o + c1 - c0], add_)
                        else:
                            last = dve.tensor_copy(h_sb[:, m, o:o + c1 - c0], bank[b][:, c0:c1])
                step(last)
                step(normalised(s, h_sb)[-1])
                for buf, op in ((gamma_bc, mul), (beta_bc, add_)):
                    for m in range(M):
                        last = tt(xn[:, m, :], xn[:, m, :], buf[:, :], op)
                    step(last)
                for m in range(M):
                    last = tt(x_sb[:, m, :], x_sb[:, m, :], xn[:, m, :], add_)
                done(last)

            norm(3, 3)
            dve.wait_ge(ld_mid, LD_MID[1])
            affine_out(4, lambda m: dve.wait_ge(*((f_mm[1], 4) if m == 0 else (w_used, used(C_FFN1 + 2)))), True)

            def gcn_out(s):
                for m in range(M):
                    dve.wait_ge(g_out, 2 * s + m + 1)
                    for (b, c0, c1, o) in NODE_BANKS[m]:
                        xs = x_sb[:, m, o:o + c1 - c0]
                        last = dve.scalar_tensor_tensor(xs, bank[b][:, c0:c1], dinv[:, m:m + 1], xs, mul, add_)
                done(last)

            norm(5, 4, bias=2)
            gcn_out(0)

            def bc(ap):
                return ap.to_broadcast([P, M, 8])

            i8 = iota8[:, :].unsqueeze(1).to_broadcast([P, M, 8])

            def first_max(p, o):
                step(dve.tensor_reduce(lg[:, o, :, 0], lg[:, p, :, :], AX.X, mx))
                step(tt(lg[:, o + 1, :, :], lg[:, p, :, :], bc(lg[:, o, :, 0:1]), ALU.is_equal))
                step(tt(lg[:, o + 1, :, :], lg[:, o + 1, :, :], i8, mul))
                step(dve.tensor_reduce(lg[:, o + 2, :, 0], lg[:, o + 1, :, :], AX.X, ALU.min))
                step(tt(lg[:, o + 3, :, :], i8, bc(lg[:, o + 2, :, 0:1]), ALU.is_equal))

            def route(s):
                dve.wait_ge(f_mm[s], 1)
                step(tt(lg[:, 0, :, :], bank[6][:, 0:M * 8].rearrange("p (m e) -> p m e", m=M),
                        rb[:, :].unsqueeze(1).to_broadcast([P, M, 8]), add_))
                step(dve.tensor_reduce(lg[:, 15, :, 0], lg[:, 0, :, :], AX.X, mx))
                tt(lg[:, 1, :, :], lg[:, 0, :, :], bc(lg[:, 15, :, 0:1]), ALU.subtract).then_inc(f_dve[s], 1)
                dve.wait_ge(f_act[s], 1)
                step(dve.tensor_reduce(lg[:, 15, :, 1], lg[:, 2, :, :], AX.X, add_))
                step(dve.reciprocal(lg[:, 15, :, 2], lg[:, 15, :, 1]))
                step(tt(lg[:, 3, :, :], lg[:, 2, :, :], bc(lg[:, 15, :, 2:3]), mul))

            norm(6, 5)
            route(2)
            first_max(3, 4)
            dve.wait_ge(f_act[2], 3)
            dve.wait_ge(w_used, used(C_FFN2 + 1))
            for m, b in enumerate((5, 7)):
                last = tt(flat(neg_b[:, 2 * m:2 * m + 2, :]), flat(z_b[:, 2 * m:2 * m + 2, :]), bank[b][:, :], mul)
            step(last)
            for m in range(M):
                hm = flat(neg_b[:, 2 * m:2 * m + 2, :]).rearrange("p (e h) -> p e h", e=EXP2)
                last = tt(hm, hm, lg[:, 7, m, :].unsqueeze(2).to_broadcast([P, EXP2, HID2]), mul)
            last.then_inc(f_dve[2], 1)
            dve.wait_ge(f_act[2], 9)
            for m in range(M):
                last = dve.scalar_tensor_tensor(x_sb[:, m, :], outb[:, m, :], lg[:, 4, m, 0:1], x_sb[:, m, :], mul, add_)
            done(last)

            norm(7, 6, bias=3)
            with step.loop(0, REL // 2, 6) as i:
                for half in range(2):
                    r = i * 2 + half
                    dve.wait_ge(ld_ct[half], i * 16 + 16)
                    step(dve.tensor_reduce(small[:, 0:M], ct[:, half, :, :], AX.X, add_))
                    step(ts(small[:, 2:4], small[:, 0:M], 1.0, mx))
                    step(dve.reciprocal(small[:, 4:6], small[:, 2:4]))
                    for m in range(M):
                        last = ts(REL_A[half][:, m, :], ct[:, half, m, :], small[:, 4 + m:5 + m], mul)
                    last.then_inc(r_norm, 1)
            dve.wait_ge(w_used, used(C_REL + REL - 1))
            for m in range(M):
                for (b, c0, c1, o) in SUM_BANKS[m]:
                    last = tt(xn[:, m, o:o + c1 - c0], bank[b][:, c0:c1], hbias_bc[:, o:o + c1 - c0], add_)
                last.then_inc(ln_xn, 1)
            transposed(7)
            gcn_out(1)

            norm(8, 8)
            route(3)
            first_max(3, 4)
            step(dve.scalar_tensor_tensor(lg[:, 8, :, :], lg[:, 7, :, :], -2.0, lg[:, 3, :, :], mul, add_))
            first_max(8, 9)
            step(tt(lg[:, 13, :, 0], lg[:, 4, :, 0], lg[:, 9, :, 0], add_))
            step(dve.reciprocal(lg[:, 13, :, 1], lg[:, 13, :, 0]))
            step(tt(lg[:, 7, :, :], lg[:, 7, :, :], bc(lg[:, 4, :, 0:1]), mul))
            step(tt(lg[:, 12, :, :], lg[:, 12, :, :], bc(lg[:, 9, :, 0:1]), mul))
            step(tt(lg[:, 14, :, :], lg[:, 7, :, :], lg[:, 12, :, :], add_))
            step(tt(lg[:, 14, :, :], lg[:, 14, :, :], bc(lg[:, 13, :, 1:2]), mul))
            dve.wait_ge(ld_mid, LD_MID[3])
            for m in range(M):
                dve.wait_ge(*((f_mm[3], 2) if m == 0 else (w_used, used(C_FFN3))))
                for (b, c0, c1, o) in NODE_BANKS[m]:
                    last = tt(h_sb[:, m, o:o + c1 - c0], bank[b][:, c0:c1], hbias_bc[:, o:o + c1 - c0], add_)
            last.then_inc(f_dve[3], 1)
            dve.wait_ge(f_act[3], 2)
            for m in range(M):
                dve.tensor_copy(ge[:, m, :, HID3], lg[:, 14, m, :])
                last = tt(ge[:, m, :, 0:HID3], h_sb[:, m, :].rearrange("p (e h) -> p e h", e=EXP3),
                          lg[:, 14, m, :].unsqueeze(2).to_broadcast([P, EXP3, HID3]), mul)
            last.then_inc(f_dve[3], 1)
            affine_out(9, lambda m: dve.wait_ge(w_used, used(C_FFN3 + 1 + m)), False)


def kernel(**inputs):
    import concourse.bacc as bacc
    from concourse.bass_utils import run_bass_kernel_spmd

    a = {name: np.asarray(v) for name, v in inputs.items()}
    arrays = {}

    def put(name, v):
        arrays[name] = np.ascontiguousarray(v)

    plain = ["x", "L0_gnn_W1", "L0_gnn_W2", "L0_gnn_a_src1", "L0_gnn_a_dst1", "L0_gnn_a_src2", "L0_gnn_a_dst2",
             "L0_gnn_b2", "L1_gnn_W1", "L1_gnn_W2", "L1_gnn_a_src1", "L1_gnn_a_dst1", "L1_gnn_a_src2", "L1_gnn_a_dst2",
             "L1_gnn_b2", "L0_ffn_gate_pair", "L0_ffn_balance_bias", "L1_ffn_bo", "L1_ffn_gamma", "L1_ffn_beta",
             "L2_gnn_W", "L2_gnn_b", "L2_ffn_router_w", "L2_ffn_router_b", "L3_gnn_W_root", "L3_gnn_b_rgcn",
             "L3_gnn_W_gcn", "L3_gnn_b_gcn", "L3_ffn_Wr", "L3_ffn_br", "L3_ffn_ln_g", "L3_ffn_ln_b"]
    for name in plain:
        put(name, a[name])
    for name in ("src", "dst", "edge_type_34"):
        put(name, a[name].reshape(ET, P).T)
    put("L0_gnn_b1", a["L0_gnn_b1"].reshape(-1, P).T)
    put("L1_gnn_b1", a["L1_gnn_b1"].reshape(-1, P).T)
    put("L1_ffn_b1", a["L1_ffn_b1"].reshape(-1, P).T)
    put("L1_ffn_b2", a["L1_ffn_b2"].reshape(-1, P).T)
    put("ffn0_in", np.concatenate([a["L0_ffn_fc1_w"].T, a["L0_ffn_atom_in_w"].transpose(2, 0, 1).reshape(D, -1)], 1))
    put("ffn0_bias", np.concatenate([a["L0_ffn_fc1_b"][None], a["L0_ffn_atom_in_b"]], 0).T)
    put("ffn0_out", np.concatenate([a["L0_ffn_fc2_w"].T, a["L0_ffn_fc2_b"][None]] +
                                   [v for d in range(ATOMS) for v in (a["L0_ffn_atom_out_w"][d].T, a["L0_ffn_atom_out_b"][d][None])], 0))
    put("L1_ffn_W1", a["L1_ffn_W1"].T)
    put("L1_ffn_W2", a["L1_ffn_W2"].T)
    put("L1_ffn_Wo", a["L1_ffn_Wo"].T)
    put("L2_ffn_w1", a["L2_ffn_w1"].transpose(1, 0, 2).reshape(D, -1))
    put("L2_ffn_w2", a["L2_ffn_w2"].transpose(1, 0, 2).reshape(D, -1))
    put("L2_ffn_w3", a["L2_ffn_w3"].reshape(-1, D))
    put("L3_gnn_W_rel", a["L3_gnn_W_rel"].reshape(-1, D))
    put("L3_ffn_W1", a["L3_ffn_W1"].transpose(1, 0, 2).reshape(D, -1))
    put("L3_ffn_b1", a["L3_ffn_b1"].reshape(-1))
    put("ffn3_out", np.concatenate([a["L3_ffn_W2"], a["L3_ffn_b2"][:, None, :]], 1).reshape(-1, D))

    nc = bacc.Bacc("TRN2", target_bir_lowering=False, num_devices=1)
    t = {}
    for name, v in arrays.items():
        t[name] = nc.dram_tensor(name, v.shape, mybir.dt.from_np(v.dtype), kind="ExternalInput").ap()
    t["out"] = nc.dram_tensor("out", (N, D), FP32, kind="ExternalOutput").ap()
    gnn_ffn_kernel(nc, t)
    r = run_bass_kernel_spmd(nc, [arrays], core_ids=[0])
    return r.results[0]["out"]
```

```python
from contextlib import ExitStack, contextmanager

import numpy as np

import concourse.bass as bass
from concourse import mybir

FP32 = mybir.dt.float32
BF16 = mybir.dt.bfloat16
FP32R = mybir.dt.float32r
INT32 = mybir.dt.int32
UINT32 = mybir.dt.uint32
ALU = mybir.AluOpType
ACT = mybir.ActivationFunctionType
AX = mybir.AxisListType

P = 128
N = 256
M = N // P
D = 768
K = D // P
E = 8192
ET = E // P
G = 8
HEADS = 8
REL = 34
HALF = D // 2
NONE = -1.0e30
LN_EPS = 1e-5
DUMP = REL * N
ROWS = DUMP + 2 * N
NCLS, ATOMS, FH = 6, 5, 96
INNER = 512
EXP2, HID2 = 8, 64
EXP3, HID3 = 8, 96


class Steps:

    def __init__(self, eng, sem):
        self.eng, self.sem, self.base, self.n = eng, sem, 0, 0

    def __call__(self, ins):
        ins.then_inc(self.sem, 1)
        self.n += 1
        self.eng.wait_ge(self.sem, self.base + self.n)

    @contextmanager
    def loop(self, first, last, each):
        before = self.n
        with self.eng.Fori(first, last) as i:
            self.base, self.n = (i - first) * each + before, 0
            yield i
            assert self.n == each, self.n
        self.base, self.n = 0, before + (last - first) * each


def gnn_ffn_kernel(nc, t):
    ctx = ExitStack()
    with ctx:
        def sb(name, shape, dt=FP32):
            return ctx.enter_context(nc.sbuf_tensor(name, shape, dt))

        def sem(name):
            return ctx.enter_context(nc.semaphore(name))

        w_in = sb("w_in", [P, 2, 3, D])
        w_hi = sb("w_hi", [P, 2, K, D], FP32R)
        w_lo = sb("w_lo", [P, 2, K, D], FP32R)
        x_sb = sb("x_sb", [P, M, D])
        xT_hi = sb("xT_hi", [P, K, N], FP32R)
        xT_lo = sb("xT_lo", [P, K, N], FP32R)
        h_hi = sb("h_hi", [P, M, D], FP32R)
        h_lo = sb("h_lo", [P, M, D], FP32R)
        hid_hi = sb("hid_hi", [P, K, N], FP32R)
        hid_lo = sb("hid_lo", [P, K, N], FP32R)
        z_b = sb("z_b", [P, K, N])
        h_sb = z_b[:, :, :].rearrange("p (m a) n -> p m (a n)", m=M)
        neg_b = sb("neg_b", [P, K, N])
        xn = neg_b[:, :, :].rearrange("p (m a) n -> p m (a n)", m=M)
        b1_head = sb("b1_head", [P, K])
        spare = sb("spare", [P, 1552])
        junk = spare[:, 0:D]
        ge = spare[:, :].rearrange("p (m e h) -> p m e h", m=M, e=EXP3)
        a_bc = sb("a_bc", [P, 2, D])
        gamma_bc, beta_bc = a_bc[:, 0, :], a_bc[:, 1, :]
        bias_bc = sb("bias_bc", [P, D])
        hbias_bc = sb("hbias_bc", [P, D])
        b1c = sb("b1c", [P, 2, HEADS * K])
        sbias = sb("sbias", [P, 16])
        ident = sb("ident", [P, P])
        ones = sb("ones", [P, P])
        tril = sb("tril", [P, P])
        zero = sb("zero", [P, 512], BF16)
        zrow = sb("zrow", [P, N])
        iota = sb("iota", [P, N], BF16)
        pcol = sb("pcol", [P, 1])
        iota8 = sb("iota8", [P, 8])
        edge_i = sb("edge_i", [P, 3, ET], INT32)
        edge_f = sb("edge_f", [P, 3, ET])
        key = sb("key", [P, ET])
        dup = sb("dup", [P, ET])
        row_f = sb("row_f", [P, ET])
        row_i = sb("row_i", [P, ET], UINT32)
        add_rows = sb("add_rows", [P, 2, N])
        add_idx = sb("add_idx", [P, 2], UINT32)
        cnt = sb("cnt", [P, 2, M, N])
        mask = sb("mask", [P, M, N])
        cntT_hi = sb("cntT_hi", [P, M, N], FP32R)
        cntT_lo = sb("cntT_lo", [P, M, N], FP32R)
        dinv = sb("dinv", [P, M])
        scal = sb("scal", [P, 4])
        scores_b = sb("scores_b", [P, 2, M, N])
        score, leaky = scores_b[:, 0, :, :], scores_b[:, 1, :, :]
        ct = scores_b
        prob = sb("prob", [P, M, N])
        alpha = sb("alpha", [P, M, N])
        aT_hi = sb("aT_hi", [P, M, N], FP32R)
        aT_lo = sb("aT_lo", [P, M, N], FP32R)
        small = sb("small", [P, 8])
        stats = sb("stats", [P, M, 2, 6])
        mv = sb("mv", [P, M, 2])
        std = sb("std", [P, M])
        rstd = sb("rstd", [P, M])
        gp = h_sb[0:NCLS, :, :]
        bb = sb("bb", [NCLS, 2])
        gate = sb("gate", [NCLS, 40])
        wdiag = sb("wdiag", [NCLS, 2, NCLS])
        hat = sb("hat", [FH + 1, ATOMS * NCLS])
        zt = spare[0:FH + 1, D:D + ATOMS * P]
        rw = sb("rw", [P, K * 8])
        rw_hi = sb("rw_hi", [P, K * 8], FP32R)
        rw_lo = sb("rw_lo", [P, K * 8], FP32R)
        rb = sb("rb", [P, 8])
        lg = sb("lg", [P, 16, M, 8])
        outb = spare[:, 0:D].bitcast(BF16).rearrange("p (m n) -> p m n", m=M)
        deg = sb("deg", [P, M])
        sd = sb("sd", [P, M])
        osrc = spare[:, 0:G * P].bitcast(BF16).rearrange("p (g n) -> p g n", g=G)
        odst = a_bc[:, :, :].rearrange("p a n -> p (a n)")[:, 0:G * P].bitcast(BF16).rearrange("p (g n) -> p g n", g=G)
        kdiag = neg_b[:, :, :].rearrange("p a n -> p (a n)")[:, 0:G * P].rearrange("p (g n) -> p g n", g=G)
        same = prob[:, :, :].rearrange("p a n -> p (a n)").bitcast(BF16).rearrange("p (g n) -> p g n", g=G)
        rows = [z_b[:, 2 * j:2 * j + 2, :] for j in range(3)] + [leaky]
        hrow = prob[0:FH + 1, 0, :]

        bank = [ctx.enter_context(nc.psum_tensor(f"bank{i}", [P, 512], FP32)) for i in range(8)]
        rows_d = nc.dram_tensor("rows", (ET * P, N), FP32, kind="Internal").ap()
        table = nc.dram_tensor("table", (ROWS, N), FP32, kind="Internal").ap()

        w_full = [sem("w_full_0"), sem("w_full_1")]
        w_high = [sem("w_high_0"), sem("w_high_1")]
        w_low = [sem("w_low_0"), sem("w_low_1")]
        w_used = sem("w_used")
        ld_x, ld_edge, ld_const = sem("ld_x"), sem("ld_edge"), sem("ld_const")
        ld_a, ld_bias = sem("ld_a"), sem("ld_bias")
        ld_mid, ld_gate = sem("ld_mid"), sem("ld_gate")
        ld_ct = [sem("ld_ct0"), sem("ld_ct1")]
        zeroed, cleared = sem("zeroed"), sem("cleared")
        dve_step, pool_step, act_step = sem("dve_step"), sem("pool_step"), sem("act_step")
        consts = sem("consts")
        e_hot, e_key, e_same, e_rows, e_kept = sem("e_hot"), sem("e_key"), sem("e_same"), sem("e_rows"), sem("e_kept")
        e_taken, e_dup, e_turn, e_spilt = sem("e_taken"), sem("e_dup"), sem("e_turn"), sem("e_spilt")
        ld_rows = [sem("ld_rows0"), sem("ld_rows1")]
        e_cnt, e_mask, e_idx, e_added = sem("e_cnt"), sem("e_mask"), sem("e_idx"), sem("e_added")
        e_cntT, e_deg, e_std, e_dinv = sem("e_cntT"), sem("e_deg"), sem("e_std"), sem("e_dinv")
        e_cntT_high, e_cntT_low = sem("e_cntT_high"), sem("e_cntT_low")
        seeded = sem("seeded")
        ln_var, ln_std, ln_xn, ln_t, ln_high, ln_low = [sem("ln_" + s) for s in ("var", "std", "xn", "t", "high", "low")]
        h_mm, h_kept, h_high, h_low = sem("h_mm"), sem("h_kept"), sem("h_high"), sem("h_low")
        scored, src_row, masked, exped, normed = [sem(s) for s in ("scored", "src_row", "masked", "exped", "normed")]
        aT_mm, aT_high, aT_low = sem("aT_mm"), sem("aT_high"), sem("aT_low")
        hid_high, hid_low = sem("hid_high"), sem("hid_low")
        att_mm, z_kept, z_neg, z_exp, elu = sem("att_mm"), sem("z_kept"), sem("z_neg"), sem("z_exp"), sem("elu")
        h2_mm, att2_mm, x_new = sem("h2_mm"), sem("att2_mm"), sem("x_new")
        f_mm = [sem(f"ffn{s}_mm") for s in range(4)]
        f_act = [sem(f"ffn{s}_act") for s in range(4)]
        f_dve = [sem(f"ffn{s}_dve") for s in range(4)]
        g_mm, g_kept, g_high, g_low, g_out = [sem("gcn_" + s) for s in ("mm", "kept", "high", "low", "out")]
        rw_high, rw_low = sem("rw_high"), sem("rw_low")
        r_norm, r_t, r_thigh, r_tlow, r_mm, r_high, r_low = [sem("rel_" + s) for s in ("norm", "t", "thigh", "tlow", "mm", "high", "low")]
        x_high, x_low = sem("x_high"), sem("x_low")
        stored = sem("stored")


        C_GAT, C_FFN0, C_FFN1, C_GCN2, C_FFN2, C_ROOT, C_REL, C_GCN3, C_FFN3 = (0, 20), 18, 38, 41, 42, 45, 46, 80, 81

        def nth(c):
            return c - 1 if c < C_GAT[1] else c - 3

        NTH_GAT = (0, 18)
        SHAPES = {C_FFN0: (P, (3, 3), (ATOMS + 1) * FH), C_FFN0 + 1: (FH + 1, (3, 3), D), C_FFN1: (P, (3, 3), INNER),
                  C_FFN1 + 1: (P, (3, 1), D), C_FFN2: (P, (3, 3), INNER), C_FFN2 + 1: (P, (3, 3), INNER),
                  C_FFN2 + 2: (P, (3, 1), D), C_FFN3 + 1: (HID3 + 1, (3, 3), D), C_FFN3 + 2: (HID3 + 1, (1, 1), D)}
        WHOLE = (P, (3, 3), D)

        def used(c):
            return c + 3

        NCONST = 7
        LD_MID = {1: 16 * 3, 2: 16 * 6, 3: 16 * 11}

        def row_tiles(dram, n):
            return dram.rearrange("(k p) n -> p k n", p=n)

        def flat(ap):
            return ap.rearrange("p a b -> p (a b)")

        NODE_BANKS = [[(3, 0, 512, 0), (5, 0, 256, 512)], [(4, 0, 512, 0), (7, 0, 256, 512)]]
        SUM_BANKS = [[(0, 0, 512, 0), (2, 0, 256, 512)], [(1, 0, 512, 0), (2, 256, 512, 512)]]
        HT3 = [[flat(ap[0:HID3 + 1, 2 * j:2 * j + 2, :]) for ap in (hid_hi, hid_lo)] for j in range(3)] + \
              [[ap[0:HID3 + 1, 0, 0:512] for ap in (h_hi, h_lo)]]
        ZT = [flat(ap[0:FH + 1, 2:6, :])[:, 0:ATOMS * P] for ap in (hid_hi, hid_lo)]
        REL_A = [alpha, prob]
        REL_T = [(hid_hi, hid_lo), (xT_hi, xT_lo)]

        block = ctx.enter_context(nc.Block())

        @block.sync
        def _(sp):
            sp.dma_start(x_sb[:, :, :], row_tiles(t["x"], P)).then_inc(ld_x, 16)
            for j, name in enumerate(("src", "dst", "edge_type_34")):
                sp.dma_start(edge_i[:, j, :], t[name]).then_inc(ld_edge, 16)
            def load(n, dram, shape=WHOLE):
                rows_, tiles, cols = shape
                for p in range(2):
                    sp.wait_ge(w_high[p], n)
                    sp.wait_ge(w_low[p], n)
                    sp.dma_start(w_in[0:rows_, p, 0:tiles[p], 0:cols],
                                 row_tiles(dram, rows_)[:, p * tiles[0]:p * tiles[0] + tiles[p], :]).then_inc(w_full[p], 16)

            def load_chunk(c, dram):
                load(nth(c), dram, SHAPES.get(c, WHOLE))

            def gat(layer):
                w1, w2, n0 = t[f"L{layer}_gnn_W1"], t[f"L{layer}_gnn_W2"], NTH_GAT[layer]
                load(n0 + 1, w1[:, 0:D])
                if layer == 0:
                    sp.wait_ge(zeroed, 1)
                    sp.dma_start(table.rearrange("(p t) n -> p t n", p=P),
                                 zrow[:, :].unsqueeze(1).to_broadcast([P, ROWS // P, N])).then_inc(cleared, 16)
                with sp.Fori(0, HEADS - 1) as h:
                    load(h * 2 + (n0 + 2), w1[:, bass.ds((h + 1) * D, D)])
                    load(h * 2 + (n0 + 3), w2[bass.ds(h * D, D), :])
                load(n0 + 2 * HEADS, w2[(HEADS - 1) * D:HEADS * D, :])

            gat(0)
            load_chunk(C_FFN0, t["ffn0_in"])
            load_chunk(C_FFN0 + 1, t["ffn0_out"])
            gat(1)
            load_chunk(C_FFN1, t["L1_ffn_W1"])
            load_chunk(C_FFN1 + 1, t["L1_ffn_W2"])
            load_chunk(C_FFN1 + 2, t["L1_ffn_Wo"])
            load_chunk(C_GCN2, t["L2_gnn_W"])
            load_chunk(C_FFN2, t["L2_ffn_w1"])
            load_chunk(C_FFN2 + 1, t["L2_ffn_w2"])
            load_chunk(C_FFN2 + 2, t["L2_ffn_w3"])
            load_chunk(C_ROOT, t["L3_gnn_W_root"])
            with sp.Fori(0, REL) as r:
                load(r + nth(C_REL), t["L3_gnn_W_rel"][bass.ds(r * D, D), :])
            load_chunk(C_GCN3, t["L3_gnn_W_gcn"])
            load_chunk(C_FFN3, t["L3_ffn_W1"])
            load_chunk(C_FFN3 + 1, t["ffn3_out"][0:K * (HID3 + 1), :])
            load_chunk(C_FFN3 + 2, t["ffn3_out"][K * (HID3 + 1):, :])
            sp.wait_ge(x_new, 8)
            sp.dma_start(row_tiles(t["out"], P), x_sb[:, :, :]).then_inc(stored, 16)
            sp.wait_ge(stored, 16)

        @block.gpsimd
        def _(pool):
            step = Steps(pool, pool_step)
            pool.memset(zrow[:, :], 0.0).then_inc(zeroed, 1)
            pool.memset(ones[:, :], 1.0).then_inc(consts, 1)
            pool.memset(zero[:, :], 0.0).then_inc(consts, 1)
            pool.memset(hat[:, :], 1.0).then_inc(w_used, 2)
            pool.memset(add_rows[:, 1, :], 0.0).then_inc(e_kept, 4)
            for p in range(2):
                pool.memset(small[:, p:p + 1], 0.0).then_inc(w_high[p], 1)
                pool.memset(small[:, 2 + p:3 + p], 0.0).then_inc(w_low[p], 1)
            pool.memset(b1_head[:, :], 0.0).then_inc(e_spilt, 32)
            step(pool.memset(ident[:, :], 0.0))
            step(pool.memset(tril[:, :], 1.0))
            pool.affine_select(out=ident[:, :], in_=ident[:, :], compare_op=ALU.not_equal, fill=1.0, base=0,
                               pattern=[[-1, P]], channel_multiplier=1).then_inc(consts, 1)
            pool.affine_select(out=tril[:, :], in_=tril[:, :], compare_op=ALU.is_gt, fill=0.0, base=0,
                               pattern=[[-1, P]], channel_multiplier=1).then_inc(consts, 1)
            pool.iota(iota[:, :], pattern=[[1, N]], base=0, channel_multiplier=0,
                      allow_small_or_imprecise_dtypes=True).then_inc(consts, 1)
            pool.iota(pcol[:, :], pattern=[[0, 1]], base=DUMP, channel_multiplier=1,
                      allow_small_or_imprecise_dtypes=True).then_inc(consts, 1)
            pool.iota(iota8[:, :], pattern=[[1, 8]], base=-8, channel_multiplier=0,
                      allow_small_or_imprecise_dtypes=True).then_inc(consts, 1)

            def low(n, half, shape=WHOLE):
                rows_, tiles, cols = shape
                pool.wait_ge(w_high[1], n + 1)
                pool.tensor_tensor(w_lo[0:rows_, half, 3:3 + tiles[1], 0:cols], w_in[0:rows_, 1, 0:tiles[1], 0:cols],
                                   w_hi[0:rows_, half, 3:3 + tiles[1], 0:cols].bitcast(FP32), ALU.subtract).then_inc(w_low[1], 1)

            def low_chunk(c):
                low(nth(c), c % 2, SHAPES.get(c, WHOLE))

            def take(i, j):
                pool.dma_start(add_rows[:, j, :], rows_d[bass.ds(i * P, P), :]).then_inc(ld_rows[j], 16)

            def add(i, j, ahead=True):
                pool.tensor_copy(add_idx[:, j:j + 1], row_i[:, bass.ds(i, 1)]).then_inc(e_taken, 1)
                pool.wait_ge(e_added, i * 16 + 16)
                pool.wait_ge(e_taken, i + 1)
                pool.wait_ge(ld_rows[j], (i - j) * 8 + 16)
                pool.sem_inc(e_turn, 1)
                if ahead:
                    take(i + 1, 1 - j)
                pool.indirect_dma_start(
                    out=table, out_offset=bass.IndirectOffsetOnAxis(ap=add_idx[:, j:j + 1], axis=0),
                    in_=add_rows[:, j, :], in_offset=None, compute_op=ALU.add).then_inc(e_added, 16)

            EACH = ET // (2 * HEADS)

            def gat(layer):
                n0, i0 = NTH_GAT[layer], layer * HEADS * EACH
                with pool.Fori(0, HEADS - 1) as h:
                    for j in range(EACH):
                        if j == 0:
                            low(h * 2 + (n0 + 2), 0)
                        if j == EACH // 2:
                            low(h * 2 + (n0 + 3), 1)
                        add(h * EACH + (i0 + j), j % 2)
                low(n0 + 2 * HEADS, 1)
                for j in range(EACH):
                    i = i0 + (HEADS - 1) * EACH + j
                    add(i, j % 2, i + 1 < ET)

            low(1, 0)
            pool.wait_ge(e_idx, 1)
            pool.wait_ge(e_spilt, 32 + ET // G * 32)
            pool.wait_ge(cleared, 16)
            take(0, 0)
            pool.wait_ge(consts, NCONST)
            step(pool.tensor_copy(add_idx[:, 1:2], pcol[:, :]))
            pool.sem_inc(e_turn, 1)
            pool.indirect_dma_start(
                out=table, out_offset=bass.IndirectOffsetOnAxis(ap=add_idx[:, 1:2], axis=0),
                in_=add_rows[:, 1, :], in_offset=None, compute_op=ALU.add).then_inc(e_added, 16)
            gat(0)
            low_chunk(C_FFN0)
            low_chunk(C_FFN0 + 1)
            low(NTH_GAT[1] + 1, 0)
            gat(1)
            for c in range(C_FFN1, C_REL):
                low_chunk(c)
            with pool.Fori(0, REL // 2) as i:
                for half in range(2):
                    low(i * 2 + (nth(C_REL) + half), half)
            for c in range(C_GCN3, C_FFN3 + 3):
                low_chunk(c)

        @block.tensor
        def _(pe):
            def mm(out, lhsT, rhs, start=True, stop=True, **kw):
                return pe.matmul(out, lhsT, rhs, start=start, stop=stop, **kw)

            def mm3(outs, lhsT, start, stop, **kw):
                for a in range(2):
                    for out, rhs in outs:
                        for b in range(2 - a):
                            last = mm(out, lhsT[a], rhs[b], start and a + b == 0, stop and a == 1, **kw)
                return last

            def part(hi, lo, *idx):
                return hi[idx], lo[idx]

            def weights(n):
                for p in range(2):
                    pe.wait_ge(w_low[p], n + 1)

            def chunk(c):
                weights(nth(c))

            def seed(banks):
                for b in banks:
                    last = mm(bank[b][:, :], zero[:, 0:P], zero[:, :], True, False, skip_group_check=True)
                return last

            def transposed(i):
                pe.wait_ge(ln_xn, 2 * i + 2)
                for j in range(3):
                    for k in (2 * j, 2 * j + 1):
                        for m in range(M):
                            last = pe.transpose(bank[3 + j][:, (k % 2) * N + m * P:(k % 2) * N + (m + 1) * P],
                                                xn[:, m, k * P:(k + 1) * P], ident[:, :])
                    last.then_inc(ln_t, 1)
                pe.wait_ge(ln_low, 3 * i + 3)

            def nodes(m, banks, lhs, rhs):
                n = len(lhs)
                for k in range(n):
                    last = mm3([(bank[b][:, c0:c1], rhs(k, o, o + c1 - c0)) for (b, c0, c1, o) in banks[m]],
                               lhs[k], k == 0, k == n - 1)
                return last

            def add(m, lhs, rhs, end=False):
                n = len(lhs)
                for k in range(n):
                    last = mm3([(bank[b][:, c0:c1], rhs(k, o, o + c1 - c0)) for (b, c0, c1, o) in SUM_BANKS[m]],
                               lhs[k], False, end and k == n - 1, skip_group_check=True)
                return last

            def node_tile(hi, lo, m, ks):
                return [(hi[:, k, m * P:(m + 1) * P], lo[:, k, m * P:(m + 1) * P]) for k in range(ks)]

            def of_w(half, rows_=P):
                return lambda k, c0, c1: (w_hi[0:rows_, half, k, c0:c1], w_lo[0:rows_, half, k, c0:c1])

            def of_h(sm, c0, c1):
                return h_hi[:, sm, c0:c1], h_lo[:, sm, c0:c1]

            pe.wait_ge(consts, NCONST)
            seed((0,)).then_inc(e_rows, 1)
            with pe.Fori(0, ET // G) as b:
                pe.wait_ge(e_hot, b + 1)
                for g in range(G):
                    last = mm(bank[1 + g // 4][:, (g % 4) * P:(g % 4 + 1) * P], ones[:, :], kdiag[:, g, :])
                last.then_inc(e_key, 1)
                for g in range(G):
                    for m in range(M):
                        mm(bank[0][:, m * N:(m + 1) * N], odst[:, g, m * P:(m + 1) * P], osrc[:, g, :], False, False,
                           skip_group_check=True)
                pe.wait_ge(e_same, b + 1)
                pe.wait_ge(e_kept, b * 4 + 4)
                for g in range(G):
                    last = mm(bank[3 + g // 2][:, (g % 2) * N:(g % 2 + 1) * N], same[:, g, :], osrc[:, g, :])
                last.then_inc(e_rows, 1)
            mm(bank[0][:, :], zero[:, 0:P], zero[:, :], False, True, skip_group_check=True).then_inc(e_cnt, 1)
            pe.wait_ge(e_mask, 1)
            for sm in range(M):
                for m in range(M):
                    last = pe.transpose(bank[1][:, sm * N + m * P:sm * N + (m + 1) * P], cnt[:, 0, m, sm * P:(sm + 1) * P], ident[:, :])
            last.then_inc(e_cntT, 1)
            pe.wait_ge(e_cntT_low, 1)

            def spread(u):
                pe.wait_ge(scored, u + 1)
                for m in range(M):
                    last = mm(bank[7][:, m * P:(m + 1) * P], scal[:, m:m + 1].to_broadcast([P, P]), ident[:, :])
                last.then_inc(src_row, 1)

            def turn(u):
                pe.wait_ge(normed, u + 1)
                for sm in range(M):
                    for m in range(M):
                        last = pe.transpose(bank[7][:, sm * N + m * P:sm * N + (m + 1) * P], alpha[:, m, sm * P:(sm + 1) * P], ident[:, :])
                last.then_inc(aT_mm, 1)

            def parts_kept(u):
                pe.wait_ge(aT_low, u + 1)
                pe.wait_ge(h_low, u + 1)

            def gat(layer):
                c0, n0 = C_GAT[layer], NTH_GAT[layer]
                seed((0, 1, 2))

                def up(h, n, first=False):
                    weights(n)
                    for m, banks in ((0, (5, 6)), (1, (3, 4))):
                        if not first:
                            pe.wait_ge(z_kept, (h + HEADS * layer) * 3 + (-2 if m == 0 else 0))
                        for k in range(K):
                            last = mm3([(bank[banks[j]][:, 0:HALF], part(w_hi, w_lo, slice(0, P), 0, k, slice(j * HALF, (j + 1) * HALF)))
                                        for j in range(2)],
                                       part(xT_hi, xT_lo, slice(0, P), k, slice(m * P, (m + 1) * P)), k == 0, k == K - 1)
                        last.then_inc(*((h_mm, 1) if m == 0 else (w_used, 2 if first else 1)))

                def down(h, n, i0, i1, last_head=False):
                    for i in range(i0, i1):
                        m, k = i // K, i % K
                        if m == 0 and k % 2 == 0:
                            pe.wait_ge(hid_low, (h + HEADS * layer) * 3 + (k // 2 + 1))
                        if m == 0 and k % 3 == 0:
                            pe.wait_ge(w_low[k // 3], n + 1)
                        last = mm3([(bank[b][:, c0_:c1], of_w(1)(k, o, o + c1 - c0_)) for (b, c0_, c1, o) in SUM_BANKS[m]],
                                   part(hid_hi, hid_lo, slice(0, P), k, slice(m * P, (m + 1) * P)), False,
                                   last_head and k == K - 1, skip_group_check=True)
                    if i1 == M * K:
                        last.then_inc(w_used, 2 if last_head else 1)

                def attend(h):
                    for j, b in enumerate((5, 3, 4)):
                        for k in (2 * j, 2 * j + 1):
                            for sm in range(M):
                                last = mm3([(bank[b][:, (k % 2) * N:(k % 2 + 1) * N], part(aT_hi, aT_lo, slice(0, P), sm))],
                                           of_h(sm, k * P, (k + 1) * P), sm == 0, sm == M - 1)
                        last.then_inc(att_mm, 1)

                up(0, n0 + 1, True)
                spread(9 * layer)
                turn(9 * layer)
                parts_kept(9 * layer)
                attend(0)
                with pe.Fori(1, HEADS) as h:
                    up(h, h * 2 + n0)
                    down(h - 1, h * 2 + (n0 + 1), 0, 3)
                    spread(h + 9 * layer)
                    down(h - 1, h * 2 + (n0 + 1), 3, 11)
                    turn(h + 9 * layer)
                    down(h - 1, h * 2 + (n0 + 1), 11, M * K)
                    parts_kept(h + 9 * layer)
                    attend(h)
                down(HEADS - 1, n0 + 2 * HEADS, 0, M * K, True)
                spread(HEADS + 9 * layer)
                turn(HEADS + 9 * layer)
                parts_kept(HEADS + 9 * layer)
                for m in range(M):
                    nodes(m, NODE_BANKS, [part(aT_hi, aT_lo, slice(0, P), sm, slice(m * P, (m + 1) * P)) for sm in range(M)],
                          of_h).then_inc(att2_mm, 1)

            transposed(0)
            gat(0)

            transposed(1)
            chunk(C_FFN0)
            for k in range(K):
                last = mm3([(bank[3][0:FH, 0:N], part(xT_hi, xT_lo, slice(0, P), k))], of_w(0)(k, 0, FH), k == 0, k == K - 1)
            last.then_inc(f_mm[0], 1)
            for a in range(ATOMS):
                for k in range(K):
                    last = mm3([(bank[4][0:FH, a * NCLS:(a + 1) * NCLS], part(xT_hi, xT_lo, slice(0, P), k, slice(0, NCLS)))],
                               of_w(0)(k, (a + 1) * FH, (a + 2) * FH), k == 0, k == K - 1)
            last.then_inc(w_used, 1)
            pe.wait_ge(f_dve[0], 3)
            mm(bank[5][0:FH + 1, 0:2 * NCLS], ones[0:NCLS, 0:FH + 1], flat(wdiag[:, :, :])).then_inc(f_mm[0], 1)
            pe.wait_ge(f_dve[0], 7)
            chunk(C_FFN0 + 1)
            hid0 = [part(hid_hi, hid_lo, slice(0, FH + 1), 0, slice(m * P, (m + 1) * P)) for m in range(M)]
            nodes(0, NODE_BANKS, [hid0[0]] + [(ZT[0][:, d * P:(d + 1) * P], ZT[1][:, d * P:(d + 1) * P]) for d in range(ATOMS)],
                  of_w(1, FH + 1)).then_inc(f_mm[0], 1)
            nodes(1, NODE_BANKS, [hid0[1]], of_w(1, FH + 1)).then_inc(w_used, 1)

            transposed(2)
            gat(1)

            transposed(3)

            def columns(count, half, hi, lo, ks, first_bank, marks):
                for c in range(count):
                    for k in range(ks):
                        last = mm3([(bank[first_bank + c // 2][:, (c % 2) * N:(c % 2 + 1) * N], part(hi, lo, slice(0, P), k))],
                                   of_w(half)(k, c * P, (c + 1) * P), k == 0, k == ks - 1)
                    if c % 2:
                        last.then_inc(marks[c // 2], 1)

            chunk(C_FFN1)
            columns(INNER // P, 0, xT_hi, xT_lo, K, 3, (f_mm[1], w_used))
            pe.wait_ge(f_dve[1], 2)
            chunk(C_FFN1 + 1)
            columns(K, 1, hid_hi, hid_lo, INNER // P, 5, (f_mm[1], f_mm[1], w_used))
            pe.wait_ge(f_dve[1], 5)
            chunk(C_FFN1 + 2)
            nodes(0, NODE_BANKS, node_tile(xT_hi, xT_lo, 0, K), of_w(0)).then_inc(f_mm[1], 1)
            nodes(1, NODE_BANKS, node_tile(xT_hi, xT_lo, 1, K), of_w(0)).then_inc(w_used, 1)

            def gcn(s, half, c):
                chunk(c)
                nodes(0, NODE_BANKS, node_tile(xT_hi, xT_lo, 0, K), of_w(half)).then_inc(g_mm, 1)
                nodes(1, NODE_BANKS, node_tile(xT_hi, xT_lo, 1, K), of_w(half)).then_inc(w_used, 1)
                pe.wait_ge(g_low, 2 * s + 2)
                for m in range(M):
                    nodes(m, NODE_BANKS, [part(cntT_hi, cntT_lo, slice(0, P), sm, slice(m * P, (m + 1) * P)) for sm in range(M)],
                          of_h).then_inc(g_out, 1)

            def router(s):
                pe.wait_ge(rw_low, s - 1)
                for m in range(M):
                    for k in range(K):
                        last = mm3([(bank[6][:, m * 8:(m + 1) * 8], part(rw_hi, rw_lo, slice(0, P), slice(k * 8, (k + 1) * 8)))],
                                   part(xT_hi, xT_lo, slice(0, P), k, slice(m * P, (m + 1) * P)), k == 0, k == K - 1)
                last.then_inc(f_mm[s], 1)

            transposed(4)
            gcn(0, 1, C_GCN2)

            transposed(5)
            router(2)
            for half, banks in ((0, (3, 4)), (1, (5, 7))):
                chunk(C_FFN2 + half)
                for m, b in enumerate(banks):
                    for k in range(K):
                        last = mm3([(bank[b][:, :], of_w(half)(k, 0, INNER))], part(xT_hi, xT_lo, slice(0, P), k, slice(m * P, (m + 1) * P)),
                                   k == 0, k == K - 1)
                last.then_inc(w_used, 1)
            pe.wait_ge(f_dve[2], 2)
            for j in range(2):
                for k in (2 * j, 2 * j + 1):
                    for m in range(M):
                        last = pe.transpose(bank[3 + j][:, (k % 2) * N + m * P:(k % 2) * N + (m + 1) * P],
                                            flat(neg_b[:, 2 * m:2 * m + 2, :])[:, k * P:(k + 1) * P], ident[:, :])
                last.then_inc(f_mm[2], 1)
            pe.wait_ge(f_dve[2], 4)
            chunk(C_FFN2 + 2)
            nodes(0, NODE_BANKS, node_tile(hid_hi, hid_lo, 0, INNER // P), of_w(0)).then_inc(f_mm[2], 1)
            nodes(1, NODE_BANKS, node_tile(hid_hi, hid_lo, 1, INNER // P), of_w(0)).then_inc(w_used, 1)

            transposed(6)
            seed((0, 1, 2))
            chunk(C_ROOT)
            add(0, node_tile(xT_hi, xT_lo, 0, K), of_w(1))
            add(1, node_tile(xT_hi, xT_lo, 1, K), of_w(1)).then_inc(w_used, 1)

            def turn_rel(r, half):
                pe.wait_ge(r_norm, r + 1)
                for sm in range(M):
                    for m in range(M):
                        last = pe.transpose(bank[7][:, sm * N + m * P:sm * N + (m + 1) * P], REL_A[half][:, m, sm * P:(sm + 1) * P], ident[:, :])
                last.then_inc(r_t, 1)

            def mean(r):
                pe.wait_ge(r_tlow, r + 1)
                for j in range(3):
                    for k in (2 * j, 2 * j + 1):
                        for sm in range(M):
                            last = mm3([(bank[3 + j][:, (k % 2) * N:(k % 2 + 1) * N], part(aT_hi, aT_lo, slice(0, P), sm))],
                                       of_h(sm, k * P, (k + 1) * P), sm == 0, sm == M - 1)
                    last.then_inc(r_mm, 1)

            def relation(r, half, ahead=True, end=False):
                if ahead:
                    turn_rel(r + 1, 1 - half)
                pe.wait_ge(r_low, r * 3 + 3)
                weights(r + nth(C_REL))
                add(0, node_tile(*REL_T[half], 0, K), of_w(half), end)
                if ahead:
                    mean(r + 1)
                add(1, node_tile(*REL_T[half], 1, K), of_w(half), end).then_inc(w_used, 1)

            turn_rel(0, 0)
            pe.wait_ge(x_low, 1)
            mean(0)
            with pe.Fori(0, REL // 2 - 1) as i:
                relation(i * 2, 0)
                relation(i * 2 + 1, 1)
            relation(REL - 2, 0)
            relation(REL - 1, 1, False, True)
            transposed(7)
            gcn(1, 0, C_GCN3)

            transposed(8)
            router(3)
            chunk(C_FFN3)
            nodes(0, NODE_BANKS, node_tile(xT_hi, xT_lo, 0, K), of_w(1)).then_inc(f_mm[3], 1)
            nodes(1, NODE_BANKS, node_tile(xT_hi, xT_lo, 1, K), of_w(1)).then_inc(w_used, 1)
            pe.wait_ge(f_dve[3], 3)
            for j in range(4):
                for e in (2 * j, 2 * j + 1):
                    for m in range(M):
                        last = pe.transpose(bank[3 + j][0:HID3 + 1, (e % 2) * N + m * P:(e % 2) * N + (m + 1) * P],
                                            ge[:, m, e, :], ident[:, :])
                last.then_inc(f_mm[3], 1)
            pe.wait_ge(f_dve[3], 7)
            chunk(C_FFN3 + 1)
            chunk(C_FFN3 + 2)
            for m in range(M):
                last = nodes(m, NODE_BANKS, [[ap[:, (e % 2) * N + m * P:(e % 2) * N + (m + 1) * P] for ap in HT3[e // 2]] for e in range(EXP3)],
                             lambda e, a, b: of_w(e // K, HID3 + 1)(e if e < K else (e - K) * 3, a, b))
                last.then_inc(w_used, 1)

        @block.scalar
        def _(act):
            act.dma_start(b1c[:, 0, :], t["L0_gnn_b1"]).then_inc(ld_const, 16)
            act.dma_start(b1c[:, 1, :], t["L1_gnn_b1"]).then_inc(ld_const, 16)
            act.dma_start(bb[:, :], t["L0_ffn_balance_bias"]).then_inc(ld_const, 16)
            act.dma_start(sbias[0:FH, 0:ATOMS + 1], t["ffn0_bias"]).then_inc(ld_const, 16)
            act.dma_start(sbias[:, 6:10], t["L1_ffn_b1"]).then_inc(ld_const, 16)
            act.dma_start(sbias[:, 10:16], t["L1_ffn_b2"]).then_inc(ld_const, 16)

            def row_bc(out, dram, mark):
                act.dma_start(out, dram.partition_broadcast(P)).then_inc(mark, 16)

            def load_heads(layer, h):
                for j, a in enumerate(("a_src1", "a_dst1")):
                    row_bc(a_bc[:, j, :], t[f"L{layer}_gnn_{a}"][bass.ds(h, 1), :].rearrange("a n -> (a n)"), ld_a)

            def load_last(layer):
                for j, a in enumerate(("a_src2", "a_dst2")):
                    row_bc(a_bc[:, j, :], t[f"L{layer}_gnn_{a}"][0, :], ld_a)

            def keep(out, ps, mark, func=ACT.Copy, **kw):
                act.activation(out, ps, func, **kw).then_inc(mark, 1)

            def high(n, free, half, shape=WHOLE):
                rows_, tiles, cols = shape
                act.wait_ge(w_used, free)
                for p in range(2):
                    act.wait_ge(w_full[p], n * 16)
                    keep(w_hi[0:rows_, half, 3 * p:3 * p + tiles[p], 0:cols], w_in[0:rows_, p, 0:tiles[p], 0:cols], w_high[p])

            def high_chunk(c):
                high(nth(c), used(c - 2), c % 2, SHAPES.get(c, WHOLE))

            row_bc(bias_bc[:, :], t["L0_gnn_b2"], ld_bias)
            act.wait_ge(ld_const, 16 * 6)
            high(1, 1, 0)

            with act.Fori(0, ET // G) as b:
                act.wait_ge(e_rows, b + 2)
                act.wait_ge(e_spilt, b * 32 + 32)
                for j in range(G // 2):
                    keep(rows[j], bank[3 + j][:, :].rearrange("p (g n) -> p g n", g=2), e_kept)
                act.wait_ge(e_kept, b * 4 + 8)
                for first, n, buf in ((0, 6, z_b[:, :, :]), (6, 2, leaky)):
                    act.dma_start(rows_d[bass.ds((b * G + first) * P, n * P), :].rearrange("(g p) n -> p g n", p=P), buf)\
                       .then_inc(e_spilt, 16)
            load_heads(0, 0)
            act.wait_ge(e_spilt, 32 + ET // G * 32)
            act.wait_ge(e_deg, 1)
            keep(sd[:, :], deg[:, :], e_std, ACT.Sqrt)
            act.wait_ge(e_cntT, 1)
            keep(flat(cntT_hi[:, :, :]), bank[1][:, :], e_cntT_high)

            def deviation(s):
                act.wait_ge(ln_var, s + 1)
                keep(std[:, :], mv[:, :, 1], ln_std, ACT.Sqrt, bias=LN_EPS)

            def transposed(i):
                for j in range(3):
                    act.wait_ge(ln_t, 3 * i + j + 1)
                    keep(flat(xT_hi[:, 2 * j:2 * j + 2, :]), bank[3 + j][:, :], ln_high)

            def attend(u, ahead):
                act.wait_ge(masked, u + 1)
                for m in range(M):
                    keep(prob[:, m, :], score[:, m, :], exped, ACT.Exp, bias=small[:, m:m + 1])
                ahead()
                act.wait_ge(aT_mm, u + 1)
                keep(flat(aT_hi[:, :, :]), bank[7][:, :], aT_high)

            def gat(layer, after):
                c0, n0 = C_GAT[layer], NTH_GAT[layer]

                def head(h, ahead, last_head=False):
                    u = h + 9 * layer
                    for m, banks in ((0, (5, 6)), (1, (3, 4))):
                        if m == 0:
                            act.wait_ge(h_mm, h + (HEADS * layer + 1))
                        else:
                            act.wait_ge(w_used, h * 2 + used(c0))
                        for out, mark in ((h_sb, h_kept), (h_hi, h_high)):
                            for j in range(2):
                                keep(out[:, m, j * HALF:(j + 1) * HALF], bank[banks[j]][:, 0:HALF], mark)
                    if not last_head:
                        high(h * 2 + (n0 + 2), h * 2 + (c0 + 3), 0)
                    attend(u, ahead)
                    n2 = n0 + 2 * HEADS if last_head else h * 2 + (n0 + 3)
                    if last_head:
                        high(n2, h * 2 + (c0 + 4), 1)
                    a = (h + HEADS * layer) * 3
                    for j, b in enumerate((5, 3, 4)):
                        act.wait_ge(att_mm, a + (j + 1))
                        for k in (2 * j, 2 * j + 1):
                            last = act.activation(z_b[:, k, :], bank[b][:, (k % 2) * N:(k % 2 + 1) * N], ACT.Identity,
                                                  bias=b1_head[:, k:k + 1])
                        last.then_inc(z_kept, 1)
                    for j in range(3):
                        act.wait_ge(z_neg, a + (j + 1))
                        keep(neg_b[:, 2 * j:2 * j + 2, :], neg_b[:, 2 * j:2 * j + 2, :], z_exp, ACT.Exp)
                    if not last_head:
                        high(n2, h * 2 + (c0 + 4), 1)
                    for j in range(3):
                        act.wait_ge(elu, a + (j + 1))
                        keep(hid_hi[:, 2 * j:2 * j + 2, :], neg_b[:, 2 * j:2 * j + 2, :], hid_high)

                with act.Fori(0, HEADS - 1) as h:
                    head(h, lambda: load_heads(layer, h + 1))
                head(HEADS - 1, lambda: load_last(layer), True)
                act.wait_ge(w_used, used(c0 + 17))
                for m in range(M):
                    for out, mark in ((h_sb, h_kept), (h_hi, h_high)):
                        for (b, c0_, c1, o) in SUM_BANKS[m]:
                            keep(out[:, m, o:o + c1 - c0_], bank[b][:, c0_:c1], mark)
                high_chunk(c0 + 18)
                attend(HEADS + 9 * layer, after)
                high_chunk(c0 + 19)

            deviation(0)
            transposed(0)
            gat(0, lambda: load_heads(1, 0))
            act.dma_start(gp[:, :, :], t["L0_ffn_gate_pair"]).then_inc(ld_gate, 16)

            deviation(1)
            transposed(1)
            row_bc(bias_bc[:, :], t["L1_gnn_b2"], ld_bias)
            act.wait_ge(f_dve[0], 1)
            keep(gate[:, 8:11], gate[:, 0:3], f_act[0], ACT.Sqrt)
            act.wait_ge(f_dve[0], 2)
            keep(gate[:, 24:26], gate[:, 22:24], f_act[0], ACT.Exp)
            act.wait_ge(f_mm[0], 1)
            keep(hrow[0:FH, :], bank[3][0:FH, 0:N], f_act[0], ACT.Gelu, bias=sbias[0:FH, 0:1])
            act.wait_ge(w_used, used(C_FFN0))
            for a in range(ATOMS):
                keep(hat[0:FH, a * NCLS:(a + 1) * NCLS], bank[4][0:FH, a * NCLS:(a + 1) * NCLS], f_act[0], ACT.Gelu,
                     bias=sbias[0:FH, a + 1:a + 2])
            act.wait_ge(f_dve[0], 4)
            keep(hid_hi[0:FH + 1, 0, :], hrow, f_act[0])
            act.wait_ge(f_dve[0], 6)
            keep(ZT[0], zt, f_act[0])
            high(NTH_GAT[1] + 1, used(C_GAT[1] - 2), 0)

            deviation(2)
            transposed(2)
            gat(1, lambda: None)

            deviation(3)
            transposed(3)
            row_bc(hbias_bc[:, :], t["L1_ffn_bo"], ld_mid)
            row_bc(gamma_bc[:, :], t["L1_ffn_gamma"], ld_mid)
            row_bc(beta_bc[:, :], t["L1_ffn_beta"], ld_mid)
            row_bc(bias_bc[:, :], t["L2_gnn_b"], ld_bias)
            for c in range(INNER // P):
                act.wait_ge(*((f_mm[1], 1) if c < 2 else (w_used, used(C_FFN1))))
                for out in (z_b, hid_hi):
                    keep(out[:, c, :], bank[3 + c // 2][:, (c % 2) * N:(c % 2 + 1) * N], f_act[1], ACT.Relu,
                         bias=sbias[:, 6 + c:7 + c])
            high_chunk(C_FFN1 + 2)
            for c in range(K):
                act.wait_ge(*((f_mm[1], 2 + c // 2) if c < 4 else (w_used, used(C_FFN1 + 1))))
                for out in (neg_b, xT_hi):
                    keep(out[:, c, :], bank[5 + c // 2][:, (c % 2) * N:(c % 2 + 1) * N], f_act[1], ACT.Identity,
                         bias=sbias[:, 10 + c:11 + c])
            high_chunk(C_GCN2)
            deviation(4)
            high_chunk(C_FFN2)

            def gcn(s, c):
                act.wait_ge(e_dinv, 1)
                for m in range(M):
                    act.wait_ge(*((g_mm, s + 1) if m == 0 else (w_used, used(c))))
                    for out, mark in ((h_sb, g_kept), (h_hi, g_high)):
                        for (b, c0, c1, o) in NODE_BANKS[m]:
                            keep(out[:, m, o:o + c1 - c0], bank[b][:, c0:c1], mark, scale=dinv[:, m:m + 1])

            deviation(5)
            transposed(4)
            act.dma_start(rw[:, :].rearrange("p (k e) -> p k e", k=K), row_tiles(t["L2_ffn_router_w"], P)).then_inc(ld_mid, 16)
            row_bc(rb[:, :], t["L2_ffn_router_b"], ld_mid)
            row_bc(hbias_bc[:, :], t["L3_gnn_b_rgcn"], ld_mid)
            gcn(0, C_GCN2)
            act.wait_ge(ld_mid, LD_MID[2])
            keep(rw_hi[:, :], rw[:, :], rw_high)
            high_chunk(C_FFN2 + 1)

            deviation(6)
            transposed(5)
            row_bc(bias_bc[:, :], t["L3_gnn_b_gcn"], ld_bias)
            act.wait_ge(f_dve[2], 1)
            keep(lg[:, 2, :, :], lg[:, 1, :, :], f_act[2], ACT.Exp)
            act.wait_ge(w_used, used(C_FFN2))
            for m in range(M):
                keep(flat(z_b[:, 2 * m:2 * m + 2, :]), bank[3 + m][:, :], f_act[2], ACT.Silu)
            high_chunk(C_FFN2 + 2)
            for j in range(2):
                act.wait_ge(f_mm[2], 2 + j)
                keep(flat(hid_hi[:, 2 * j:2 * j + 2, :]), bank[3 + j][:, :], f_act[2])
            high_chunk(C_ROOT)
            for m in range(M):
                act.wait_ge(*((f_mm[2], 4) if m == 0 else (w_used, used(C_FFN2 + 2))))
                for (b, c0, c1, o) in NODE_BANKS[m]:
                    keep(outb[:, m, o:o + c1 - c0], bank[b][:, c0:c1], f_act[2])

            deviation(7)
            transposed(6)
            keep(h_hi[:, :, :], xn[:, :, :], x_high)
            act.wait_ge(e_added, 16 * ET + 16)

            def load_counts(r, half):
                act.dma_start(ct[:, half, :, :], table[bass.ds(r * N, N), :].rearrange("(m p) n -> p m n", p=P))\
                   .then_inc(ld_ct[half], 16)

            load_counts(0, 0)
            load_counts(1, 1)
            with act.Fori(0, REL // 2) as i:
                for half in range(2):
                    act.wait_ge(r_t, i * 2 + (half + 1))
                    keep(flat(aT_hi[:, :, :]), bank[7][:, :], r_thigh)
                    load_counts(i * 2 + (half + 2), half)
                    high(i * 2 + (nth(C_REL) + half), i * 2 + (used(C_REL - 2) + half), half)
                    for j in range(3):
                        act.wait_ge(r_mm, i * 6 + (3 * half + j + 1))
                        keep(flat(REL_T[half][0][:, 2 * j:2 * j + 2, :]), bank[3 + j][:, :], r_high)
            high_chunk(C_GCN3)
            transposed(7)
            act.dma_start(rw[:, :].rearrange("p (k e) -> p k e", k=K), row_tiles(t["L3_ffn_Wr"], P)).then_inc(ld_mid, 16)
            row_bc(rb[:, :], t["L3_ffn_br"], ld_mid)
            row_bc(hbias_bc[:, :], t["L3_ffn_b1"], ld_mid)
            row_bc(gamma_bc[:, :], t["L3_ffn_ln_g"], ld_mid)
            row_bc(beta_bc[:, :], t["L3_ffn_ln_b"], ld_mid)
            high_chunk(C_FFN3)
            gcn(1, C_GCN3)
            act.wait_ge(ld_mid, LD_MID[3])
            keep(rw_hi[:, :], rw[:, :], rw_high)
            high_chunk(C_FFN3 + 1)

            deviation(8)
            transposed(8)
            act.wait_ge(f_dve[3], 1)
            keep(lg[:, 2, :, :], lg[:, 1, :, :], f_act[3], ACT.Exp)
            act.wait_ge(f_dve[3], 2)
            keep(h_sb[:, :, :], h_sb[:, :, :], f_act[3], ACT.Gelu_apprx_tanh)
            high_chunk(C_FFN3 + 2)
            for j in range(4):
                act.wait_ge(f_mm[3], 3 + j)
                keep(HT3[j][0], bank[3 + j][0:HID3 + 1, :], f_act[3])
            deviation(9)

        @block.vector
        def _(dve):
            step = Steps(dve, dve_step)
            add_, mul, mx = ALU.add, ALU.mult, ALU.max

            def tt(out, a, b, op):
                return dve.tensor_tensor(out, a, b, op)

            def ts(out, a, s1, op0, s2=None, op1=None):
                return dve.tensor_scalar(out, a, s1, s2, op0, op1) if op1 is not None else dve.tensor_scalar(out, a, s1, None, op0)

            def dot(out, a, b, acc, op0=mul, op1=add_):
                return dve.tensor_tensor_reduce(out=out, in0=a, in1=b, scale=1.0, scalar=0.0, op0=op0, op1=op1, accum_out=acc)

            def low_of(out, whole, high_, mark):
                tt(out, whole, high_.bitcast(FP32), ALU.subtract).then_inc(mark, 1)

            def low(n, half, shape=WHOLE):
                rows_, tiles, cols = shape
                dve.wait_ge(w_high[0], n + 1)
                low_of(w_lo[0:rows_, half, 0:tiles[0], 0:cols], w_in[0:rows_, 0, 0:tiles[0], 0:cols],
                       w_hi[0:rows_, half, 0:tiles[0], 0:cols], w_low[0])

            def low_chunk(c):
                low(nth(c), c % 2, SHAPES.get(c, WHOLE))

            def stats_of(buf):
                for m in range(M):
                    for j in range(2):
                        last = dve.bn_stats(stats[:, m, j, :], buf[:, m, j * HALF:(j + 1) * HALF])
                step(last)
                for m in range(M):
                    last = dve.bn_aggr(mv[:, m, :], flat(stats[:, m, :, :]))
                last.then_inc(ln_var, 1)

            def normalised(s, buf):
                stats_of(buf)
                dve.wait_ge(ln_std, s + 1)
                step(dve.reciprocal(rstd[:, :], std[:, :]))
                return [ts(xn[:, m, :], buf[:, m, :], mv[:, m, 0:1], ALU.subtract, rstd[:, m:m + 1], mul) for m in range(M)]

            def transposed(i):
                for j in range(3):
                    dve.wait_ge(ln_high, 3 * i + j + 1)
                    low_of(flat(xT_lo[:, 2 * j:2 * j + 2, :]), bank[3 + j][:, :], flat(xT_hi[:, 2 * j:2 * j + 2, :]), ln_low)

            def norm(s, i, bias=None):
                for ins in normalised(s, x_sb):
                    ins.then_inc(ln_xn, 1)
                dve.wait_ge(ln_xn, 2 * i + 2)
                transposed(i)
                if bias is not None:
                    dve.wait_ge(ld_bias, 16 * (bias + 1))
                    for m in range(M):
                        last = tt(x_sb[:, m, :], x_sb[:, m, :], bias_bc[:, :], add_)
                    step(last)

            low(1, 0)
            dve.wait_ge(ld_edge, 48)
            dve.wait_ge(consts, NCONST)
            step(dve.tensor_copy(edge_f[:, :, :], edge_i[:, :, :]))
            step(dve.scalar_tensor_tensor(key[:, :], edge_f[:, 2, :], float(N), edge_f[:, 1, :], mul, add_))
            with dve.Fori(0, ET // G) as b:
                dve.wait_ge(e_rows, b + 1)
                for g in range(G):
                    dve.tensor_scalar(osrc[:, g, :], iota[:, :], edge_f[:, 0, bass.ds(b * G + g, 1)], None, ALU.is_equal)
                    dve.tensor_scalar(odst[:, g, :], iota[:, :], edge_f[:, 1, bass.ds(b * G + g, 1)], None, ALU.is_equal)
                    last = dve.tensor_scalar(kdiag[:, g, :], ident[:, :], key[:, bass.ds(b * G + g, 1)], None, mul)
                last.then_inc(e_hot, 1)
                dve.wait_ge(e_key, b + 1)
                for g in range(G):
                    last = dve.tensor_scalar(same[:, g, :], bank[1 + g // 4][:, (g % 4) * P:(g % 4 + 1) * P],
                                             key[:, bass.ds(b * G + g, 1)], None, ALU.is_equal)
                last.then_inc(e_same, 1)
                dve.wait_ge(e_same, b + 1)
                tt(kdiag, same, tril[:, :].unsqueeze(1).to_broadcast([P, G, P]), mul).then_inc(e_dup, 1)
                dve.wait_ge(e_dup, b * 2 + 1)
                dve.tensor_reduce(dup[:, bass.ds(b * G, G)], kdiag, AX.X, add_).then_inc(e_dup, 1)
                dve.wait_ge(e_dup, b * 2 + 2)
            step(ts(dup[:, :], dup[:, :], 1.0, ALU.min))
            step(ts(row_f[:, :], key[:, :], -1.0, mul, pcol[:, 0:1], add_))
            step(tt(row_f[:, :], row_f[:, :], dup[:, :], mul))
            step(tt(row_f[:, :], row_f[:, :], key[:, :], add_))
            dve.tensor_copy(row_i[:, :], row_f[:, :]).then_inc(e_idx, 1)
            dve.wait_ge(e_cnt, 1)
            for j in range(2):
                last = dve.tensor_copy(flat(cnt[:, j, :, :]), bank[0][:, :])
            step(last)
            for m in range(M):
                last = tt(cnt[:, 0, m, m * P:(m + 1) * P], cnt[:, 0, m, m * P:(m + 1) * P], ident[:, :], add_)
            last.then_inc(e_mask, 1)
            dve.wait_ge(e_mask, 1)
            dve.tensor_reduce(deg[:, :], cnt[:, 0, :, :], AX.X, add_).then_inc(e_deg, 1)
            dve.wait_ge(e_std, 1)
            dve.reciprocal(dinv[:, :], sd[:, :]).then_inc(e_dinv, 1)
            dve.wait_ge(e_dinv, 1)
            dve.wait_ge(e_cntT_high, 1)
            low_of(flat(cntT_lo[:, :, :]), bank[1][:, :], flat(cntT_hi[:, :, :]), e_cntT_low)

            def scores(u, layer, ahead):
                dve.wait_ge(ld_a, u * 32 + 32)
                for j, m in ((0, 0), (1, 0), (0, 1), (1, 1)):
                    dve.wait_ge(h_kept, u * 4 + (2 * m + 2))
                    last = dot(junk[:, :], h_sb[:, m, :], a_bc[:, j, :], scal[:, 2 * j + m:2 * j + m + 1])
                    if (j, m) == (0, 1):
                        last.then_inc(scored, 1)
                        dve.wait_ge(scored, u + 1)
                    else:
                        step(last)
                dve.wait_ge(h_high, u * 4 + 4)
                low_of(h_lo[:, :, :], h_sb[:, :, :], h_hi[:, :, :], h_low)
                dve.wait_ge(src_row, u + 1)
                for m in range(M):
                    last = ts(score[:, m, :], bank[7][:, 0:N], scal[:, 2 + m:3 + m], add_)
                step(last)
                step(dve.scalar_tensor_tensor(flat(leaky[:, :, :]), flat(score[:, :, :]), 0.2, flat(score[:, :, :]), mul, mx))
                step(tt(flat(score[:, :, :]), flat(leaky[:, :, :]), flat(mask[:, :, :]), add_))
                dve.tensor_reduce(small[:, 0:M], score[:, :, :], AX.X, mx, negate=True).then_inc(masked, 1)
                ahead()
                for m in range(M):
                    dve.wait_ge(exped, u * 2 + m + 1)
                    last = dot(leaky[:, m, :], prob[:, m, :], cnt[:, layer, m, :], small[:, 2 + m:3 + m])
                step(last)
                if layer == 1:
                    step(ts(small[:, 2:4], small[:, 2:4], 1e-16, add_))
                step(dve.reciprocal(small[:, 4:6], small[:, 2:4]))
                for m in range(M):
                    last = ts(alpha[:, m, :], leaky[:, m, :], small[:, 4 + m:5 + m], mul)
                last.then_inc(normed, 1)
                dve.wait_ge(aT_high, u + 1)
                low_of(flat(aT_lo[:, :, :]), bank[7][:, :], flat(aT_hi[:, :, :]), aT_low)

            def gat(layer):
                c0, n0 = C_GAT[layer], NTH_GAT[layer]
                step(ts(flat(mask[:, :, :]), flat(cnt[:, layer, :, :]), 0.0, ALU.is_equal, NONE, mul))

                def head(h, last_head=False):
                    step(dve.tensor_copy(b1_head[:, :], b1c[:, layer, bass.ds(h * K, K)]))
                    scores(h + 9 * layer, layer, lambda: None if last_head else low(h * 2 + (n0 + 2), 0))
                    if last_head:
                        low(n0 + 2 * HEADS, 1)
                    a = (h + HEADS * layer) * 3
                    for j in range(3):
                        dve.wait_ge(z_kept, a + (j + 1))
                        ts(flat(neg_b[:, 2 * j:2 * j + 2, :]), flat(z_b[:, 2 * j:2 * j + 2, :]), 0.0, ALU.min).then_inc(z_neg, 1)
                    for j in range(3):
                        dve.wait_ge(z_exp, a + (j + 1))
                        dve.scalar_tensor_tensor(flat(neg_b[:, 2 * j:2 * j + 2, :]), flat(neg_b[:, 2 * j:2 * j + 2, :]), -1.0,
                                                 flat(z_b[:, 2 * j:2 * j + 2, :]), add_, mx).then_inc(elu, 1)
                    for j in range(3):
                        dve.wait_ge(hid_high, a + (j + 1))
                        low_of(hid_lo[:, 2 * j:2 * j + 2, :], neg_b[:, 2 * j:2 * j + 2, :], hid_hi[:, 2 * j:2 * j + 2, :], hid_low)
                    if not last_head:
                        low(h * 2 + (n0 + 3), 1)

                with step.loop(0, HEADS - 1, 9 + layer) as h:
                    head(h)
                head(HEADS - 1, True)
                scores(HEADS + 9 * layer, layer, lambda: None)
                low_chunk(c0 + 18)
                low_chunk(c0 + 19)
                for m in range(M):
                    dve.wait_ge(att2_mm, 2 * layer + m + 1)
                    last = to_stream(m)
                done(last)

            def to_stream(m):
                for (b, c0, c1, o) in NODE_BANKS[m]:
                    last = tt(x_sb[:, m, o:o + c1 - c0], x_sb[:, m, o:o + c1 - c0], bank[b][:, c0:c1], add_)
                return last

            blocks = [0]

            def done(last):
                blocks[0] += 1
                last.then_inc(x_new, 1)
                dve.wait_ge(x_new, blocks[0])

            dve.wait_ge(ld_x, 16)
            norm(0, 0, bias=0)
            gat(0)

            norm(1, 1)
            cls = xn[0:NCLS, 0, :]
            dve.wait_ge(ld_const, 16 * 6)
            dve.wait_ge(ld_gate, 16)
            step(dot(junk[0:NCLS, :], cls, cls, gate[:, 0:1]))
            for r in range(2):
                step(dot(junk[0:NCLS, :], gp[:, r, :], gp[:, r, :], gate[:, 1 + r:2 + r]))
                last = dot(junk[0:NCLS, :], cls, gp[:, r, :], gate[:, 3 + r:4 + r])
                if r == 0:
                    step(last)
            last.then_inc(f_dve[0], 1)
            dve.wait_ge(f_act[0], 1)
            step(ts(gate[:, 12:15], gate[:, 8:11], 1e-12, mx))
            step(dve.reciprocal(gate[:, 16:19], gate[:, 12:15]))
            step(ts(gate[:, 20:22], gate[:, 3:5], gate[:, 16:17], mul))
            step(tt(gate[:, 20:22], gate[:, 20:22], gate[:, 17:19], mul))
            step(tt(gate[:, 20:22], gate[:, 20:22], bb[:, :], add_))
            step(dve.tensor_reduce(gate[:, 19:20], gate[:, 20:22], AX.X, mx, negate=True))
            ts(gate[:, 22:24], gate[:, 20:22], gate[:, 19:20], add_).then_inc(f_dve[0], 1)
            dve.wait_ge(f_act[0], 2)
            step(dve.tensor_reduce(gate[:, 26:27], gate[:, 24:26], AX.X, add_))
            step(dve.reciprocal(gate[:, 27:28], gate[:, 26:27]))
            step(ts(gate[:, 28:30], gate[:, 24:26], gate[:, 27:28], mul))
            step(tt(gate[:, 30:31], gate[:, 28:29], gate[:, 29:30], ALU.is_ge))
            step(ts(gate[:, 31:32], gate[:, 30:31], -1.0, mul, 1.0, add_))
            step(tt(gate[:, 32:34], gate[:, 28:30], gate[:, 30:32], mul))
            for r in range(2):
                last = ts(wdiag[:, r, :], ident[0:NCLS, 0:NCLS], gate[:, 32 + r:33 + r], mul)
            last.then_inc(f_dve[0], 1)
            dve.wait_ge(f_act[0], 3)
            step(dve.memset(hrow[FH:FH + 1, :], 1.0))
            dve.memset(hrow[:, 0:NCLS], 0.0).then_inc(f_dve[0], 1)
            step(dve.memset(zt, 0.0))
            dve.wait_ge(f_act[0], 4 + ATOMS)
            low_of(hid_lo[0:FH + 1, 0, :], hrow, hid_hi[0:FH + 1, 0, :], f_dve[0])
            dve.wait_ge(f_mm[0], 2)
            for d, n0, dn, s0, ds_, cnt_, r in [(3, 0, 2, 0, 1, 3, 0), (4, 1, 2, 0, 1, 3, 0)] + \
                    [(l, 2 * l, 1, 3, 1, 2, 1) for l in range(3)]:
                a0, da = s0 * NCLS + n0, ds_ * NCLS + dn
                last = tt(zt[:, d * P + n0:d * P + n0 + dn * (cnt_ - 1) + 1:dn], hat[:, a0:a0 + da * (cnt_ - 1) + 1:da],
                          bank[5][0:FH + 1, r * NCLS + n0:r * NCLS + n0 + dn * (cnt_ - 1) + 1:dn], mul)
            last.then_inc(f_dve[0], 1)
            dve.wait_ge(f_act[0], 5 + ATOMS)
            low_of(ZT[1], zt, ZT[0], f_dve[0])
            low(NTH_GAT[1] + 1, 0)
            dve.wait_ge(f_mm[0], 3)
            to_stream(0)
            dve.wait_ge(w_used, used(C_FFN0 + 1))
            done(to_stream(1))

            norm(2, 2, bias=1)
            gat(1)

            def affine_out(s, banks_ready, bias):
                for m in range(M):
                    banks_ready(m)
                    for (b, c0, c1, o) in NODE_BANKS[m]:
                        if bias:
                            last = tt(h_sb[:, m, o:o + c1 - c0], bank[b][:, c0:c1], hbias_bc[:, o:o + c1 - c0], add_)
                        else:
                            last = dve.tensor_copy(h_sb[:, m, o:o + c1 - c0], bank[b][:, c0:c1])
                step(last)
                step(normalised(s, h_sb)[-1])
                for buf, op in ((gamma_bc, mul), (beta_bc, add_)):
                    for m in range(M):
                        last = tt(xn[:, m, :], xn[:, m, :], buf[:, :], op)
                    step(last)
                for m in range(M):
                    last = tt(x_sb[:, m, :], x_sb[:, m, :], xn[:, m, :], add_)
                done(last)

            norm(3, 3)
            for j in range(2):
                dve.wait_ge(f_act[1], 4 * j + 4)
                low_of(hid_lo[:, 2 * j:2 * j + 2, :], z_b[:, 2 * j:2 * j + 2, :], hid_hi[:, 2 * j:2 * j + 2, :], f_dve[1])
            low_chunk(C_FFN1 + 2)
            for j in range(3):
                dve.wait_ge(f_act[1], 8 + 4 * j + 4)
                low_of(xT_lo[:, 2 * j:2 * j + 2, :], neg_b[:, 2 * j:2 * j + 2, :], xT_hi[:, 2 * j:2 * j + 2, :], f_dve[1])
            low_chunk(C_GCN2)
            dve.wait_ge(ld_mid, LD_MID[1])
            affine_out(4, lambda m: dve.wait_ge(*((f_mm[1], 4) if m == 0 else (w_used, used(C_FFN1 + 2)))), True)

            def gcn_low(s):
                for m in range(M):
                    dve.wait_ge(g_kept, 4 * s + 2 * m + 2)
                    dve.wait_ge(g_high, 4 * s + 2 * m + 2)
                    low_of(h_lo[:, m, :], h_sb[:, m, :], h_hi[:, m, :], g_low)
                dve.wait_ge(rw_high, s + 1)
                low_of(rw_lo[:, :], rw[:, :], rw_hi[:, :], rw_low)

            def gcn_out(s):
                for m in range(M):
                    dve.wait_ge(g_out, 2 * s + m + 1)
                    for (b, c0, c1, o) in NODE_BANKS[m]:
                        xs = x_sb[:, m, o:o + c1 - c0]
                        last = dve.scalar_tensor_tensor(xs, bank[b][:, c0:c1], dinv[:, m:m + 1], xs, mul, add_)
                done(last)

            norm(5, 4, bias=2)
            low_chunk(C_FFN2)
            gcn_low(0)
            low_chunk(C_FFN2 + 1)
            gcn_out(0)

            def bc(ap):
                return ap.to_broadcast([P, M, 8])

            i8 = iota8[:, :].unsqueeze(1).to_broadcast([P, M, 8])

            def first_max(p, o):
                step(dve.tensor_reduce(lg[:, o, :, 0], lg[:, p, :, :], AX.X, mx))
                step(tt(lg[:, o + 1, :, :], lg[:, p, :, :], bc(lg[:, o, :, 0:1]), ALU.is_equal))
                step(tt(lg[:, o + 1, :, :], lg[:, o + 1, :, :], i8, mul))
                step(dve.tensor_reduce(lg[:, o + 2, :, 0], lg[:, o + 1, :, :], AX.X, ALU.min))
                step(tt(lg[:, o + 3, :, :], i8, bc(lg[:, o + 2, :, 0:1]), ALU.is_equal))

            def route(s):
                dve.wait_ge(f_mm[s], 1)
                step(tt(lg[:, 0, :, :], bank[6][:, 0:M * 8].rearrange("p (m e) -> p m e", m=M),
                        rb[:, :].unsqueeze(1).to_broadcast([P, M, 8]), add_))
                step(dve.tensor_reduce(lg[:, 15, :, 0], lg[:, 0, :, :], AX.X, mx))
                tt(lg[:, 1, :, :], lg[:, 0, :, :], bc(lg[:, 15, :, 0:1]), ALU.subtract).then_inc(f_dve[s], 1)
                dve.wait_ge(f_act[s], 1)
                step(dve.tensor_reduce(lg[:, 15, :, 1], lg[:, 2, :, :], AX.X, add_))
                step(dve.reciprocal(lg[:, 15, :, 2], lg[:, 15, :, 1]))
                step(tt(lg[:, 3, :, :], lg[:, 2, :, :], bc(lg[:, 15, :, 2:3]), mul))

            norm(6, 5)
            route(2)
            first_max(3, 4)
            dve.wait_ge(f_act[2], 3)
            dve.wait_ge(w_used, used(C_FFN2 + 1))
            for m, b in enumerate((5, 7)):
                last = tt(flat(neg_b[:, 2 * m:2 * m + 2, :]), flat(z_b[:, 2 * m:2 * m + 2, :]), bank[b][:, :], mul)
            step(last)
            for m in range(M):
                hm = flat(neg_b[:, 2 * m:2 * m + 2, :]).rearrange("p (e h) -> p e h", e=EXP2)
                last = tt(hm, hm, lg[:, 7, m, :].unsqueeze(2).to_broadcast([P, EXP2, HID2]), mul)
            last.then_inc(f_dve[2], 1)
            low_chunk(C_FFN2 + 2)
            for j in range(2):
                dve.wait_ge(f_act[2], 4 + j)
                low_of(flat(hid_lo[:, 2 * j:2 * j + 2, :]), bank[3 + j][:, :], flat(hid_hi[:, 2 * j:2 * j + 2, :]), f_dve[2])
            low_chunk(C_ROOT)
            dve.wait_ge(f_act[2], 9)
            for m in range(M):
                last = dve.scalar_tensor_tensor(x_sb[:, m, :], outb[:, m, :], lg[:, 4, m, 0:1], x_sb[:, m, :], mul, add_)
            done(last)

            norm(7, 6, bias=3)
            dve.wait_ge(x_high, 1)
            low_of(h_lo[:, :, :], xn[:, :, :], h_hi[:, :, :], x_low)

            def shares(half, landed):
                dve.wait_ge(ld_ct[half], landed)
                step(dve.tensor_reduce(small[:, 0:M], ct[:, half, :, :], AX.X, add_))
                step(ts(small[:, 2:4], small[:, 0:M], 1.0, mx))
                step(dve.reciprocal(small[:, 4:6], small[:, 2:4]))
                for m in range(M):
                    last = ts(REL_A[half][:, m, :], ct[:, half, m, :], small[:, 4 + m:5 + m], mul)
                last.then_inc(r_norm, 1)

            shares(0, 16)
            with step.loop(0, REL // 2, 6) as i:
                for half in range(2):
                    dve.wait_ge(r_thigh, i * 2 + (half + 1))
                    low_of(flat(aT_lo[:, :, :]), bank[7][:, :], flat(aT_hi[:, :, :]), r_tlow)
                    low(i * 2 + (nth(C_REL) + half), half)
                    shares(1 - half, i * 16 + (16 + 16 * half))
                    for j in range(3):
                        dve.wait_ge(r_high, i * 6 + (3 * half + j + 1))
                        low_of(flat(REL_T[half][1][:, 2 * j:2 * j + 2, :]), bank[3 + j][:, :],
                               flat(REL_T[half][0][:, 2 * j:2 * j + 2, :]), r_low)
            low_chunk(C_GCN3)
            dve.wait_ge(w_used, used(C_REL + REL - 1))
            for m in range(M):
                for (b, c0, c1, o) in SUM_BANKS[m]:
                    last = tt(xn[:, m, o:o + c1 - c0], bank[b][:, c0:c1], hbias_bc[:, o:o + c1 - c0], add_)
                last.then_inc(ln_xn, 1)
            transposed(7)
            low_chunk(C_FFN3)
            gcn_low(1)
            low_chunk(C_FFN3 + 1)
            gcn_out(1)

            norm(8, 8)
            route(3)
            first_max(3, 4)
            step(dve.scalar_tensor_tensor(lg[:, 8, :, :], lg[:, 7, :, :], -2.0, lg[:, 3, :, :], mul, add_))
            first_max(8, 9)
            step(tt(lg[:, 13, :, 0], lg[:, 4, :, 0], lg[:, 9, :, 0], add_))
            step(dve.reciprocal(lg[:, 13, :, 1], lg[:, 13, :, 0]))
            step(tt(lg[:, 7, :, :], lg[:, 7, :, :], bc(lg[:, 4, :, 0:1]), mul))
            step(tt(lg[:, 12, :, :], lg[:, 12, :, :], bc(lg[:, 9, :, 0:1]), mul))
            step(tt(lg[:, 14, :, :], lg[:, 7, :, :], lg[:, 12, :, :], add_))
            step(tt(lg[:, 14, :, :], lg[:, 14, :, :], bc(lg[:, 13, :, 1:2]), mul))
            dve.wait_ge(ld_mid, LD_MID[3])
            for m in range(M):
                dve.wait_ge(*((f_mm[3], 2) if m == 0 else (w_used, used(C_FFN3))))
                for (b, c0, c1, o) in NODE_BANKS[m]:
                    last = tt(h_sb[:, m, o:o + c1 - c0], bank[b][:, c0:c1], hbias_bc[:, o:o + c1 - c0], add_)
            last.then_inc(f_dve[3], 1)
            dve.wait_ge(f_act[3], 2)
            for m in range(M):
                dve.tensor_copy(ge[:, m, :, HID3], lg[:, 14, m, :])
                last = tt(ge[:, m, :, 0:HID3], h_sb[:, m, :].rearrange("p (e h) -> p e h", e=EXP3),
                          lg[:, 14, m, :].unsqueeze(2).to_broadcast([P, EXP3, HID3]), mul)
            last.then_inc(f_dve[3], 1)
            low_chunk(C_FFN3 + 2)
            for j in range(4):
                dve.wait_ge(f_act[3], 3 + j)
                low_of(HT3[j][1], bank[3 + j][0:HID3 + 1, :], HT3[j][0], f_dve[3])
            affine_out(9, lambda m: dve.wait_ge(w_used, used(C_FFN3 + 1 + m)), False)


def kernel(**inputs):
    import concourse.bacc as bacc
    from concourse.bass_utils import run_bass_kernel_spmd

    a = {name: np.asarray(v) for name, v in inputs.items()}
    arrays = {}

    def put(name, v):
        arrays[name] = np.ascontiguousarray(v)

    plain = ["x", "L0_gnn_W1", "L0_gnn_W2", "L0_gnn_a_src1", "L0_gnn_a_dst1", "L0_gnn_a_src2", "L0_gnn_a_dst2",
             "L0_gnn_b2", "L1_gnn_W1", "L1_gnn_W2", "L1_gnn_a_src1", "L1_gnn_a_dst1", "L1_gnn_a_src2", "L1_gnn_a_dst2",
             "L1_gnn_b2", "L0_ffn_gate_pair", "L0_ffn_balance_bias", "L1_ffn_bo", "L1_ffn_gamma", "L1_ffn_beta",
             "L2_gnn_W", "L2_gnn_b", "L2_ffn_router_w", "L2_ffn_router_b", "L3_gnn_W_root", "L3_gnn_b_rgcn",
             "L3_gnn_W_gcn", "L3_gnn_b_gcn", "L3_ffn_Wr", "L3_ffn_br", "L3_ffn_ln_g", "L3_ffn_ln_b"]
    for name in plain:
        put(name, a[name])
    for name in ("src", "dst", "edge_type_34"):
        put(name, a[name].reshape(ET, P).T)
    put("L0_gnn_b1", a["L0_gnn_b1"].reshape(-1, P).T)
    put("L1_gnn_b1", a["L1_gnn_b1"].reshape(-1, P).T)
    put("L1_ffn_b1", a["L1_ffn_b1"].reshape(-1, P).T)
    put("L1_ffn_b2", a["L1_ffn_b2"].reshape(-1, P).T)
    put("ffn0_in", np.concatenate([a["L0_ffn_fc1_w"].T, a["L0_ffn_atom_in_w"].transpose(2, 0, 1).reshape(D, -1)], 1))
    put("ffn0_bias", np.concatenate([a["L0_ffn_fc1_b"][None], a["L0_ffn_atom_in_b"]], 0).T)
    put("ffn0_out", np.concatenate([a["L0_ffn_fc2_w"].T, a["L0_ffn_fc2_b"][None]] +
                                   [v for d in range(ATOMS) for v in (a["L0_ffn_atom_out_w"][d].T, a["L0_ffn_atom_out_b"][d][None])], 0))
    put("L1_ffn_W1", a["L1_ffn_W1"].T)
    put("L1_ffn_W2", a["L1_ffn_W2"].T)
    put("L1_ffn_Wo", a["L1_ffn_Wo"].T)
    put("L2_ffn_w1", a["L2_ffn_w1"].transpose(1, 0, 2).reshape(D, -1))
    put("L2_ffn_w2", a["L2_ffn_w2"].transpose(1, 0, 2).reshape(D, -1))
    put("L2_ffn_w3", a["L2_ffn_w3"].reshape(-1, D))
    put("L3_gnn_W_rel", a["L3_gnn_W_rel"].reshape(-1, D))
    put("L3_ffn_W1", a["L3_ffn_W1"].transpose(1, 0, 2).reshape(D, -1))
    put("L3_ffn_b1", a["L3_ffn_b1"].reshape(-1))
    put("ffn3_out", np.concatenate([a["L3_ffn_W2"], a["L3_ffn_b2"][:, None, :]], 1).reshape(-1, D))

    nc = bacc.Bacc("TRN2", target_bir_lowering=False, num_devices=1)
    t = {}
    for name, v in arrays.items():
        t[name] = nc.dram_tensor(name, v.shape, mybir.dt.from_np(v.dtype), kind="ExternalInput").ap()
    t["out"] = nc.dram_tensor("out", (N, D), FP32, kind="ExternalOutput").ap()
    gnn_ffn_kernel(nc, t)
    r = run_bass_kernel_spmd(nc, [arrays], core_ids=[0])
    return r.results[0]["out"]
```

```python
from contextlib import ExitStack, contextmanager

import numpy as np

import concourse.bass as bass
from concourse import mybir

FP32 = mybir.dt.float32
BF16 = mybir.dt.bfloat16
FP32R = mybir.dt.float32r
INT32 = mybir.dt.int32
UINT32 = mybir.dt.uint32
ALU = mybir.AluOpType
ACT = mybir.ActivationFunctionType
AX = mybir.AxisListType

P = 128
N = 256
M = N // P
D = 768
K = D // P
E = 8192
ET = E // P
G = 4
RING = 3
HEADS = 8
REL = 34
HALF = D // 2
NONE = -1.0e30
LN_EPS = 1e-5
DUMP = REL * N
ROWS = DUMP + 2 * N
NCLS, ATOMS, FH = 6, 5, 96
INNER = 512
EXP2, HID2 = 8, 64
EXP3, HID3 = 8, 96


class Steps:

    def __init__(self, eng, sem):
        self.eng, self.sem, self.base, self.n = eng, sem, 0, 0

    def __call__(self, ins):
        ins.then_inc(self.sem, 1)
        self.n += 1
        self.eng.wait_ge(self.sem, self.base + self.n)

    @contextmanager
    def loop(self, first, last, each):
        before = self.n
        with self.eng.Fori(first, last) as i:
            self.base, self.n = (i - first) * each + before, 0
            yield i
            assert self.n == each, self.n
        self.base, self.n = 0, before + (last - first) * each


def gnn_ffn_kernel(nc, t):
    ctx = ExitStack()
    with ctx:
        def sb(name, shape, dt=FP32):
            return ctx.enter_context(nc.sbuf_tensor(name, shape, dt))

        def sem(name):
            return ctx.enter_context(nc.semaphore(name))

        w_in = sb("w_in", [P, 2, 3, D])
        w_hi = sb("w_hi", [P, 2, K, D], FP32R)
        w_lo = sb("w_lo", [P, 2, K, D], FP32R)
        x_sb = sb("x_sb", [P, M, D])
        xT_hi = sb("xT_hi", [P, K, N], FP32R)
        xT_lo = sb("xT_lo", [P, K, N], FP32R)
        h_hi = sb("h_hi", [P, M, D], FP32R)
        h_lo = sb("h_lo", [P, M, D], FP32R)
        hid_hi = sb("hid_hi", [P, K, N], FP32R)
        hid_lo = sb("hid_lo", [P, K, N], FP32R)
        z_b = sb("z_b", [P, K, N])
        h_sb = z_b[:, :, :].rearrange("p (m a) n -> p m (a n)", m=M)
        neg_b = sb("neg_b", [P, K, N])
        xn = neg_b[:, :, :].rearrange("p (m a) n -> p m (a n)", m=M)
        b1_head = sb("b1_head", [P, K])
        spare = sb("spare", [P, 1552])
        junk = spare[:, 0:D]
        ge = spare[:, :].rearrange("p (m e h) -> p m e h", m=M, e=EXP3)
        a_bc = sb("a_bc", [P, 2, D])
        gamma_bc, beta_bc = a_bc[:, 0, :], a_bc[:, 1, :]
        bias_bc = sb("bias_bc", [P, D])
        hbias_bc = sb("hbias_bc", [P, D])
        b1c = sb("b1c", [P, 2, HEADS * K])
        sbias = sb("sbias", [P, 16])
        ident = sb("ident", [P, P])
        ones = sb("ones", [P, P])
        tril = sb("tril", [P, P])
        zero = sb("zero", [P, 512], BF16)
        zrow = sb("zrow", [P, N])
        iota = sb("iota", [P, N], BF16)
        pcol = sb("pcol", [P, 1])
        iota8 = sb("iota8", [P, 8])
        edge_i = sb("edge_i", [P, 3, ET], INT32)
        edge_f = sb("edge_f", [P, 3, ET])
        key = sb("key", [P, ET])
        spill = sb("spill", [P, ET])
        osrc = sb("osrc", [P, G, N], BF16)
        kdiag = sb("kdiag", [P, G, P])
        same = sb("same", [P, G, P], BF16)
        first = sb("first", [P, G])
        row_f = sb("row_f", [P, G])
        row_i = sb("row_i", [P, G], UINT32)
        dump_i = sb("dump_i", [P, 1], UINT32)
        rows = sb("rows", [P, G, N])
        cnt = sb("cnt", [P, 2, M, N])
        mask = sb("mask", [P, M, N])
        cntT_hi = sb("cntT_hi", [P, M, N], FP32R)
        cntT_lo = sb("cntT_lo", [P, M, N], FP32R)
        dinv = sb("dinv", [P, M])
        scal = sb("scal", [P, 4])
        scores_b = sb("scores_b", [P, 2, M, N])
        score, leaky = scores_b[:, 0, :, :], scores_b[:, 1, :, :]
        ct = scores_b
        prob = sb("prob", [P, M, N])
        alpha = sb("alpha", [P, M, N])
        aT_hi = sb("aT_hi", [P, M, N], FP32R)
        aT_lo = sb("aT_lo", [P, M, N], FP32R)
        small = sb("small", [P, 8])
        stats = sb("stats", [P, M, 2, 6])
        mv = sb("mv", [P, M, 2])
        std = sb("std", [P, M])
        rstd = sb("rstd", [P, M])
        gp = h_sb[0:NCLS, :, :]
        bb = sb("bb", [NCLS, 2])
        gate = sb("gate", [NCLS, 40])
        wdiag = sb("wdiag", [NCLS, 2, NCLS])
        hat = sb("hat", [FH + 1, ATOMS * NCLS])
        zt = spare[0:FH + 1, D:D + ATOMS * P]
        rw = sb("rw", [P, K * 8])
        rw_hi = sb("rw_hi", [P, K * 8], FP32R)
        rw_lo = sb("rw_lo", [P, K * 8], FP32R)
        rb = sb("rb", [P, 8])
        lg = sb("lg", [P, 16, M, 8])
        outb = spare[:, 0:D].bitcast(BF16).rearrange("p (m n) -> p m n", m=M)
        deg = sb("deg", [P, M])
        sd = sb("sd", [P, M])
        def batches(buf):
            return buf[:, 0:RING * G * N // 2].bitcast(BF16).rearrange("p (a g n) -> p a g n", a=RING, g=G)

        all_src, all_dst = batches(spare), batches(a_bc[:, :, :].rearrange("p a n -> p (a n)"))
        hrow = prob[0:FH + 1, 0, :]

        bank = [ctx.enter_context(nc.psum_tensor(f"bank{i}", [P, 512], FP32)) for i in range(8)]
        table = nc.dram_tensor("table", (ROWS, N), FP32, kind="Internal").ap()

        w_full = [sem("w_full_0"), sem("w_full_1")]
        w_high = [sem("w_high_0"), sem("w_high_1")]
        w_low = [sem("w_low_0"), sem("w_low_1")]
        w_used = sem("w_used")
        ld_x, ld_edge, ld_const = sem("ld_x"), sem("ld_edge"), sem("ld_const")
        ld_a, ld_bias = sem("ld_a"), sem("ld_bias")
        ld_mid, ld_gate = sem("ld_mid"), sem("ld_gate")
        ld_ct = [sem("ld_ct0"), sem("ld_ct1")]
        zeroed, cleared = sem("zeroed"), sem("cleared")
        dve_step, pool_step, act_step = sem("dve_step"), sem("pool_step"), sem("act_step")
        consts = sem("consts")
        e_hot, e_used, e_cnt, e_mask = sem("e_hot"), sem("e_used"), sem("e_cnt"), sem("e_mask")
        b_hot, b_key, b_same, b_tri, b_first, b_rows, b_kept = [sem("b_" + s) for s in ("hot", "key", "same", "tri", "first", "rows", "kept")]
        b_taken, b_turn, e_added = sem("b_taken"), sem("b_turn"), sem("e_added")
        e_cntT, e_deg, e_std, e_dinv = sem("e_cntT"), sem("e_deg"), sem("e_std"), sem("e_dinv")
        e_cntT_high, e_cntT_low = sem("e_cntT_high"), sem("e_cntT_low")
        seeded = sem("seeded")
        ln_var, ln_std, ln_xn, ln_t, ln_high, ln_low = [sem("ln_" + s) for s in ("var", "std", "xn", "t", "high", "low")]
        h_mm, h_kept, h_high, h_low = sem("h_mm"), sem("h_kept"), sem("h_high"), sem("h_low")
        scored, src_row, masked, exped, normed = [sem(s) for s in ("scored", "src_row", "masked", "exped", "normed")]
        aT_mm, aT_high, aT_low = sem("aT_mm"), sem("aT_high"), sem("aT_low")
        hid_high, hid_low = sem("hid_high"), sem("hid_low")
        att_mm, z_kept, z_neg, z_exp, elu = sem("att_mm"), sem("z_kept"), sem("z_neg"), sem("z_exp"), sem("elu")
        att2_mm, out_ready = sem("att2_mm"), sem("out_ready")
        f_mm = [sem(f"ffn{s}_mm") for s in range(4)]
        f_act = [sem(f"ffn{s}_act") for s in range(4)]
        f_dve = [sem(f"ffn{s}_dve") for s in range(4)]
        g_mm, g_kept, g_high, g_low, g_out = [sem("gcn_" + s) for s in ("mm", "kept", "high", "low", "out")]
        rw_high, rw_low = sem("rw_high"), sem("rw_low")
        r_norm, r_t, r_thigh, r_tlow, r_mm, r_high, r_low = [sem("rel_" + s) for s in ("norm", "t", "thigh", "tlow", "mm", "high", "low")]
        x_high, x_low = sem("x_high"), sem("x_low")
        stored = sem("stored")


        C_GAT, C_FFN0, C_FFN1, C_GCN2, C_FFN2, C_ROOT, C_REL, C_GCN3, C_FFN3 = (0, 20), 18, 38, 41, 42, 45, 46, 80, 81

        def nth(c):
            return c - 1 if c < C_GAT[1] else c - 3

        NTH_GAT = (0, 18)
        SHAPES = {C_FFN0: (P, (3, 3), (ATOMS + 1) * FH), C_FFN0 + 1: (FH + 1, (3, 3), D), C_FFN1: (P, (3, 3), INNER),
                  C_FFN1 + 1: (P, (3, 1), D), C_FFN2: (P, (3, 3), INNER), C_FFN2 + 1: (P, (3, 3), INNER),
                  C_FFN2 + 2: (P, (3, 1), D), C_FFN3 + 1: (HID3 + 1, (3, 3), D), C_FFN3 + 2: (HID3 + 1, (1, 1), D)}
        WHOLE = (P, (3, 3), D)

        def used(c):
            return c + 3

        NCONST = 7
        LD_MID = {1: 16 * 3, 2: 16 * 6, 3: 16 * 11}

        def row_tiles(dram, n):
            return dram.rearrange("(k p) n -> p k n", p=n)

        def flat(ap):
            return ap.rearrange("p a b -> p (a b)")

        NODE_BANKS = [[(3, 0, 512, 0), (5, 0, 256, 512)], [(6, 0, 512, 0), (7, 0, 256, 512)]]
        SUM_BANKS = [[(0, 0, 512, 0), (2, 0, 256, 512)], [(1, 0, 512, 0), (2, 256, 512, 512)]]
        HT3 = [[flat(ap[0:HID3 + 1, 2 * j:2 * j + 2, :]) for ap in (hid_hi, hid_lo)] for j in range(3)] + \
              [[ap[0:HID3 + 1, 0, 0:512] for ap in (h_hi, h_lo)]]
        ZT = [flat(ap[0:FH + 1, 2:6, :])[:, 0:ATOMS * P] for ap in (hid_hi, hid_lo)]
        REL_A = [alpha, prob]
        REL_T = [(hid_hi, hid_lo), (xT_hi, xT_lo)]

        block = ctx.enter_context(nc.Block())

        @block.sync
        def _(sp):
            sp.dma_start(x_sb[:, :, :], row_tiles(t["x"], P)).then_inc(ld_x, 16)
            for j, name in enumerate(("src", "dst", "edge_type_34")):
                sp.dma_start(edge_i[:, j, :], t[name]).then_inc(ld_edge, 16)
            def load(n, dram, shape=WHOLE):
                rows_, tiles, cols = shape
                for p in range(2):
                    sp.wait_ge(w_high[p], n)
                    sp.wait_ge(w_low[p], n)
                    sp.dma_start(w_in[0:rows_, p, 0:tiles[p], 0:cols],
                                 row_tiles(dram, rows_)[:, p * tiles[0]:p * tiles[0] + tiles[p], :]).then_inc(w_full[p], 16)

            def load_chunk(c, dram):
                load(nth(c), dram, SHAPES.get(c, WHOLE))

            def gat(layer):
                w1, w2, n0 = t[f"L{layer}_gnn_W1"], t[f"L{layer}_gnn_W2"], NTH_GAT[layer]
                load(n0 + 1, w1[:, 0:D])
                if layer == 0:
                    sp.wait_ge(zeroed, 1)
                    sp.dma_start(table.rearrange("(p t) n -> p t n", p=P),
                                 zrow[:, :].unsqueeze(1).to_broadcast([P, ROWS // P, N])).then_inc(cleared, 16)
                with sp.Fori(0, HEADS - 1) as h:
                    load(h * 2 + (n0 + 2), w1[:, bass.ds((h + 1) * D, D)])
                    load(h * 2 + (n0 + 3), w2[bass.ds(h * D, D), :])
                load(n0 + 2 * HEADS, w2[(HEADS - 1) * D:HEADS * D, :])

            gat(0)
            load_chunk(C_FFN0, t["ffn0_in"])
            load_chunk(C_FFN0 + 1, t["ffn0_out"])
            gat(1)
            load_chunk(C_FFN1, t["L1_ffn_W1"])
            load_chunk(C_FFN1 + 1, t["L1_ffn_W2"])
            load_chunk(C_FFN1 + 2, t["L1_ffn_Wo"])
            load_chunk(C_GCN2, t["L2_gnn_W"])
            load_chunk(C_FFN2, t["L2_ffn_w1"])
            load_chunk(C_FFN2 + 1, t["L2_ffn_w2"])
            load_chunk(C_FFN2 + 2, t["L2_ffn_w3"])
            load_chunk(C_ROOT, t["L3_gnn_W_root"])
            with sp.Fori(0, REL) as r:
                load(r + nth(C_REL), t["L3_gnn_W_rel"][bass.ds(r * D, D), :])
            load_chunk(C_GCN3, t["L3_gnn_W_gcn"])
            load_chunk(C_FFN3, t["L3_ffn_W1"])
            load_chunk(C_FFN3 + 1, t["ffn3_out"][0:K * (HID3 + 1), :])
            load_chunk(C_FFN3 + 2, t["ffn3_out"][K * (HID3 + 1):, :])
            for m in range(M):
                sp.wait_ge(out_ready, m + 1)
                sp.dma_start(t["out"][m * P:(m + 1) * P, :], x_sb[:, m, :]).then_inc(stored, 16)
            sp.wait_ge(stored, 16 * M)

        @block.gpsimd
        def _(pool):
            step = Steps(pool, pool_step)
            pool.memset(zrow[:, :], 0.0).then_inc(zeroed, 1)
            pool.memset(ones[:, :], 1.0).then_inc(consts, 1)
            pool.memset(zero[:, :], 0.0).then_inc(consts, 1)
            pool.memset(hat[:, :], 1.0).then_inc(w_used, 2)
            pool.memset(first[:, :], 0.0).then_inc(b_taken, 1)
            for p in range(2):
                pool.memset(small[:, p:p + 1], 0.0).then_inc(w_high[p], 1)
                pool.memset(small[:, 2 + p:3 + p], 0.0).then_inc(w_low[p], 1)
            step(pool.memset(ident[:, :], 0.0))
            step(pool.memset(tril[:, :], 1.0))
            pool.affine_select(out=ident[:, :], in_=ident[:, :], compare_op=ALU.not_equal, fill=1.0, base=0,
                               pattern=[[-1, P]], channel_multiplier=1).then_inc(consts, 1)
            pool.affine_select(out=tril[:, :], in_=tril[:, :], compare_op=ALU.is_gt, fill=0.0, base=0,
                               pattern=[[-1, P]], channel_multiplier=1).then_inc(consts, 1)
            pool.iota(iota[:, :], pattern=[[1, N]], base=0, channel_multiplier=0,
                      allow_small_or_imprecise_dtypes=True).then_inc(consts, 1)
            pool.iota(pcol[:, :], pattern=[[0, 1]], base=DUMP, channel_multiplier=1,
                      allow_small_or_imprecise_dtypes=True).then_inc(consts, 1)
            pool.iota(iota8[:, :], pattern=[[1, 8]], base=-8, channel_multiplier=0,
                      allow_small_or_imprecise_dtypes=True).then_inc(consts, 1)

            def low(n, half, shape=WHOLE):
                rows_, tiles, cols = shape
                pool.wait_ge(w_high[1], n + 1)
                pool.tensor_tensor(w_lo[0:rows_, half, 3:3 + tiles[1], 0:cols], w_in[0:rows_, 1, 0:tiles[1], 0:cols],
                                   w_hi[0:rows_, half, 3:3 + tiles[1], 0:cols].bitcast(FP32), ALU.subtract).then_inc(w_low[1], 1)

            def low_chunk(c):
                low(nth(c), c % 2, SHAPES.get(c, WHOLE))

            def index(b):
                pool.wait_ge(e_added, b * (16 * G) + 16)
                pool.wait_ge(b_first, b + 1)
                step(pool.tensor_tensor(row_f[:, :], spill[:, bass.ds(b * G, G)], first[:, :], ALU.mult))
                step(pool.tensor_tensor(row_f[:, :], row_f[:, :], key[:, bass.ds(b * G, G)], ALU.add))
                pool.sem_inc(b_turn, 1)
                step(pool.tensor_copy(row_i[:, :], row_f[:, :]))
                pool.sem_inc(b_taken, 1)

            def add(b, g):
                pool.wait_ge(b_kept, b * 2 + (g // 2 + 1))
                pool.wait_ge(e_added, b * (16 * G) + (16 * g + 16))
                pool.sem_inc(b_turn, 1)
                pool.indirect_dma_start(
                    out=table, out_offset=bass.IndirectOffsetOnAxis(ap=row_i[:, g:g + 1], axis=0),
                    in_=rows[:, g, :], in_offset=None, compute_op=ALU.add).then_inc(e_added, 16)

            def batch(b):
                index(b)
                for g in range(G):
                    add(b, g)

            def gat(layer):
                c0, n0, b0 = C_GAT[layer], NTH_GAT[layer], layer * HEADS

                def head(h):
                    low(h * 2 + (n0 + 2), 0)
                    batch(h + (b0 - 1))
                    low(h * 2 + (n0 + 3), 1)

                for half in range(2):
                    low(n0 + 2 + half, half)
                with step.loop(1, HEADS - 1, 3) as h:
                    head(h)
                low(n0 + 2 * HEADS, 1)
                low_chunk(c0 + 18)
                batch(HEADS - 2 + b0)
                low_chunk(c0 + 19)
                batch(HEADS - 1 + b0)

            low(1, 0)
            pool.wait_ge(consts, NCONST)
            step(pool.tensor_copy(dump_i[:, :], pcol[:, :]))
            pool.wait_ge(cleared, 16)
            pool.indirect_dma_start(
                out=table, out_offset=bass.IndirectOffsetOnAxis(ap=dump_i[:, :], axis=0),
                in_=zrow[:, :], in_offset=None, compute_op=ALU.add).then_inc(e_added, 16)
            gat(0)
            low(NTH_GAT[1] + 1, 0)
            gat(1)
            for c in range(C_FFN1 + 2, C_REL):
                low_chunk(c)
            with pool.Fori(0, REL // 2) as i:
                for half in range(2):
                    low(i * 2 + (nth(C_REL) + half), half)
            for c in range(C_GCN3, C_FFN3 + 3):
                low_chunk(c)

        @block.tensor
        def _(pe):
            def mm(out, lhsT, rhs, start=True, stop=True, **kw):
                return pe.matmul(out, lhsT, rhs, start=start, stop=stop, **kw)

            def mm3(outs, lhsT, start, stop, **kw):
                for a in range(2):
                    for out, rhs in outs:
                        for b in range(2 - a):
                            last = mm(out, lhsT[a], rhs[b], start and a + b == 0, stop and a == 1, **kw)
                return last

            def part(hi, lo, *idx):
                return hi[idx], lo[idx]

            def weights(n):
                for p in range(2):
                    pe.wait_ge(w_low[p], n + 1)

            def chunk(c):
                weights(nth(c))

            def seed(banks):
                for b in banks:
                    last = mm(bank[b][:, :], zero[:, 0:P], zero[:, :], True, False, skip_group_check=True)
                return last

            def transposed(i):
                for m in range(M):
                    pe.wait_ge(ln_xn, 2 * i + m + 1)
                    for j in range(3):
                        for k in (2 * j, 2 * j + 1):
                            last = pe.transpose(bank[3 + j][:, (k % 2) * N + m * P:(k % 2) * N + (m + 1) * P],
                                                xn[:, m, k * P:(k + 1) * P], ident[:, :])
                        if m == M - 1:
                            last.then_inc(ln_t, 1)
                pe.wait_ge(ln_low, 3 * i + 3)

            def nodes(m, banks, lhs, rhs):
                n = len(lhs)
                for k in range(n):
                    last = mm3([(bank[b][:, c0:c1], rhs(k, o, o + c1 - c0)) for (b, c0, c1, o) in banks[m]],
                               lhs[k], k == 0, k == n - 1)
                return last

            def add(m, lhs, rhs, end=False):
                n = len(lhs)
                for k in range(n):
                    last = mm3([(bank[b][:, c0:c1], rhs(k, o, o + c1 - c0)) for (b, c0, c1, o) in SUM_BANKS[m]],
                               lhs[k], False, end and k == n - 1, skip_group_check=True)
                return last

            def node_tile(hi, lo, m, ks):
                return [(hi[:, k, m * P:(m + 1) * P], lo[:, k, m * P:(m + 1) * P]) for k in range(ks)]

            def of_w(half, rows_=P):
                return lambda k, c0, c1: (w_hi[0:rows_, half, k, c0:c1], w_lo[0:rows_, half, k, c0:c1])

            def of_h(sm, c0, c1):
                return h_hi[:, sm, c0:c1], h_lo[:, sm, c0:c1]

            def batch_keys(b):
                pe.wait_ge(b_hot, b + 1)
                for g in range(G):
                    last = mm(bank[7][:, g * P:(g + 1) * P], ones[:, :], kdiag[:, g, :])
                last.then_inc(b_key, 1)

            def batch_rows(b, j, to=7):
                pe.wait_ge(b_same, b + 1)
                if j == 1 and to == 7:
                    pe.wait_ge(b_kept, b * 2 + 1)
                for g in range(2):
                    last = mm(bank[to][:, g * N:(g + 1) * N], same[:, 2 * j + g, :], osrc[:, 2 * j + g, :])
                last.then_inc(b_rows, 1)

            def spread(u):
                pe.wait_ge(scored, u + 1)
                for m in range(M):
                    last = mm(bank[7][:, m * P:(m + 1) * P], scal[:, m:m + 1].to_broadcast([P, P]), ident[:, :])
                last.then_inc(src_row, 1)

            def turn(u):
                pe.wait_ge(normed, u + 1)
                for sm in range(M):
                    for m in range(M):
                        last = pe.transpose(bank[7][:, sm * N + m * P:sm * N + (m + 1) * P], alpha[:, m, sm * P:(sm + 1) * P], ident[:, :])
                last.then_inc(aT_mm, 1)

            def parts_kept(u):
                pe.wait_ge(aT_low, u + 1)
                pe.wait_ge(h_low, u * 2 + 2)

            def gat(layer, between=lambda: None):
                c0, n0, b0 = C_GAT[layer], NTH_GAT[layer], layer * HEADS

                def up(h, n, first=False):
                    for m, banks in ((0, (5, 6)), (1, (3, 4))):
                        if not first:
                            pe.wait_ge(z_kept, (h + HEADS * layer) * 3 + (-2 if m == 0 else 0))
                        if m == 1:
                            between() if first else batch_rows(h + (b0 - 1), 0)
                        for k in range(K):
                            if m == 0 and k % 3 == 0:
                                pe.wait_ge(w_low[k // 3], n + 1)
                            last = mm3([(bank[banks[j]][:, 0:HALF], part(w_hi, w_lo, slice(0, P), 0, k, slice(j * HALF, (j + 1) * HALF)))
                                        for j in range(2)],
                                       part(xT_hi, xT_lo, slice(0, P), k, slice(m * P, (m + 1) * P)), k == 0, k == K - 1)
                        last.then_inc(*((h_mm, 1) if m == 0 else (w_used, 2 if first else 1)))
                    if not first:
                        batch_rows(h + (b0 - 1), 1)

                def down(h, n, i0, i1, last_head=False):
                    for i in range(i0, i1):
                        m, k = i // K, i % K
                        if m == 0 and k % 2 == 0:
                            pe.wait_ge(hid_low, (h + HEADS * layer) * 3 + (k // 2 + 1))
                        if m == 0 and k % 3 == 0:
                            pe.wait_ge(w_low[k // 3], n + 1)
                        last = mm3([(bank[b][:, c0_:c1], of_w(1)(k, o, o + c1 - c0_)) for (b, c0_, c1, o) in SUM_BANKS[m]],
                                   part(hid_hi, hid_lo, slice(0, P), k, slice(m * P, (m + 1) * P)), False,
                                   last_head and k == K - 1, skip_group_check=True)
                    if i1 == M * K:
                        last.then_inc(w_used, 2 if last_head else 1)

                def attend(h):
                    for j, b in enumerate((5, 3, 4)):
                        for k in (2 * j, 2 * j + 1):
                            for sm in range(M):
                                last = mm3([(bank[b][:, (k % 2) * N:(k % 2 + 1) * N], part(aT_hi, aT_lo, slice(0, P), sm))],
                                           of_h(sm, k * P, (k + 1) * P), sm == 0, sm == M - 1)
                        last.then_inc(att_mm, 1)

                up(0, n0 + 1, True)
                pe.wait_ge(*((e_mask, 1) if layer == 0 else (b_kept, 2 * b0)))
                seed((0, 1, 2))
                spread(9 * layer)
                turn(9 * layer)
                parts_kept(9 * layer)
                attend(0)
                with pe.Fori(1, HEADS) as h:
                    batch_keys(h + (b0 - 1))
                    up(h, h * 2 + n0)
                    down(h - 1, h * 2 + (n0 + 1), 0, 3)
                    pe.wait_ge(b_kept, h * 2 + 2 * b0)
                    spread(h + 9 * layer)
                    down(h - 1, h * 2 + (n0 + 1), 3, 11)
                    turn(h + 9 * layer)
                    down(h - 1, h * 2 + (n0 + 1), 11, M * K)
                    parts_kept(h + 9 * layer)
                    attend(h)
                batch_keys(HEADS - 1 + b0)
                down(HEADS - 1, n0 + 2 * HEADS, 0, M * K, True)
                pe.wait_ge(b_same, HEADS + b0)
                spread(HEADS + 9 * layer)
                pe.wait_ge(h_high, (HEADS + 9 * layer) * 4 + 4)
                for j in range(2):
                    batch_rows(HEADS - 1 + b0, j, to=j)
                turn(HEADS + 9 * layer)
                parts_kept(HEADS + 9 * layer)
                for m in range(M):
                    nodes(m, NODE_BANKS, [part(aT_hi, aT_lo, slice(0, P), sm, slice(m * P, (m + 1) * P)) for sm in range(M)],
                          of_h).then_inc(att2_mm, 1)

            pe.wait_ge(consts, NCONST)
            seed((0,)).then_inc(e_used, RING)
            transposed(0)

            def count():
                def count_batch(b, a):
                    pe.wait_ge(e_hot, b + 1)
                    for g in range(G):
                        for m in range(M):
                            last = mm(bank[0][:, m * N:(m + 1) * N], all_dst[:, a, g, m * P:(m + 1) * P], all_src[:, a, g, :],
                                      False, False, skip_group_check=True)
                    last.then_inc(e_used, 1)

                with pe.Fori(0, ET // G // RING) as i:
                    for a in range(RING):
                        count_batch(i * RING + a, a)
                for a in range(ET // G % RING):
                    count_batch(ET // G // RING * RING + a, a)
                mm(bank[0][:, :], zero[:, 0:P], zero[:, :], False, True, skip_group_check=True).then_inc(e_cnt, 1)

            gat(0, count)

            transposed(1)
            chunk(C_FFN0)
            for k in range(K):
                last = mm3([(bank[3][0:FH, 0:N], part(xT_hi, xT_lo, slice(0, P), k))], of_w(0)(k, 0, FH), k == 0, k == K - 1)
            last.then_inc(f_mm[0], 1)
            for a in range(ATOMS):
                for k in range(K):
                    last = mm3([(bank[4][0:FH, a * NCLS:(a + 1) * NCLS], part(xT_hi, xT_lo, slice(0, P), k, slice(0, NCLS)))],
                               of_w(0)(k, (a + 1) * FH, (a + 2) * FH), k == 0, k == K - 1)
            last.then_inc(w_used, 1)
            pe.wait_ge(f_dve[0], 3)
            mm(bank[5][0:FH + 1, 0:2 * NCLS], ones[0:NCLS, 0:FH + 1], flat(wdiag[:, :, :])).then_inc(f_mm[0], 1)
            pe.wait_ge(f_dve[0], 7)
            chunk(C_FFN0 + 1)
            hid0 = [part(hid_hi, hid_lo, slice(0, FH + 1), 0, slice(m * P, (m + 1) * P)) for m in range(M)]
            nodes(0, NODE_BANKS, [hid0[0]] + [(ZT[0][:, d * P:(d + 1) * P], ZT[1][:, d * P:(d + 1) * P]) for d in range(ATOMS)],
                  of_w(1, FH + 1)).then_inc(f_mm[0], 1)
            nodes(1, NODE_BANKS, [hid0[1]], of_w(1, FH + 1)).then_inc(w_used, 1)

            transposed(2)
            gat(1)

            transposed(3)

            def columns(count, half, hi, lo, ks, first_bank, marks):
                for c in range(count):
                    for k in range(ks):
                        last = mm3([(bank[first_bank + c // 2][:, (c % 2) * N:(c % 2 + 1) * N], part(hi, lo, slice(0, P), k))],
                                   of_w(half)(k, c * P, (c + 1) * P), k == 0, k == ks - 1)
                    if c % 2:
                        last.then_inc(marks[c // 2], 1)

            chunk(C_FFN1)
            columns(INNER // P, 0, xT_hi, xT_lo, K, 3, (f_mm[1], w_used))
            pe.wait_ge(b_kept, 4 * HEADS)
            for sm in range(M):
                for m in range(M):
                    last = pe.transpose(bank[1][:, sm * N + m * P:sm * N + (m + 1) * P], cnt[:, 0, m, sm * P:(sm + 1) * P], ident[:, :])
            last.then_inc(e_cntT, 1)
            pe.wait_ge(f_dve[1], 2)
            chunk(C_FFN1 + 1)
            columns(K, 1, hid_hi, hid_lo, INNER // P, 5, (f_mm[1], f_mm[1], w_used))
            pe.wait_ge(f_dve[1], 5)
            chunk(C_FFN1 + 2)
            nodes(0, NODE_BANKS, node_tile(xT_hi, xT_lo, 0, K), of_w(0)).then_inc(f_mm[1], 1)
            nodes(1, NODE_BANKS, node_tile(xT_hi, xT_lo, 1, K), of_w(0)).then_inc(w_used, 1)

            def gcn(s, half, c):
                chunk(c)
                nodes(0, NODE_BANKS, node_tile(xT_hi, xT_lo, 0, K), of_w(half)).then_inc(g_mm, 1)
                nodes(1, NODE_BANKS, node_tile(xT_hi, xT_lo, 1, K), of_w(half)).then_inc(w_used, 1)
                pe.wait_ge(e_cntT_low, 1)
                pe.wait_ge(g_low, 2 * s + 2)
                for m in range(M):
                    nodes(m, NODE_BANKS, [part(cntT_hi, cntT_lo, slice(0, P), sm, slice(m * P, (m + 1) * P)) for sm in range(M)],
                          of_h).then_inc(g_out, 1)

            def router(s):
                pe.wait_ge(rw_low, s - 1)
                for m in range(M):
                    for k in range(K):
                        last = mm3([(bank[6][:, m * 8:(m + 1) * 8], part(rw_hi, rw_lo, slice(0, P), slice(k * 8, (k + 1) * 8)))],
                                   part(xT_hi, xT_lo, slice(0, P), k, slice(m * P, (m + 1) * P)), k == 0, k == K - 1)
                last.then_inc(f_mm[s], 1)

            transposed(4)
            gcn(0, 1, C_GCN2)

            transposed(5)
            router(2)
            for half, banks in ((0, (3, 4)), (1, (5, 7))):
                chunk(C_FFN2 + half)
                for m, b in enumerate(banks):
                    for k in range(K):
                        last = mm3([(bank[b][:, :], of_w(half)(k, 0, INNER))], part(xT_hi, xT_lo, slice(0, P), k, slice(m * P, (m + 1) * P)),
                                   k == 0, k == K - 1)
                last.then_inc(w_used, 1)
            pe.wait_ge(f_dve[2], 2)
            for j in range(2):
                for k in (2 * j, 2 * j + 1):
                    for m in range(M):
                        last = pe.transpose(bank[3 + j][:, (k % 2) * N + m * P:(k % 2) * N + (m + 1) * P],
                                            flat(neg_b[:, 2 * m:2 * m + 2, :])[:, k * P:(k + 1) * P], ident[:, :])
                last.then_inc(f_mm[2], 1)
            pe.wait_ge(f_dve[2], 4)
            chunk(C_FFN2 + 2)
            nodes(0, NODE_BANKS, node_tile(hid_hi, hid_lo, 0, INNER // P), of_w(0)).then_inc(f_mm[2], 1)
            nodes(1, NODE_BANKS, node_tile(hid_hi, hid_lo, 1, INNER // P), of_w(0)).then_inc(w_used, 1)

            transposed(6)
            seed((0, 1, 2))
            chunk(C_ROOT)
            add(0, node_tile(xT_hi, xT_lo, 0, K), of_w(1))
            add(1, node_tile(xT_hi, xT_lo, 1, K), of_w(1)).then_inc(w_used, 1)

            def turn_rel(r, half):
                pe.wait_ge(r_norm, r + 1)
                for sm in range(M):
                    for m in range(M):
                        last = pe.transpose(bank[7][:, sm * N + m * P:sm * N + (m + 1) * P], REL_A[half][:, m, sm * P:(sm + 1) * P], ident[:, :])
                last.then_inc(r_t, 1)

            def mean(r):
                pe.wait_ge(r_tlow, r + 1)
                for j in range(3):
                    for k in (2 * j, 2 * j + 1):
                        for sm in range(M):
                            last = mm3([(bank[3 + j][:, (k % 2) * N:(k % 2 + 1) * N], part(aT_hi, aT_lo, slice(0, P), sm))],
                                       of_h(sm, k * P, (k + 1) * P), sm == 0, sm == M - 1)
                    last.then_inc(r_mm, 1)

            def relation(r, half, ahead=True, end=False):
                if ahead:
                    turn_rel(r + 1, 1 - half)
                pe.wait_ge(r_low, r * 3 + 3)
                weights(r + nth(C_REL))
                add(0, node_tile(*REL_T[half], 0, K), of_w(half), end)
                if ahead:
                    mean(r + 1)
                add(1, node_tile(*REL_T[half], 1, K), of_w(half), end).then_inc(w_used, 1)

            turn_rel(0, 0)
            pe.wait_ge(x_low, 1)
            mean(0)
            with pe.Fori(0, REL // 2 - 1) as i:
                relation(i * 2, 0)
                relation(i * 2 + 1, 1)
            relation(REL - 2, 0)
            relation(REL - 1, 1, False, True)
            transposed(7)
            gcn(1, 0, C_GCN3)

            transposed(8)
            router(3)
            chunk(C_FFN3)
            nodes(0, NODE_BANKS, node_tile(xT_hi, xT_lo, 0, K), of_w(1)).then_inc(f_mm[3], 1)
            pe.wait_ge(f_dve[3], 1)
            nodes(1, NODE_BANKS, node_tile(xT_hi, xT_lo, 1, K), of_w(1)).then_inc(w_used, 1)
            pe.wait_ge(f_dve[3], 3)
            for j in range(4):
                for e in (2 * j, 2 * j + 1):
                    for m in range(M):
                        last = pe.transpose(bank[3 + j][0:HID3 + 1, (e % 2) * N + m * P:(e % 2) * N + (m + 1) * P],
                                            ge[:, m, e, :], ident[:, :])
                last.then_inc(f_mm[3], 1)
            pe.wait_ge(f_dve[3], 7)
            chunk(C_FFN3 + 1)
            chunk(C_FFN3 + 2)
            for m in range(M):
                last = nodes(m, NODE_BANKS, [[ap[:, (e % 2) * N + m * P:(e % 2) * N + (m + 1) * P] for ap in HT3[e // 2]] for e in range(EXP3)],
                             lambda e, a, b: of_w(e // K, HID3 + 1)(e if e < K else (e - K) * 3, a, b))
                last.then_inc(w_used, 1)

        @block.scalar
        def _(act):
            act.dma_start(bias_bc[:, :], t["L0_gnn_b2"].partition_broadcast(P)).then_inc(ld_bias, 16)
            act.dma_start(b1c[:, 0, :], t["L0_gnn_b1"]).then_inc(ld_const, 16)
            act.dma_start(b1c[:, 1, :], t["L1_gnn_b1"]).then_inc(ld_const, 16)
            act.dma_start(bb[:, :], t["L0_ffn_balance_bias"]).then_inc(ld_const, 16)
            act.dma_start(sbias[0:FH, 0:ATOMS + 1], t["ffn0_bias"]).then_inc(ld_const, 16)
            act.dma_start(sbias[:, 6:10], t["L1_ffn_b1"]).then_inc(ld_const, 16)
            act.dma_start(sbias[:, 10:16], t["L1_ffn_b2"]).then_inc(ld_const, 16)

            def row_bc(out, dram, mark):
                act.dma_start(out, dram.partition_broadcast(P)).then_inc(mark, 16)

            def load_heads(layer, h):
                for j, a in enumerate(("a_src1", "a_dst1")):
                    row_bc(a_bc[:, j, :], t[f"L{layer}_gnn_{a}"][bass.ds(h, 1), :].rearrange("a n -> (a n)"), ld_a)

            def load_last(layer):
                for j, a in enumerate(("a_src2", "a_dst2")):
                    row_bc(a_bc[:, j, :], t[f"L{layer}_gnn_{a}"][0, :], ld_a)

            def keep(out, ps, mark, func=ACT.Copy, **kw):
                act.activation(out, ps, func, **kw).then_inc(mark, 1)

            def high(n, free, half, shape=WHOLE):
                rows_, tiles, cols = shape
                act.wait_ge(w_used, free)
                for p in range(2):
                    act.wait_ge(w_full[p], n * 16)
                    keep(w_hi[0:rows_, half, 3 * p:3 * p + tiles[p], 0:cols], w_in[0:rows_, p, 0:tiles[p], 0:cols], w_high[p])

            def high_chunk(c):
                high(nth(c), used(c - 2), c % 2, SHAPES.get(c, WHOLE))

            deviations = [0]

            def deviation(*tiles):
                for m in tiles:
                    deviations[0] += 1
                    act.wait_ge(ln_var, deviations[0])
                    keep(std[:, m:m + 1], mv[:, m, 1:2], ln_std, ACT.Sqrt, bias=LN_EPS)

            def transposed(i):
                for j in range(3):
                    act.wait_ge(ln_t, 3 * i + j + 1)
                    keep(flat(xT_hi[:, 2 * j:2 * j + 2, :]), bank[3 + j][:, :], ln_high)

            def attend(u, ahead):
                act.wait_ge(masked, u + 1)
                for m in range(M):
                    keep(prob[:, m, :], score[:, m, :], exped, ACT.Exp, bias=small[:, m:m + 1])
                ahead()
                act.wait_ge(aT_mm, u + 1)
                keep(flat(aT_hi[:, :, :]), bank[7][:, :], aT_high)

            def batch_rows(b, j, at=7):
                if j == 0:
                    act.wait_ge(e_added, b * (16 * G) + 16)
                act.wait_ge(b_rows, b * 2 + (j + 1))
                keep(flat(rows[:, 2 * j:2 * j + 2, :]), bank[at][:, :], b_kept)

            def gat(layer, after):
                c0, n0, b0 = C_GAT[layer], NTH_GAT[layer], layer * HEADS

                def head(h, ahead, first_head=False, last_head=False):
                    u = h + 9 * layer
                    for m, banks in ((0, (5, 6)), (1, (3, 4))):
                        if m == 0:
                            act.wait_ge(h_mm, h + (HEADS * layer + 1))
                        else:
                            act.wait_ge(w_used, h * 2 + used(c0))
                        for out, mark in ((h_sb, h_kept), (h_hi, h_high)):
                            for j in range(2):
                                keep(out[:, m, j * HALF:(j + 1) * HALF], bank[banks[j]][:, 0:HALF], mark)
                        if not first_head:
                            batch_rows(h + (b0 - 1), m)
                    if not last_head:
                        high(h * 2 + (n0 + 2), h * 2 + (c0 + 3), 0)
                    attend(u, ahead)
                    n2 = n0 + 2 * HEADS if last_head else h * 2 + (n0 + 3)
                    if last_head:
                        high(n2, h * 2 + (c0 + 4), 1)
                    a = (h + HEADS * layer) * 3
                    for j, b in enumerate((5, 3, 4)):
                        act.wait_ge(att_mm, a + (j + 1))
                        for k in (2 * j, 2 * j + 1):
                            last = act.activation(z_b[:, k, :], bank[b][:, (k % 2) * N:(k % 2 + 1) * N], ACT.Identity,
                                                  bias=b1_head[:, k:k + 1])
                        last.then_inc(z_kept, 1)
                    for j in range(3):
                        act.wait_ge(z_neg, a + (j + 1))
                        keep(neg_b[:, 2 * j:2 * j + 2, :], neg_b[:, 2 * j:2 * j + 2, :], z_exp, ACT.Exp)
                    if not last_head:
                        high(n2, h * 2 + (c0 + 4), 1)
                    for j in range(3):
                        act.wait_ge(elu, a + (j + 1))
                        keep(hid_hi[:, 2 * j:2 * j + 2, :], neg_b[:, 2 * j:2 * j + 2, :], hid_high)

                head(0, lambda: load_heads(layer, 1), first_head=True)
                with act.Fori(1, HEADS - 1) as h:
                    head(h, lambda: load_heads(layer, h + 1))
                head(HEADS - 1, lambda: load_last(layer), last_head=True)
                high(nth(c0 + 18), c0 + 17, 0, SHAPES.get(c0 + 18, WHOLE))
                act.wait_ge(w_used, used(c0 + 17))
                for out, mark in ((h_sb, h_kept), (h_hi, h_high)):
                    for m in range(M):
                        for (b, c0_, c1, o) in SUM_BANKS[m]:
                            keep(out[:, m, o:o + c1 - c0_], bank[b][:, c0_:c1], mark)
                attend(HEADS + 9 * layer, after)
                high_chunk(c0 + 19)

            deviation(0, 1)
            transposed(0)
            high(1, 1, 0)
            act.wait_ge(ld_const, 16 * 6)
            act.wait_ge(e_cnt, 1)
            load_heads(0, 0)
            gat(0, lambda: load_heads(1, 0))
            act.wait_ge(h_low, 2 * (HEADS + 1))
            act.dma_start(gp[:, :, :], t["L0_ffn_gate_pair"]).then_inc(ld_gate, 16)

            deviation(0, 1)
            transposed(1)
            for j in range(2):
                batch_rows(HEADS * 1 - 1, j, at=j)
            row_bc(bias_bc[:, :], t["L1_gnn_b2"], ld_bias)
            act.wait_ge(f_dve[0], 1)
            keep(gate[:, 8:11], gate[:, 0:3], f_act[0], ACT.Sqrt)
            act.wait_ge(f_dve[0], 2)
            keep(gate[:, 24:26], gate[:, 22:24], f_act[0], ACT.Exp)
            act.wait_ge(f_mm[0], 1)
            keep(hrow[0:FH, :], bank[3][0:FH, 0:N], f_act[0], ACT.Gelu, bias=sbias[0:FH, 0:1])
            act.wait_ge(w_used, used(C_FFN0))
            for a in range(ATOMS):
                keep(hat[0:FH, a * NCLS:(a + 1) * NCLS], bank[4][0:FH, a * NCLS:(a + 1) * NCLS], f_act[0], ACT.Gelu,
                     bias=sbias[0:FH, a + 1:a + 2])
            act.wait_ge(f_dve[0], 4)
            keep(hid_hi[0:FH + 1, 0, :], hrow, f_act[0])
            act.wait_ge(f_dve[0], 6)
            keep(ZT[0], zt, f_act[0])
            high(NTH_GAT[1] + 1, used(C_GAT[1] - 2), 0)

            deviation(0, 1)
            transposed(2)
            gat(1, lambda: None)

            deviation(0, 1)
            transposed(3)
            for j in range(2):
                batch_rows(HEADS * 2 - 1, j, at=j)
            row_bc(hbias_bc[:, :], t["L1_ffn_bo"], ld_mid)
            row_bc(gamma_bc[:, :], t["L1_ffn_gamma"], ld_mid)
            row_bc(beta_bc[:, :], t["L1_ffn_beta"], ld_mid)
            row_bc(bias_bc[:, :], t["L2_gnn_b"], ld_bias)
            for c in range(INNER // P):
                act.wait_ge(*((f_mm[1], 1) if c < 2 else (w_used, used(C_FFN1))))
                for out in (z_b, hid_hi):
                    keep(out[:, c, :], bank[3 + c // 2][:, (c % 2) * N:(c % 2 + 1) * N], f_act[1], ACT.Relu,
                         bias=sbias[:, 6 + c:7 + c])
            high_chunk(C_FFN1 + 2)
            act.wait_ge(e_cntT, 1)
            keep(flat(cntT_hi[:, :, :]), bank[1][:, :], e_cntT_high)
            act.wait_ge(e_deg, 1)
            keep(sd[:, :], deg[:, :], e_std, ACT.Sqrt)
            for c in range(K):
                act.wait_ge(*((f_mm[1], 2 + c // 2) if c < 4 else (w_used, used(C_FFN1 + 1))))
                for out in (neg_b, xT_hi):
                    keep(out[:, c, :], bank[5 + c // 2][:, (c % 2) * N:(c % 2 + 1) * N], f_act[1], ACT.Identity,
                         bias=sbias[:, 10 + c:11 + c])
            high_chunk(C_GCN2)
            deviation(0, 0, 1, 1)
            high_chunk(C_FFN2)

            def gcn(s, c):
                act.wait_ge(e_dinv, 1)
                for m in range(M):
                    act.wait_ge(*((g_mm, s + 1) if m == 0 else (w_used, used(c))))
                    for out, mark in ((h_sb, g_kept), (h_hi, g_high)):
                        for (b, c0, c1, o) in NODE_BANKS[m]:
                            keep(out[:, m, o:o + c1 - c0], bank[b][:, c0:c1], mark, scale=dinv[:, m:m + 1])

            transposed(4)
            act.dma_start(rw[:, :].rearrange("p (k e) -> p k e", k=K), row_tiles(t["L2_ffn_router_w"], P)).then_inc(ld_mid, 16)
            row_bc(rb[:, :], t["L2_ffn_router_b"], ld_mid)
            row_bc(hbias_bc[:, :], t["L3_gnn_b_rgcn"], ld_mid)
            gcn(0, C_GCN2)
            act.wait_ge(ld_mid, LD_MID[2])
            keep(rw_hi[:, :], rw[:, :], rw_high)
            high_chunk(C_FFN2 + 1)

            deviation(0, 1)
            transposed(5)
            row_bc(bias_bc[:, :], t["L3_gnn_b_gcn"], ld_bias)
            act.wait_ge(f_dve[2], 1)
            keep(lg[:, 2, :, :], lg[:, 1, :, :], f_act[2], ACT.Exp)
            act.wait_ge(w_used, used(C_FFN2))
            for m in range(M):
                keep(flat(z_b[:, 2 * m:2 * m + 2, :]), bank[3 + m][:, :], f_act[2], ACT.Silu)
            high_chunk(C_FFN2 + 2)
            for j in range(2):
                act.wait_ge(f_mm[2], 2 + j)
                keep(flat(hid_hi[:, 2 * j:2 * j + 2, :]), bank[3 + j][:, :], f_act[2])
            high_chunk(C_ROOT)
            for m in range(M):
                act.wait_ge(*((f_mm[2], 4) if m == 0 else (w_used, used(C_FFN2 + 2))))
                for (b, c0, c1, o) in NODE_BANKS[m]:
                    keep(outb[:, m, o:o + c1 - c0], bank[b][:, c0:c1], f_act[2])

            deviation(0, 1)
            transposed(6)
            keep(h_hi[:, :, :], xn[:, :, :], x_high)
            act.wait_ge(e_added, 16 * ET + 16)

            def load_counts(r, half):
                act.dma_start(ct[:, half, :, :], table[bass.ds(r * N, N), :].rearrange("(m p) n -> p m n", p=P))\
                   .then_inc(ld_ct[half], 16)

            load_counts(0, 0)
            load_counts(1, 1)
            with act.Fori(0, REL // 2) as i:
                for half in range(2):
                    act.wait_ge(r_t, i * 2 + (half + 1))
                    keep(flat(aT_hi[:, :, :]), bank[7][:, :], r_thigh)
                    load_counts(i * 2 + (half + 2), half)
                    high(i * 2 + (nth(C_REL) + half), i * 2 + (used(C_REL - 2) + half), half)
                    for j in range(3):
                        act.wait_ge(r_mm, i * 6 + (3 * half + j + 1))
                        keep(flat(REL_T[half][0][:, 2 * j:2 * j + 2, :]), bank[3 + j][:, :], r_high)
            high_chunk(C_GCN3)
            transposed(7)
            act.dma_start(rw[:, :].rearrange("p (k e) -> p k e", k=K), row_tiles(t["L3_ffn_Wr"], P)).then_inc(ld_mid, 16)
            row_bc(rb[:, :], t["L3_ffn_br"], ld_mid)
            row_bc(hbias_bc[:, :], t["L3_ffn_b1"], ld_mid)
            row_bc(gamma_bc[:, :], t["L3_ffn_ln_g"], ld_mid)
            row_bc(beta_bc[:, :], t["L3_ffn_ln_b"], ld_mid)
            high_chunk(C_FFN3)
            gcn(1, C_GCN3)
            act.wait_ge(ld_mid, LD_MID[3])
            keep(rw_hi[:, :], rw[:, :], rw_high)
            high_chunk(C_FFN3 + 1)

            deviation(0, 1)
            transposed(8)
            act.wait_ge(f_dve[3], 1)
            keep(lg[:, 2, :, :], lg[:, 1, :, :], f_act[3], ACT.Exp)
            act.wait_ge(f_dve[3], 2)
            keep(h_sb[:, :, :], h_sb[:, :, :], f_act[3], ACT.Gelu_apprx_tanh)
            high_chunk(C_FFN3 + 2)
            for j in range(4):
                act.wait_ge(f_mm[3], 3 + j)
                keep(HT3[j][0], bank[3 + j][0:HID3 + 1, :], f_act[3])
            deviation(0, 1)

        @block.vector
        def _(dve):
            step = Steps(dve, dve_step)
            add_, mul, mx = ALU.add, ALU.mult, ALU.max

            def tt(out, a, b, op):
                return dve.tensor_tensor(out, a, b, op)

            def ts(out, a, s1, op0, s2=None, op1=None):
                return dve.tensor_scalar(out, a, s1, s2, op0, op1) if op1 is not None else dve.tensor_scalar(out, a, s1, None, op0)

            def dot(out, a, b, acc, op0=mul, op1=add_):
                return dve.tensor_tensor_reduce(out=out, in0=a, in1=b, scale=1.0, scalar=0.0, op0=op0, op1=op1, accum_out=acc)

            def low_of(out, whole, high_, mark):
                tt(out, whole, high_.bitcast(FP32), ALU.subtract).then_inc(mark, 1)

            def low(n, half, shape=WHOLE):
                rows_, tiles, cols = shape
                dve.wait_ge(w_high[0], n + 1)
                low_of(w_lo[0:rows_, half, 0:tiles[0], 0:cols], w_in[0:rows_, 0, 0:tiles[0], 0:cols],
                       w_hi[0:rows_, half, 0:tiles[0], 0:cols], w_low[0])

            def low_chunk(c):
                low(nth(c), c % 2, SHAPES.get(c, WHOLE))

            moments_taken = [0]

            def moments(buf, m):
                for j in range(2):
                    last = dve.bn_stats(stats[:, m, j, :], buf[:, m, j * HALF:(j + 1) * HALF])
                step(last)
                dve.bn_aggr(mv[:, m, :], flat(stats[:, m, :, :])).then_inc(ln_var, 1)
                moments_taken[0] += 1
                dve.wait_ge(ln_std, moments_taken[0])
                step(dve.reciprocal(rstd[:, m:m + 1], std[:, m:m + 1]))

            def normalise(m):
                moments(x_sb, m)
                ts(xn[:, m, :], x_sb[:, m, :], mv[:, m, 0:1], ALU.subtract, rstd[:, m:m + 1], mul).then_inc(ln_xn, 1)

            def transposed(i):
                for j in range(3):
                    dve.wait_ge(ln_high, 3 * i + j + 1)
                    low_of(flat(xT_lo[:, 2 * j:2 * j + 2, :]), bank[3 + j][:, :], flat(xT_hi[:, 2 * j:2 * j + 2, :]), ln_low)

            def turned(i, bias=None):
                dve.wait_ge(ln_xn, 2 * i + 2)
                transposed(i)
                if bias is not None:
                    dve.wait_ge(ld_bias, 16 * (bias + 1))
                    for m in range(M):
                        last = tt(x_sb[:, m, :], x_sb[:, m, :], bias_bc[:, :], add_)
                    step(last)

            def scores(u, layer, ahead, together=False):
                dve.wait_ge(ld_a, u * 32 + 32)
                def h_parts(m):
                    dve.wait_ge(h_high, u * 4 + (2 * m + 2))
                    low_of(h_lo[:, m, :], h_sb[:, m, :], h_hi[:, m, :], h_low)

                for j, m in ((0, 0), (0, 1), (1, 0), (1, 1)) if together else ((0, 0), (1, 0), (0, 1), (1, 1)):
                    if not together and (j, m) == (0, 1):
                        h_parts(0)
                    dve.wait_ge(h_kept, u * 4 + (2 * m + 2))
                    last = dot(junk[:, :], h_sb[:, m, :], a_bc[:, j, :], scal[:, 2 * j + m:2 * j + m + 1])
                    if (j, m) == (0, 1):
                        last.then_inc(scored, 1)
                        dve.wait_ge(scored, u + 1)
                    else:
                        step(last)
                dve.wait_ge(src_row, u + 1)
                for m in range(M):
                    last = ts(score[:, m, :], bank[7][:, 0:N], scal[:, 2 + m:3 + m], add_)
                step(last)
                step(dve.scalar_tensor_tensor(flat(leaky[:, :, :]), flat(score[:, :, :]), 0.2, flat(score[:, :, :]), mul, mx))
                step(tt(flat(score[:, :, :]), flat(leaky[:, :, :]), flat(mask[:, :, :]), add_))
                dve.tensor_reduce(small[:, 0:M], score[:, :, :], AX.X, mx, negate=True).then_inc(masked, 1)
                if together:
                    h_parts(0)
                ahead()
                for m in range(M):
                    dve.wait_ge(exped, u * 2 + m + 1)
                    last = dot(leaky[:, m, :], prob[:, m, :], cnt[:, layer, m, :], small[:, 2 + m:3 + m])
                step(last)
                if layer == 1:
                    step(ts(small[:, 2:4], small[:, 2:4], 1e-16, add_))
                step(dve.reciprocal(small[:, 4:6], small[:, 2:4]))
                for m in range(M):
                    last = ts(alpha[:, m, :], leaky[:, m, :], small[:, 4 + m:5 + m], mul)
                last.then_inc(normed, 1)
                h_parts(1)
                dve.wait_ge(aT_high, u + 1)
                low_of(flat(aT_lo[:, :, :]), bank[7][:, :], flat(aT_hi[:, :, :]), aT_low)

            def batch_firsts(b):
                dve.wait_ge(b_key, b + 1)
                for g in range(G):
                    last = dve.tensor_scalar(same[:, g, :], bank[7][:, g * P:(g + 1) * P], key[:, bass.ds(b * G + g, 1)], None, ALU.is_equal)
                last.then_inc(b_same, 1)
                dve.wait_ge(b_same, b + 1)
                tt(kdiag[:, :, :], same[:, :, :], tril[:, :].unsqueeze(1).to_broadcast([P, G, P]), mul).then_inc(b_tri, 1)
                dve.wait_ge(b_tri, b + 1)
                dve.wait_ge(b_taken, b + 1)
                dve.tensor_reduce(first[:, :], kdiag[:, :, :], AX.X, mx).then_inc(b_first, 1)

            def gat(layer):
                c0, n0 = C_GAT[layer], NTH_GAT[layer]
                step(ts(flat(mask[:, :, :]), flat(cnt[:, layer, :, :]), 0.0, ALU.is_equal, NONE, mul))

                def head(h, first_head=False, last_head=False):
                    b = h + HEADS * layer
                    step(dve.tensor_copy(b1_head[:, :], b1c[:, layer, bass.ds(h * K, K)]))
                    scores(h + 9 * layer, layer, lambda: None if first_head or last_head else low(h * 2 + (n0 + 2), 0))
                    if first_head:
                        low(n0 + 2, 0)
                    for g in range(G):
                        dve.tensor_scalar(osrc[:, g, :], iota[:, :], edge_f[:, 0, bass.ds(b * G + g, 1)], None, ALU.is_equal)
                        last = dve.tensor_scalar(kdiag[:, g, :], ident[:, :], key[:, bass.ds(b * G + g, 1)], None, mul)
                    last.then_inc(b_hot, 1)
                    if last_head:
                        low(n0 + 2 * HEADS, 1)
                    a = (h + HEADS * layer) * 3
                    for j in range(3):
                        dve.wait_ge(z_kept, a + (j + 1))
                        ts(flat(neg_b[:, 2 * j:2 * j + 2, :]), flat(z_b[:, 2 * j:2 * j + 2, :]), 0.0, ALU.min).then_inc(z_neg, 1)
                    for j in range(3):
                        dve.wait_ge(z_exp, a + (j + 1))
                        dve.scalar_tensor_tensor(flat(neg_b[:, 2 * j:2 * j + 2, :]), flat(neg_b[:, 2 * j:2 * j + 2, :]), -1.0,
                                                 flat(z_b[:, 2 * j:2 * j + 2, :]), add_, mx).then_inc(elu, 1)
                    if not last_head:
                        batch_firsts(b)
                    for j in range(3):
                        dve.wait_ge(hid_high, a + (j + 1))
                        low_of(hid_lo[:, 2 * j:2 * j + 2, :], neg_b[:, 2 * j:2 * j + 2, :], hid_hi[:, 2 * j:2 * j + 2, :], hid_low)
                    if last_head:
                        batch_firsts(b)
                    else:
                        low(h * 2 + (n0 + 3), 1)

                head(0, first_head=True)
                with step.loop(1, HEADS - 1, 9 + layer) as h:
                    head(h)
                head(HEADS - 1, last_head=True)
                low_chunk(c0 + 18)
                scores(HEADS + 9 * layer, layer, lambda: None, together=True)
                low_chunk(c0 + 19)
                for m in range(M):
                    dve.wait_ge(att2_mm, 2 * layer + m + 1)
                    step(to_stream(m))
                    normalise(m)

            def to_stream(m):
                for (b, c0, c1, o) in NODE_BANKS[m]:
                    last = tt(x_sb[:, m, o:o + c1 - c0], x_sb[:, m, o:o + c1 - c0], bank[b][:, c0:c1], add_)
                return last

            dve.wait_ge(consts, NCONST)
            dve.wait_ge(ld_x, 16)
            for m in range(M):
                normalise(m)
            turned(0, bias=0)
            low(1, 0)
            dve.wait_ge(ld_edge, 48)
            step(dve.tensor_copy(edge_f[:, :, :], edge_i[:, :, :]))
            step(dve.scalar_tensor_tensor(key[:, :], edge_f[:, 2, :], float(N), edge_f[:, 1, :], mul, add_))
            step(ts(spill[:, :], key[:, :], -1.0, mul, pcol[:, 0:1], add_))
            def one_hot(b, a):
                dve.wait_ge(e_used, b + 1)
                for g in range(G):
                    for j, out in ((0, all_src), (1, all_dst)):
                        last = dve.tensor_scalar(out[:, a, g, :], iota[:, :], edge_f[:, j, bass.ds(b * G + g, 1)], None, ALU.is_equal)
                last.then_inc(e_hot, 1)

            with dve.Fori(0, ET // G // RING) as i:
                for a in range(RING):
                    one_hot(i * RING + a, a)
            for a in range(ET // G % RING):
                one_hot(ET // G // RING * RING + a, a)
            dve.wait_ge(e_cnt, 1)
            for j in range(2):
                last = dve.tensor_copy(flat(cnt[:, j, :, :]), bank[0][:, :])
            step(last)
            for m in range(M):
                last = tt(cnt[:, 0, m, m * P:(m + 1) * P], cnt[:, 0, m, m * P:(m + 1) * P], ident[:, :], add_)
            last.then_inc(e_mask, 1)
            dve.wait_ge(e_mask, 1)
            dve.wait_ge(ld_const, 16 * 6)
            gat(0)

            turned(1)
            cls = xn[0:NCLS, 0, :]
            dve.wait_ge(ld_const, 16 * 6)
            dve.wait_ge(ld_gate, 16)
            step(dot(junk[0:NCLS, :], cls, cls, gate[:, 0:1]))
            for r in range(2):
                step(dot(junk[0:NCLS, :], gp[:, r, :], gp[:, r, :], gate[:, 1 + r:2 + r]))
                last = dot(junk[0:NCLS, :], cls, gp[:, r, :], gate[:, 3 + r:4 + r])
                if r == 0:
                    step(last)
            last.then_inc(f_dve[0], 1)
            dve.wait_ge(f_act[0], 1)
            step(ts(gate[:, 12:15], gate[:, 8:11], 1e-12, mx))
            step(dve.reciprocal(gate[:, 16:19], gate[:, 12:15]))
            step(ts(gate[:, 20:22], gate[:, 3:5], gate[:, 16:17], mul))
            step(tt(gate[:, 20:22], gate[:, 20:22], gate[:, 17:19], mul))
            step(tt(gate[:, 20:22], gate[:, 20:22], bb[:, :], add_))
            step(dve.tensor_reduce(gate[:, 19:20], gate[:, 20:22], AX.X, mx, negate=True))
            ts(gate[:, 22:24], gate[:, 20:22], gate[:, 19:20], add_).then_inc(f_dve[0], 1)
            dve.wait_ge(f_act[0], 2)
            step(dve.tensor_reduce(gate[:, 26:27], gate[:, 24:26], AX.X, add_))
            step(dve.reciprocal(gate[:, 27:28], gate[:, 26:27]))
            step(ts(gate[:, 28:30], gate[:, 24:26], gate[:, 27:28], mul))
            step(tt(gate[:, 30:31], gate[:, 28:29], gate[:, 29:30], ALU.is_ge))
            step(ts(gate[:, 31:32], gate[:, 30:31], -1.0, mul, 1.0, add_))
            step(tt(gate[:, 32:34], gate[:, 28:30], gate[:, 30:32], mul))
            for r in range(2):
                last = ts(wdiag[:, r, :], ident[0:NCLS, 0:NCLS], gate[:, 32 + r:33 + r], mul)
            last.then_inc(f_dve[0], 1)
            dve.wait_ge(f_act[0], 3)
            step(dve.memset(hrow[FH:FH + 1, :], 1.0))
            dve.memset(hrow[:, 0:NCLS], 0.0).then_inc(f_dve[0], 1)
            step(dve.memset(zt, 0.0))
            dve.wait_ge(f_act[0], 4 + ATOMS)
            low_of(hid_lo[0:FH + 1, 0, :], hrow, hid_hi[0:FH + 1, 0, :], f_dve[0])
            dve.wait_ge(f_mm[0], 2)
            for d, n0, dn, s0, ds_, cnt_, r in [(3, 0, 2, 0, 1, 3, 0), (4, 1, 2, 0, 1, 3, 0)] + \
                    [(l, 2 * l, 1, 3, 1, 2, 1) for l in range(3)]:
                a0, da = s0 * NCLS + n0, ds_ * NCLS + dn
                last = tt(zt[:, d * P + n0:d * P + n0 + dn * (cnt_ - 1) + 1:dn], hat[:, a0:a0 + da * (cnt_ - 1) + 1:da],
                          bank[5][0:FH + 1, r * NCLS + n0:r * NCLS + n0 + dn * (cnt_ - 1) + 1:dn], mul)
            last.then_inc(f_dve[0], 1)
            dve.wait_ge(f_act[0], 5 + ATOMS)
            low_of(ZT[1], zt, ZT[0], f_dve[0])
            low(NTH_GAT[1] + 1, 0)
            dve.wait_ge(f_mm[0], 3)
            step(to_stream(0))
            normalise(0)
            dve.wait_ge(w_used, used(C_FFN0 + 1))
            step(to_stream(1))
            normalise(1)

            turned(2, bias=1)
            gat(1)

            def plus_beta():
                for m in range(M):
                    last = tt(x_sb[:, m, :], x_sb[:, m, :], beta_bc[:, :], add_)
                step(last)

            def affine_out(m, bias):
                for (b, c0, c1, o) in NODE_BANKS[m]:
                    if bias:
                        last = tt(h_sb[:, m, o:o + c1 - c0], bank[b][:, c0:c1], hbias_bc[:, o:o + c1 - c0], add_)
                    else:
                        last = dve.tensor_copy(h_sb[:, m, o:o + c1 - c0], bank[b][:, c0:c1])
                step(last)
                moments(h_sb, m)
                step(dve.scalar_tensor_tensor(h_sb[:, m, :], h_sb[:, m, :], mv[:, m, 0:1], gamma_bc[:, :], ALU.subtract, mul))
                return dve.scalar_tensor_tensor(x_sb[:, m, :], h_sb[:, m, :], rstd[:, m:m + 1], x_sb[:, m, :], mul, add_)

            turned(3)
            for j in range(2):
                dve.wait_ge(f_act[1], 4 * j + 4)
                low_of(hid_lo[:, 2 * j:2 * j + 2, :], z_b[:, 2 * j:2 * j + 2, :], hid_hi[:, 2 * j:2 * j + 2, :], f_dve[1])
            low_chunk(C_FFN1 + 2)
            dve.tensor_reduce(deg[:, :], cnt[:, 0, :, :], AX.X, add_).then_inc(e_deg, 1)
            dve.wait_ge(e_cntT_high, 1)
            low_of(flat(cntT_lo[:, :, :]), bank[1][:, :], flat(cntT_hi[:, :, :]), e_cntT_low)
            dve.wait_ge(e_std, 1)
            dve.reciprocal(dinv[:, :], sd[:, :]).then_inc(e_dinv, 1)
            for j in range(3):
                dve.wait_ge(f_act[1], 8 + 4 * j + 4)
                low_of(xT_lo[:, 2 * j:2 * j + 2, :], neg_b[:, 2 * j:2 * j + 2, :], xT_hi[:, 2 * j:2 * j + 2, :], f_dve[1])
            low_chunk(C_GCN2)
            dve.wait_ge(ld_mid, LD_MID[1])
            plus_beta()
            for m in range(M):
                dve.wait_ge(*((f_mm[1], 4) if m == 0 else (w_used, used(C_FFN1 + 2))))
                step(affine_out(m, True))
                normalise(m)

            def gcn_low(s):
                for m in range(M):
                    dve.wait_ge(g_kept, 4 * s + 2 * m + 2)
                    dve.wait_ge(g_high, 4 * s + 2 * m + 2)
                    low_of(h_lo[:, m, :], h_sb[:, m, :], h_hi[:, m, :], g_low)
                dve.wait_ge(rw_high, s + 1)
                low_of(rw_lo[:, :], rw[:, :], rw_hi[:, :], rw_low)

            def gcn_out(s):
                for m in range(M):
                    dve.wait_ge(g_out, 2 * s + m + 1)
                    for (b, c0, c1, o) in NODE_BANKS[m]:
                        xs = x_sb[:, m, o:o + c1 - c0]
                        last = dve.scalar_tensor_tensor(xs, bank[b][:, c0:c1], dinv[:, m:m + 1], xs, mul, add_)
                    step(last)
                    normalise(m)

            dve.wait_ge(e_dinv, 1)
            turned(4, bias=2)
            low_chunk(C_FFN2)
            gcn_low(0)
            low_chunk(C_FFN2 + 1)
            gcn_out(0)

            def bc(ap):
                return ap.to_broadcast([P, M, 8])

            i8 = iota8[:, :].unsqueeze(1).to_broadcast([P, M, 8])

            def first_max(p, o):
                step(dve.tensor_reduce(lg[:, o, :, 0], lg[:, p, :, :], AX.X, mx))
                step(tt(lg[:, o + 1, :, :], lg[:, p, :, :], bc(lg[:, o, :, 0:1]), ALU.is_equal))
                step(tt(lg[:, o + 1, :, :], lg[:, o + 1, :, :], i8, mul))
                step(dve.tensor_reduce(lg[:, o + 2, :, 0], lg[:, o + 1, :, :], AX.X, ALU.min))
                step(tt(lg[:, o + 3, :, :], i8, bc(lg[:, o + 2, :, 0:1]), ALU.is_equal))

            def route(s):
                dve.wait_ge(f_mm[s], 1)
                step(tt(lg[:, 0, :, :], bank[6][:, 0:M * 8].rearrange("p (m e) -> p m e", m=M),
                        rb[:, :].unsqueeze(1).to_broadcast([P, M, 8]), add_))
                step(dve.tensor_reduce(lg[:, 15, :, 0], lg[:, 0, :, :], AX.X, mx))
                tt(lg[:, 1, :, :], lg[:, 0, :, :], bc(lg[:, 15, :, 0:1]), ALU.subtract).then_inc(f_dve[s], 1)
                dve.wait_ge(f_act[s], 1)
                step(dve.tensor_reduce(lg[:, 15, :, 1], lg[:, 2, :, :], AX.X, add_))
                step(dve.reciprocal(lg[:, 15, :, 2], lg[:, 15, :, 1]))
                step(tt(lg[:, 3, :, :], lg[:, 2, :, :], bc(lg[:, 15, :, 2:3]), mul))

            turned(5)
            route(2)
            first_max(3, 4)
            dve.wait_ge(f_act[2], 3)
            dve.wait_ge(w_used, used(C_FFN2 + 1))
            for m, b in enumerate((5, 7)):
                last = tt(flat(neg_b[:, 2 * m:2 * m + 2, :]), flat(z_b[:, 2 * m:2 * m + 2, :]), bank[b][:, :], mul)
            step(last)
            for m in range(M):
                hm = flat(neg_b[:, 2 * m:2 * m + 2, :]).rearrange("p (e h) -> p e h", e=EXP2)
                last = tt(hm, hm, lg[:, 7, m, :].unsqueeze(2).to_broadcast([P, EXP2, HID2]), mul)
            last.then_inc(f_dve[2], 1)
            low_chunk(C_FFN2 + 2)
            for j in range(2):
                dve.wait_ge(f_act[2], 4 + j)
                low_of(flat(hid_lo[:, 2 * j:2 * j + 2, :]), bank[3 + j][:, :], flat(hid_hi[:, 2 * j:2 * j + 2, :]), f_dve[2])
            low_chunk(C_ROOT)
            for m in range(M):
                dve.wait_ge(f_act[2], 7 + 2 * m)
                step(dve.scalar_tensor_tensor(x_sb[:, m, :], outb[:, m, :], lg[:, 4, m, 0:1], x_sb[:, m, :], mul, add_))
                normalise(m)

            turned(6, bias=3)
            dve.wait_ge(x_high, 1)
            low_of(h_lo[:, :, :], xn[:, :, :], h_hi[:, :, :], x_low)

            def shares(half, landed):
                dve.wait_ge(ld_ct[half], landed)
                step(dve.tensor_reduce(small[:, 0:M], ct[:, half, :, :], AX.X, add_))
                step(ts(small[:, 2:4], small[:, 0:M], 1.0, mx))
                step(dve.reciprocal(small[:, 4:6], small[:, 2:4]))
                for m in range(M):
                    last = ts(REL_A[half][:, m, :], ct[:, half, m, :], small[:, 4 + m:5 + m], mul)
                last.then_inc(r_norm, 1)

            shares(0, 16)
            with step.loop(0, REL // 2, 6) as i:
                for half in range(2):
                    dve.wait_ge(r_thigh, i * 2 + (half + 1))
                    low_of(flat(aT_lo[:, :, :]), bank[7][:, :], flat(aT_hi[:, :, :]), r_tlow)
                    low(i * 2 + (nth(C_REL) + half), half)
                    shares(1 - half, i * 16 + (16 + 16 * half))
                    for j in range(3):
                        dve.wait_ge(r_high, i * 6 + (3 * half + j + 1))
                        low_of(flat(REL_T[half][1][:, 2 * j:2 * j + 2, :]), bank[3 + j][:, :],
                               flat(REL_T[half][0][:, 2 * j:2 * j + 2, :]), r_low)
            low_chunk(C_GCN3)
            dve.wait_ge(w_used, used(C_REL + REL - 1))
            for m in range(M):
                for (b, c0, c1, o) in SUM_BANKS[m]:
                    last = tt(xn[:, m, o:o + c1 - c0], bank[b][:, c0:c1], hbias_bc[:, o:o + c1 - c0], add_)
                last.then_inc(ln_xn, 1)
            transposed(7)
            low_chunk(C_FFN3)
            gcn_low(1)
            low_chunk(C_FFN3 + 1)
            gcn_out(1)

            turned(8)
            route(3)
            first_max(3, 4)
            step(dve.scalar_tensor_tensor(lg[:, 8, :, :], lg[:, 7, :, :], -2.0, lg[:, 3, :, :], mul, add_))
            first_max(8, 9)
            step(tt(lg[:, 13, :, 0], lg[:, 4, :, 0], lg[:, 9, :, 0], add_))
            step(dve.reciprocal(lg[:, 13, :, 1], lg[:, 13, :, 0]))
            step(tt(lg[:, 7, :, :], lg[:, 7, :, :], bc(lg[:, 4, :, 0:1]), mul))
            step(tt(lg[:, 12, :, :], lg[:, 12, :, :], bc(lg[:, 9, :, 0:1]), mul))
            step(tt(lg[:, 14, :, :], lg[:, 7, :, :], lg[:, 12, :, :], add_))
            step(tt(lg[:, 14, :, :], lg[:, 14, :, :], bc(lg[:, 13, :, 1:2]), mul))
            dve.wait_ge(ld_mid, LD_MID[3])
            for m in range(M):
                dve.wait_ge(*((f_mm[3], 2) if m == 0 else (w_used, used(C_FFN3))))
                for (b, c0, c1, o) in NODE_BANKS[m]:
                    last = tt(h_sb[:, m, o:o + c1 - c0], bank[b][:, c0:c1], hbias_bc[:, o:o + c1 - c0], add_)
            last.then_inc(f_dve[3], 1)
            dve.wait_ge(f_act[3], 2)
            for m in range(M):
                dve.tensor_copy(ge[:, m, :, HID3], lg[:, 14, m, :])
                last = tt(ge[:, m, :, 0:HID3], h_sb[:, m, :].rearrange("p (e h) -> p e h", e=EXP3),
                          lg[:, 14, m, :].unsqueeze(2).to_broadcast([P, EXP3, HID3]), mul)
            last.then_inc(f_dve[3], 1)
            low_chunk(C_FFN3 + 2)
            for j in range(4):
                dve.wait_ge(f_act[3], 3 + j)
                low_of(HT3[j][1], bank[3 + j][0:HID3 + 1, :], HT3[j][0], f_dve[3])
            plus_beta()
            for m in range(M):
                dve.wait_ge(w_used, used(C_FFN3 + 1 + m))
                affine_out(m, False).then_inc(out_ready, 1)
                dve.wait_ge(out_ready, m + 1)


def kernel(**inputs):
    import concourse.bacc as bacc
    from concourse.bass_utils import run_bass_kernel_spmd

    a = {name: np.asarray(v) for name, v in inputs.items()}
    arrays = {}

    def put(name, v):
        arrays[name] = np.ascontiguousarray(v)

    plain = ["x", "L0_gnn_W1", "L0_gnn_W2", "L0_gnn_a_src1", "L0_gnn_a_dst1", "L0_gnn_a_src2", "L0_gnn_a_dst2",
             "L0_gnn_b2", "L1_gnn_W1", "L1_gnn_W2", "L1_gnn_a_src1", "L1_gnn_a_dst1", "L1_gnn_a_src2", "L1_gnn_a_dst2",
             "L1_gnn_b2", "L0_ffn_gate_pair", "L0_ffn_balance_bias", "L1_ffn_bo", "L1_ffn_gamma", "L1_ffn_beta",
             "L2_gnn_W", "L2_gnn_b", "L2_ffn_router_w", "L2_ffn_router_b", "L3_gnn_W_root", "L3_gnn_b_rgcn",
             "L3_gnn_W_gcn", "L3_gnn_b_gcn", "L3_ffn_Wr", "L3_ffn_br", "L3_ffn_ln_g", "L3_ffn_ln_b"]
    for name in plain:
        put(name, a[name])
    for name in ("src", "dst", "edge_type_34"):
        put(name, a[name].reshape(ET, P).T)
    put("L0_gnn_b1", a["L0_gnn_b1"].reshape(-1, P).T)
    put("L1_gnn_b1", a["L1_gnn_b1"].reshape(-1, P).T)
    put("L1_ffn_b1", a["L1_ffn_b1"].reshape(-1, P).T)
    put("L1_ffn_b2", a["L1_ffn_b2"].reshape(-1, P).T)
    put("ffn0_in", np.concatenate([a["L0_ffn_fc1_w"].T, a["L0_ffn_atom_in_w"].transpose(2, 0, 1).reshape(D, -1)], 1))
    put("ffn0_bias", np.concatenate([a["L0_ffn_fc1_b"][None], a["L0_ffn_atom_in_b"]], 0).T)
    put("ffn0_out", np.concatenate([a["L0_ffn_fc2_w"].T, a["L0_ffn_fc2_b"][None]] +
                                   [v for d in range(ATOMS) for v in (a["L0_ffn_atom_out_w"][d].T, a["L0_ffn_atom_out_b"][d][None])], 0))
    put("L1_ffn_W1", a["L1_ffn_W1"].T)
    put("L1_ffn_W2", a["L1_ffn_W2"].T)
    put("L1_ffn_Wo", a["L1_ffn_Wo"].T)
    put("L2_ffn_w1", a["L2_ffn_w1"].transpose(1, 0, 2).reshape(D, -1))
    put("L2_ffn_w2", a["L2_ffn_w2"].transpose(1, 0, 2).reshape(D, -1))
    put("L2_ffn_w3", a["L2_ffn_w3"].reshape(-1, D))
    put("L3_gnn_W_rel", a["L3_gnn_W_rel"].reshape(-1, D))
    put("L3_ffn_W1", a["L3_ffn_W1"].transpose(1, 0, 2).reshape(D, -1))
    put("L3_ffn_b1", a["L3_ffn_b1"].reshape(-1))
    put("ffn3_out", np.concatenate([a["L3_ffn_W2"], a["L3_ffn_b2"][:, None, :]], 1).reshape(-1, D))

    nc = bacc.Bacc("TRN2", target_bir_lowering=False, num_devices=1)
    t = {}
    for name, v in arrays.items():
        t[name] = nc.dram_tensor(name, v.shape, mybir.dt.from_np(v.dtype), kind="ExternalInput").ap()
    t["out"] = nc.dram_tensor("out", (N, D), FP32, kind="ExternalOutput").ap()
    gnn_ffn_kernel(nc, t)
    r = run_bass_kernel_spmd(nc, [arrays], core_ids=[0])
    return r.results[0]["out"]
```
